# Optimizing a Trainium2 kernel written in Bass

```python
import numpy as np
import jax
import jax.numpy as jnp

def _softmax(x, axis=-1):
    return jax.nn.softmax(x, axis=axis)

def _gelu(x):
    return jax.nn.gelu(x, approximate=True)

def _silu(x):
    return jax.nn.silu(x)

def _sigmoid(x):
    return jax.nn.sigmoid(x)

def _layernorm(x, axis=-1, eps=1e-05):
    m = jnp.mean(x, axis=axis, keepdims=True)
    v = jnp.var(x, axis=axis, keepdims=True)
    return (x - m) / jnp.sqrt(v + eps)

def _scatter_add(tgt, idx, src, axis=0):
    return tgt.at[idx].add(src)

def _segment_sum(src, seg, n):
    return jax.ops.segment_sum(src, seg, n)
kernel_name = 'mk_macaron_d1_jaxref_r4_1c3fae'

def setup_inputs(seed: int=0):
    np.random.seed(seed)
    _w = jnp.asarray

    def _L0_attn_setup():
        import jax, jax.numpy as jnp
        import numpy as np
        B, T, C = (4, 256, 256)
        HEAD_SIZE = 64
        H = C // HEAD_SIZE
        N_LAYER, LAYER_ID = (24, 12)
        D_MIX_LORA, D_DECAY_LORA = (32, 64)
        HEAD_SIZE_DIVISOR = 8
        LN_EPS = 1e-05 * HEAD_SIZE_DIVISOR ** 2

        def _wkv6(r, k, v, w, u):

            def step(S, inp):
                r_t, k_t, v_t, w_t = inp
                y = jnp.einsum('bhj,bhji->bhi', r_t, S) + jnp.sum(r_t * u * k_t, axis=-1, keepdims=True) * v_t
                decay = jnp.exp(-jnp.exp(w_t))
                S = decay[..., None] * S + k_t[..., None] * v_t[..., None, :]
                return (S, y)
            to_t = lambda a: jnp.transpose(a, (1, 0, 2, 3))
            S0 = jnp.zeros(r.shape[:1] + (r.shape[2], r.shape[3], r.shape[3]), r.dtype)
            _, ys = jax.lax.scan(step, S0, (to_t(r), to_t(k), to_t(v), to_t(w)))
            return jnp.transpose(ys, (1, 0, 2, 3))
        key = jax.random.key(seed)
        ks = jax.random.split(key, 16)
        x = jax.random.normal(ks[0], (B, T, C), jnp.float32)
        r01 = LAYER_ID / (N_LAYER - 1)
        r10 = 1.0 - LAYER_ID / N_LAYER
        ddd = np.arange(C, dtype=np.float64) / C
        time_maa_x = jnp.asarray((1.0 - ddd ** r10).astype(np.float32))
        time_maa_w = jnp.asarray((1.0 - ddd ** r10).astype(np.float32))
        time_maa_k = jnp.asarray((1.0 - ddd ** r10).astype(np.float32))
        time_maa_v = jnp.asarray((1.0 - (ddd ** r10 + 0.3 * r01)).astype(np.float32))
        time_maa_r = jnp.asarray((1.0 - ddd ** (0.5 * r10)).astype(np.float32))
        time_maa_g = jnp.asarray((1.0 - ddd ** (0.5 * r10)).astype(np.float32))
        n = np.arange(C, dtype=np.float64)
        time_decay = jnp.asarray((-6.0 + 5.0 * (n / (C - 1)) ** (0.7 + 1.3 * r01)).astype(np.float32))
        zigzag = ((n + 1) % 3 - 1) * 0.1
        time_faaaa = jnp.asarray((r01 * (1.0 - n / (C - 1)) + zigzag).astype(np.float32)).reshape(H, HEAD_SIZE)
        u = lambda k, shp: jax.random.uniform(k, shp, jnp.float32, -0.01, 0.01)
        time_maa_w1 = u(ks[1], (C, D_MIX_LORA * 5))
        time_maa_w2 = u(ks[2], (5, D_MIX_LORA, C))
        time_decay_w1 = u(ks[3], (C, D_DECAY_LORA))
        time_decay_w2 = u(ks[4], (D_DECAY_LORA, C))
        s = 1.0 / np.sqrt(C)
        Wr = jax.random.normal(ks[5], (C, C), jnp.float32) * s
        Wk = jax.random.normal(ks[6], (C, C), jnp.float32) * s
        Wv = jax.random.normal(ks[7], (C, C), jnp.float32) * s
        Wg = jax.random.normal(ks[8], (C, C), jnp.float32) * s
        Wo = jax.random.normal(ks[9], (C, C), jnp.float32) * s
        ln_w = jnp.ones((C,), jnp.float32)
        ln_b = jnp.zeros((C,), jnp.float32)
        return dict(x=x, time_maa_x=time_maa_x, time_maa_w=time_maa_w, time_maa_k=time_maa_k, time_maa_v=time_maa_v, time_maa_r=time_maa_r, time_maa_g=time_maa_g, time_maa_w1=time_maa_w1, time_maa_w2=time_maa_w2, time_decay=time_decay, time_decay_w1=time_decay_w1, time_decay_w2=time_decay_w2, time_faaaa=time_faaaa, Wr=Wr, Wk=Wk, Wv=Wv, Wg=Wg, Wo=Wo, ln_w=ln_w, ln_b=ln_b)
    _L0_attn_in = _L0_attn_setup()

    def _L0_ffn_setup():
        import jax, jax.numpy as jnp
        import numpy as np
        H = 256
        I = 1024
        E = 4
        LN_EPS = 1e-12

        def _layer_norm(x, gamma, beta, eps=LN_EPS):
            mu = jnp.mean(x, axis=-1, keepdims=True)
            var = jnp.mean(jnp.square(x - mu), axis=-1, keepdims=True)
            return (x - mu) * jax.lax.rsqrt(var + eps) * gamma + beta
        key = jax.random.key(seed)
        ks = jax.random.split(key, 8)
        B, S = (4, 128)
        scale = 0.02
        return {'hidden_states': jax.random.normal(ks[0], (B, S, H), jnp.float32), 'W_router': jax.random.normal(ks[1], (H, E), jnp.float32) * scale, 'W1': jax.random.normal(ks[2], (E, H, I), jnp.float32) * scale, 'b1': jax.random.normal(ks[3], (E, I), jnp.float32) * scale, 'Wo': jax.random.normal(ks[4], (I, H), jnp.float32) * scale, 'bo': jax.random.normal(ks[5], (H,), jnp.float32) * scale, 'ln_gamma': jnp.ones((H,), jnp.float32), 'ln_beta': jnp.zeros((H,), jnp.float32)}
    _L0_ffn_in = _L0_ffn_setup()
    _d = {'L0_attn_x': _L0_attn_in['x'], 'L0_attn_time_maa_x': _L0_attn_in['time_maa_x'], 'L0_attn_time_maa_w': _L0_attn_in['time_maa_w'], 'L0_attn_time_maa_k': _L0_attn_in['time_maa_k'], 'L0_attn_time_maa_v': _L0_attn_in['time_maa_v'], 'L0_attn_time_maa_r': _L0_attn_in['time_maa_r'], 'L0_attn_time_maa_g': _L0_attn_in['time_maa_g'], 'L0_attn_time_maa_w1': _L0_attn_in['time_maa_w1'], 'L0_attn_time_maa_w2': _L0_attn_in['time_maa_w2'], 'L0_attn_time_decay': _L0_attn_in['time_decay'], 'L0_attn_time_decay_w1': _L0_attn_in['time_decay_w1'], 'L0_attn_time_decay_w2': _L0_attn_in['time_decay_w2'], 'L0_attn_time_faaaa': _L0_attn_in['time_faaaa'], 'L0_attn_Wr': _L0_attn_in['Wr'], 'L0_attn_Wk': _L0_attn_in['Wk'], 'L0_attn_Wv': _L0_attn_in['Wv'], 'L0_attn_Wg': _L0_attn_in['Wg'], 'L0_attn_Wo': _L0_attn_in['Wo'], 'L0_attn_ln_w': _L0_attn_in['ln_w'], 'L0_attn_ln_b': _L0_attn_in['ln_b'], 'L0_ffn_W_router': _L0_ffn_in['W_router'], 'L0_ffn_W1': _L0_ffn_in['W1'], 'L0_ffn_b1': _L0_ffn_in['b1'], 'L0_ffn_Wo': _L0_ffn_in['Wo'], 'L0_ffn_bo': _L0_ffn_in['bo'], 'L0_ffn_ln_gamma': _L0_ffn_in['ln_gamma'], 'L0_ffn_ln_beta': _L0_ffn_in['ln_beta']}
    _x0 = _d['L0_attn_x']
    _d['L0_attn_x'] = jax.random.normal(jax.random.fold_in(jax.random.key(seed), 1), (8, 512, 256), dtype=_x0.dtype)
    del _x0
    return _d

def reference(L0_attn_x, L0_attn_time_maa_x, L0_attn_time_maa_w, L0_attn_time_maa_k, L0_attn_time_maa_v, L0_attn_time_maa_r, L0_attn_time_maa_g, L0_attn_time_maa_w1, L0_attn_time_maa_w2, L0_attn_time_decay, L0_attn_time_decay_w1, L0_attn_time_decay_w2, L0_attn_time_faaaa, L0_attn_Wr, L0_attn_Wk, L0_attn_Wv, L0_attn_Wg, L0_attn_Wo, L0_attn_ln_w, L0_attn_ln_b, L0_ffn_W_router, L0_ffn_W1, L0_ffn_b1, L0_ffn_Wo, L0_ffn_bo, L0_ffn_ln_gamma, L0_ffn_ln_beta):

    def _L0_attn_ref(x, time_maa_x, time_maa_w, time_maa_k, time_maa_v, time_maa_r, time_maa_g, time_maa_w1, time_maa_w2, time_decay, time_decay_w1, time_decay_w2, time_faaaa, Wr, Wk, Wv, Wg, Wo, ln_w, ln_b):
        import jax, jax.numpy as jnp
        import numpy as np
        B, T, C = (4, 256, 256)
        HEAD_SIZE = 64
        H = C // HEAD_SIZE
        N_LAYER, LAYER_ID = (24, 12)
        D_MIX_LORA, D_DECAY_LORA = (32, 64)
        HEAD_SIZE_DIVISOR = 8
        LN_EPS = 1e-05 * HEAD_SIZE_DIVISOR ** 2

        def _wkv6(r, k, v, w, u):

            def step(S, inp):
                r_t, k_t, v_t, w_t = inp
                y = jnp.einsum('bhj,bhji->bhi', r_t, S) + jnp.sum(r_t * u * k_t, axis=-1, keepdims=True) * v_t
                decay = jnp.exp(-jnp.exp(w_t))
                S = decay[..., None] * S + k_t[..., None] * v_t[..., None, :]
                return (S, y)
            to_t = lambda a: jnp.transpose(a, (1, 0, 2, 3))
            S0 = jnp.zeros(r.shape[:1] + (r.shape[2], r.shape[3], r.shape[3]), r.dtype)
            _, ys = jax.lax.scan(step, S0, (to_t(r), to_t(k), to_t(v), to_t(w)))
            return jnp.transpose(ys, (1, 0, 2, 3))
        b, t, c = x.shape
        h, n = (H, HEAD_SIZE)
        xx = jnp.concatenate([jnp.zeros_like(x[:, :1]), x[:, :-1]], axis=1) - x
        xxx = x + xx * time_maa_x
        mix = jnp.tanh(xxx @ time_maa_w1).reshape(b, t, 5, D_MIX_LORA)
        m = jnp.einsum('btsd,sdc->sbtc', mix, time_maa_w2)
        xw = x + xx * (time_maa_w + m[0])
        xk = x + xx * (time_maa_k + m[1])
        xv = x + xx * (time_maa_v + m[2])
        xr = x + xx * (time_maa_r + m[3])
        xg = x + xx * (time_maa_g + m[4])
        r = xr @ Wr
        k = xk @ Wk
        v = xv @ Wv
        g = jax.nn.silu(xg @ Wg)
        w = time_decay + jnp.tanh(xw @ time_decay_w1) @ time_decay_w2
        y = _wkv6(r.reshape(b, t, h, n), k.reshape(b, t, h, n), v.reshape(b, t, h, n), w.reshape(b, t, h, n), time_faaaa)
        mu = y.mean(-1, keepdims=True)
        var = y.var(-1, keepdims=True)
        yn = ((y - mu) / jnp.sqrt(var + LN_EPS)).reshape(b, t, c) * ln_w + ln_b
        return yn * g @ Wo

    def _L0_ffn_ref(hidden_states, W_router, W1, b1, Wo, bo, ln_gamma, ln_beta):
        import jax, jax.numpy as jnp
        import numpy as np
        H = 256
        I = 1024
        E = 4
        LN_EPS = 1e-12

        def _layer_norm(x, gamma, beta, eps=LN_EPS):
            mu = jnp.mean(x, axis=-1, keepdims=True)
            var = jnp.mean(jnp.square(x - mu), axis=-1, keepdims=True)
            return (x - mu) * jax.lax.rsqrt(var + eps) * gamma + beta
        B, S, _ = hidden_states.shape
        x = hidden_states.reshape(-1, H)
        logits = x @ W_router
        expert_idx = jnp.argmax(logits, axis=-1)
        h = jnp.einsum('th,ehi->tei', x, W1) + b1
        h = jax.nn.gelu(h, approximate=False)
        onehot = jax.nn.one_hot(expert_idx, E, dtype=x.dtype)
        intermediate = jnp.einsum('te,tei->ti', onehot, h)
        y = intermediate @ Wo + bo + x
        y = _layer_norm(y, ln_gamma, ln_beta)
        return y.reshape(B, S, H)
    x = L0_attn_x
    x = x + 0.5 * _L0_ffn_ref(_layernorm(x, axis=-1), L0_ffn_W_router, L0_ffn_W1, L0_ffn_b1, L0_ffn_Wo, L0_ffn_bo, L0_ffn_ln_gamma, L0_ffn_ln_beta)
    x = x + _L0_attn_ref(_layernorm(x, axis=-1), L0_attn_time_maa_x, L0_attn_time_maa_w, L0_attn_time_maa_k, L0_attn_time_maa_v, L0_attn_time_maa_r, L0_attn_time_maa_g, L0_attn_time_maa_w1, L0_attn_time_maa_w2, L0_attn_time_decay, L0_attn_time_decay_w1, L0_attn_time_decay_w2, L0_attn_time_faaaa, L0_attn_Wr, L0_attn_Wk, L0_attn_Wv, L0_attn_Wg, L0_attn_Wo, L0_attn_ln_w, L0_attn_ln_b)
    x = x + 0.5 * _L0_ffn_ref(_layernorm(x, axis=-1), L0_ffn_W_router, L0_ffn_W1, L0_ffn_b1, L0_ffn_Wo, L0_ffn_bo, L0_ffn_ln_gamma, L0_ffn_ln_beta)
    return x

_drawn_inputs = setup_inputs


def setup_inputs(seed=0):
    import zlib

    import numpy as np

    out = dict(_drawn_inputs(seed))
    spreads = {'L0_attn_ln_w': (1.0, 0.2),
     'L0_attn_ln_b': (0.0, 0.1),
     'L0_ffn_ln_gamma': (1.0, 0.2),
     'L0_ffn_ln_beta': (0.0, 0.1)}
    factors = {'L0_attn_time_maa_x': 8.0,
     'L0_attn_time_maa_w': 44.645,
     'L0_attn_time_maa_w1': 8.0,
     'L0_attn_time_maa_w2': 8.0,
     'L0_attn_time_decay_w1': 37.576,
     'L0_attn_time_decay_w2': 37.372,
     'L0_attn_time_faaaa': 2.754,
     'L0_ffn_b1': 8.0,
     'L0_ffn_bo': 4.336}
    for name, (base, spread) in spreads.items():
        noise = np.random.default_rng([zlib.crc32(name.encode()), seed]).standard_normal(out[name].shape)
        drawn = base * np.exp(spread * noise) if base else spread * noise
        out[name] = jnp.asarray(drawn.astype(out[name].dtype))
    for name, factor in factors.items():
        out[name] = (out[name] * factor).astype(out[name].dtype)
    return out
```

```python
from contextlib import ExitStack

import concourse.bass as bass
from concourse import mybir

F32 = mybir.dt.float32
U32 = mybir.dt.uint32
I32 = mybir.dt.int32
U8 = mybir.dt.uint8
ALU = mybir.AluOpType
ACT = mybir.ActivationFunctionType
AX = mybir.AxisListType

P = 128
B, T, C = 8, 512, 256
NTOK = B * T
NT = NTOK // P
TB = T // P
CC = C // P
E = 4
I = 1024
IC = I // P
HB = 512
NH = I // HB
NS = NT + E - 1
NONE = 2 * NTOK
LN_EPS = 1e-5
FFN_EPS = 1e-12


def ds(i, n=1):
    return bass.ds(i, n)


class Shared:

    def __init__(self, nc, ctx):
        self.nc, self.ctx, self.n, self.halved = nc, ctx, 0, False

    def sem(self, name):
        self.n += 1
        return self.ctx.enter_context(self.nc.semaphore(f"{name}_{self.n}"))

    def sb(self, name, shape, dt=F32, ctx=None):
        self.n += 1
        return (ctx or self.ctx).enter_context(self.nc.sbuf_tensor(f"{name}_{self.n}", shape, dt))

    def ps(self, name, shape, dt=F32, ctx=None):
        self.n += 1
        return (ctx or self.ctx).enter_context(self.nc.psum_tensor(f"{name}_{self.n}", shape, dt))


def load_constants(sh, d):
    nc, ctx = sh.nc, sh.ctx
    sh.ident = sh.sb("ident", [P, P])
    sh.ones = sh.sb("ones", [P, P])
    sh.before = sh.sb("before", [P, P])
    sh.count = sh.sb("count", [P, P])
    sh.token = sh.sb("token", [P, NT])
    sh.steps = sh.sb("steps", [P, NS + 1])
    sh.w_router = sh.sb("w_router", [P, CC, E])
    sh.w1 = sh.sb("w1", [P, E, CC, I])
    sh.b1 = sh.sb("b1", [P, E, I])
    sh.wo = sh.sb("wo_ffn", [P, IC, C])
    sh.bo = sh.sb("bo", [P, C])
    sh.gamma = sh.sb("gamma", [P, C])
    sh.beta = sh.sb("beta", [P, C])
    sh.lane = sh.sb("minus_half", [P, HB // 8])

    sh.router_in = sh.sem("router_in")
    sh.ffn_in = sh.sem("ffn_in")
    sh.built = sh.sem("built")
    ready = sh.sem("constants_ready")

    with nc.Block() as block:

        @block.sync
        def _(sp):
            sp.dma_start(sh.w_router[:], d["W_router"].rearrange("(c p) e -> p c e", p=P)).then_inc(sh.router_in, 16)

        @block.gpsimd
        def _(pool):
            g = nc.gpsimd
            g.memset(sh.ident[:], 0.0).then_inc(sh.built, 1)
            g.memset(sh.before[:], 1.0).then_inc(sh.built, 1)
            g.memset(sh.ones[:], 1.0)
            g.memset(sh.lane[:], -0.5)
            pool.wait_ge(sh.built, 2)
            g.affine_select(out=sh.ident[:], in_=sh.ident[:], compare_op=ALU.not_equal, fill=1.0, base=0,
                            pattern=[[-1, P]], channel_multiplier=1)
            g.affine_select(out=sh.before[:], in_=sh.before[:], compare_op=ALU.is_gt, fill=0.0, base=0,
                            pattern=[[1, P]], channel_multiplier=-1)
            g.iota(sh.count[:], pattern=[[1, P]], base=0, channel_multiplier=0, allow_small_or_imprecise_dtypes=True)
            g.iota(sh.token[:], pattern=[[P, NT]], base=-NONE, channel_multiplier=1,
                   allow_small_or_imprecise_dtypes=True)
            g.iota(sh.steps[:], pattern=[[P, NS + 1]], base=0, channel_multiplier=0,
                   allow_small_or_imprecise_dtypes=True).then_inc(ready, 1)
            pool.wait_ge(ready, 1)


def start_ffn_loads(sp, sh, d):
    sp.dma_start(sh.bo[:], d["bo"].partition_broadcast(P)).then_inc(sh.ffn_in, 16)
    sp.dma_start(sh.gamma[:], d["ln_gamma"].partition_broadcast(P)).then_inc(sh.ffn_in, 16)
    sp.dma_start(sh.beta[:], d["ln_beta"].partition_broadcast(P)).then_inc(sh.ffn_in, 16)
    for e in range(E):
        sp.dma_start(sh.b1[:, e, :], d["b1"][e].partition_broadcast(P)).then_inc(sh.ffn_in, 16)
        sp.dma_start(sh.w1[:, e, :, :], d["W1"][e].rearrange("(c p) i -> p c i", p=P)).then_inc(sh.ffn_in, 16)
    sp.dma_start(sh.wo[:], d["Wo"].rearrange("(c p) n -> p c n", p=P)).then_inc(sh.ffn_in, 16)


FFN_LOADED = 16 * (3 + 2 * E + 1)


def at_least(eng, sem, value):
    if not isinstance(value, int) or value > 0:
        eng.wait_ge(sem, value)


def over(eng, total, step, tail=0):
    pairs = (total - tail) // 2
    step(0, 0, 0)
    step(1, 0, 1)
    with eng.Fori(1, pairs) as k:
        for u in range(2):
            step(2 * k + u, k, u)
    for j in range(2 * pairs, total):
        step(j, j // 2, j % 2)


def choose_experts(sh, src, onehot, extra_loads=None):
    nc = sh.nc
    src_v = src.rearrange("(b t p) c -> b p t c", p=P, t=TB)
    with ExitStack() as own:
        x = [sh.sb("x_in", [P, TB, C], ctx=own) for _ in range(2)]
        xn = [sh.sb("xn", [P, TB, C], ctx=own) for _ in range(2)]
        xt = [sh.sb("xn_t", [P, CC, T], ctx=own) for _ in range(2)]
        st = sh.sb("stats", [P, TB, 6], ctx=own)
        mv = sh.sb("mean_var", [P, TB, 2], ctx=own)
        ve = sh.sb("var_eps", [P, TB], ctx=own)
        rs = sh.sb("rstd", [P, TB], ctx=own)
        mx = sh.sb("top", [P, TB, 1], ctx=own)
        sc = sh.sb("score", [P, TB, E], ctx=own)
        rank = sh.sb("rank", [P, TB, E], ctx=own)
        pt = [sh.ps("ps_xt", [P, CC, T], ctx=own) for _ in range(2)]
        pl = sh.ps("ps_logit", [P, TB, E], ctx=own)

        x_in = [sh.sem("x_in") for _ in range(2)]
        did_aggr = sh.sem("did_aggr")
        did_var = sh.sem("did_var")
        did_rstd = sh.sem("did_rstd")
        did_xn = sh.sem("did_xn")
        did_pt = sh.sem("did_transposes")
        did_xt = sh.sem("did_xt")
        did_logit = sh.sem("did_logit")
        did_top = sh.sem("did_top")
        did_eq = sh.sem("did_eq")
        did_sc = sh.sem("did_score")
        did_best = sh.sem("did_best")
        did_hot = sh.sem("did_onehot")
        did_rank = sh.sem("did_rank")
        with nc.Block() as block:

            @block.sync
            def _(sp):
                sp.dma_start(x[0][:], src_v[0]).then_inc(x_in[0], 16)
                sp.dma_start(x[1][:], src_v[1]).then_inc(x_in[1], 16)
                if extra_loads:
                    extra_loads(sp)
                with sp.Fori(1, B // 2) as k:
                    for u in range(2):
                        sp.wait_ge(did_xn, 2 * k + u - 1)
                        sp.dma_start(x[u][:], src_v[ds(2 * k + u)].rearrange("a p t c -> (a p) t c")
                                     ).then_inc(x_in[u], 16)

            @block.gpsimd
            def _(pool):
                g = nc.gpsimd
                g.iota(rank[:], pattern=[[0, TB], [-1, E]], base=E, channel_multiplier=0,
                       allow_small_or_imprecise_dtypes=True).then_inc(did_rank, 1)

                def step(b, k, u):
                    pool.wait_ge(did_var, b + 1)
                    at_least(pool, did_xn, b)
                    g.tensor_tensor(rs[:], ve[:], sh.lane[:, 0:TB], ALU.pow).then_inc(did_rstd, 1)

                over(pool, B, step)

            @block.vector
            def _(dve):
                v = nc.vector
                dve.wait_ge(did_rank, 1)

                def step(b, k, u):
                    dve.wait_ge(x_in[u], 16 * k + 16)
                    for t in range(TB):
                        v.bn_stats(st[:, t, :], x[u][:, t, :])
                    dve.drain()
                    for t in range(TB):
                        s = v.bn_aggr(mv[:, t, :], st[:, t, :])
                    s.then_inc(did_aggr, 1)
                    dve.wait_ge(did_aggr, b + 1)
                    at_least(dve, did_rstd, b)
                    v.tensor_scalar(ve[:], mv[:, :, 1], LN_EPS, None, ALU.add).then_inc(did_var, 1)
                    dve.wait_ge(did_rstd, b + 1)
                    at_least(dve, did_pt, b)
                    for t in range(TB):
                        s = v.tensor_scalar(xn[u][:, t, :], x[u][:, t, :], mv[:, t, 0:1], rs[:, t:t + 1],
                                            ALU.subtract, ALU.mult)
                    s.then_inc(did_xn, 1)
                    dve.wait_ge(did_logit, b + 1)
                    v.tensor_reduce(mx[:], pl[:], AX.X, ALU.max).then_inc(did_top, 1)
                    dve.wait_ge(did_top, b + 1)
                    v.tensor_tensor(sc[:], pl[:], mx[:].to_broadcast([P, TB, E]), ALU.is_equal
                                    ).then_inc(did_eq, 1)
                    dve.wait_ge(did_eq, b + 1)
                    v.tensor_tensor(sc[:], sc[:], rank[:], ALU.mult).then_inc(did_sc, 1)
                    dve.wait_ge(did_sc, b + 1)
                    v.tensor_reduce(mx[:], sc[:], AX.X, ALU.max).then_inc(did_best, 1)
                    dve.wait_ge(did_best, b + 1)
                    v.tensor_tensor(onehot[:, ds(TB * b, TB), :], sc[:], mx[:].to_broadcast([P, TB, E]),
                                    ALU.is_equal).then_inc(did_hot, 1)
                    dve.wait_ge(did_hot, b + 1)

                over(dve, B, step)

            @block.tensor
            def _(pe):
                pe.wait_ge(sh.router_in, 16)

                def step(b, k, u):
                    pe.wait_ge(did_xn, b + 1)
                    at_least(pe, did_xt, b)
                    for c in range(CC):
                        for t in range(TB):
                            m = nc.tensor.transpose(pt[u][:, c, t * P:(t + 1) * P],
                                                    xn[u][:, t, c * P:(c + 1) * P], sh.ident[:])
                    m.then_inc(did_pt, 1)
                    pe.wait_ge(did_xt, b + 1)
                    at_least(pe, did_hot, b)
                    for t in range(TB):
                        for c in range(CC):
                            m = nc.tensor.matmul(pl[:, t, :], xt[u][:, c, t * P:(t + 1) * P],
                                                 sh.w_router[:, c, :], start=(c == 0), stop=(c == CC - 1))
                    m.then_inc(did_logit, 1)

                over(pe, B, step)

            @block.scalar
            def _(act):

                def step(b, k, u):
                    act.wait_ge(did_pt, b + 1)
                    at_least(act, did_logit, b)
                    for c in range(CC):
                        s = nc.scalar.activation(xt[u][:, c, :], pt[u][:, c, :], ACT.Copy)
                    s.then_inc(did_xt, 1)

                over(act, B, step)


def place_tokens(sh, onehot, index, expert):
    nc = sh.nc
    with ExitStack() as own:
        a = lambda name, shape, dt=F32: sh.sb(name, shape, dt, ctx=own)
        upto = a("upto", [P, E, NT])
        more = a("more", [P, E, NT])
        tiles = a("tiles", [P, E])
        ends = a("ends", [P, E])
        first = a("first", [P, E])
        slots = a("slots", [P, NT, E])
        slots2 = a("slots2", [P, NT, E])
        slot = a("slot", [P, NT])
        beyond = a("beyond", [P, NT, NS])
        tile_of = a("tile_of", [P, NT])
        row_of = a("row_of", [P, NT])
        is_row = a("is_row", [P, NT, P])
        is_tile = a("is_tile", [P, NT, NS])
        kind = a("kind", [P, 3, NS])
        pp = sh.ps("ps_prefix", [P, 2, NT, E], ctx=own)
        pi = sh.ps("ps_index", [P, NS], ctx=own)
        did_sums = sh.sem("did_sums")
        did_inverse = sh.sem("did_inverse")
        did = sh.sem("placing")
        with nc.Block() as block:

            @block.tensor
            def _(pe):
                flat = onehot[:].rearrange("p t e -> p (t e)")
                nc.tensor.matmul(pp[:, 0, :, :].rearrange("p t e -> p (t e)"), sh.before[:], flat,
                                 start=True, stop=True)
                nc.tensor.matmul(pp[:, 1, :, :].rearrange("p t e -> p (t e)"), sh.ones[:], flat,
                                 start=True, stop=True).then_inc(did_sums, 1)
                pe.wait_ge(did, STEPS_TO_ROWS)
                for t in range(NT):
                    m = nc.tensor.matmul(pi[:], is_row[:, t, :], is_tile[:, t, :], start=(t == 0), stop=(t == NT - 1))
                m.then_inc(did_inverse, 1)

            @block.vector
            def _(dve):
                v = nc.vector
                n = [0]

                def step(ins):
                    n[0] += 1
                    ins.then_inc(did, 1)
                    dve.wait_ge(did, n[0])

                dve.wait_ge(did_sums, 1)
                for e in range(E):
                    s = v.tensor_tensor_scan(upto[:, e, :], sh.ones[:, 0:NT], pp[:, 1, :, e], 0.0, ALU.mult, ALU.add)
                step(s)
                step(v.tensor_tensor(more[:], upto[:, :, NT - 1:NT].to_broadcast([P, E, NT]),
                                     sh.steps[:, 0:NT].unsqueeze(1).to_broadcast([P, E, NT]), ALU.is_gt))
                step(v.tensor_reduce(tiles[:].unsqueeze(2), more[:], AX.X, ALU.add))
                step(v.tensor_tensor_scan(ends[:], sh.ones[:, 0:E], tiles[:], 0.0, ALU.mult, ALU.add))
                step(v.tensor_tensor(first[:], ends[:], tiles[:], ALU.subtract))
                step(v.tensor_tensor(slots[:], upto[:].rearrange("p e t -> p t e"), pp[:, 1, :, :], ALU.subtract))
                step(v.tensor_tensor(slots[:], slots[:], pp[:, 0, :, :], ALU.add))
                for e in range(E):
                    s = v.scalar_tensor_tensor(slots2[:, :, e], first[:, e:e + 1].to_broadcast([P, NT]), float(P),
                                               slots[:, :, e], ALU.mult, ALU.add)
                step(s)
                step(v.tensor_tensor(slots2[:], slots2[:], onehot[:], ALU.mult))
                step(v.tensor_reduce(slot[:].unsqueeze(2), slots2[:], AX.X, ALU.add))
                step(v.tensor_tensor(beyond[:], slot[:].unsqueeze(2).to_broadcast([P, NT, NS]),
                                     sh.steps[:, 1:NS + 1].unsqueeze(1).to_broadcast([P, NT, NS]), ALU.is_ge))
                step(v.tensor_reduce(tile_of[:].unsqueeze(2), beyond[:], AX.X, ALU.add))
                step(v.scalar_tensor_tensor(row_of[:], tile_of[:], -float(P), slot[:], ALU.mult, ALU.add))
                step(v.tensor_tensor(is_tile[:], tile_of[:].unsqueeze(2).to_broadcast([P, NT, NS]),
                                     sh.count[:, 0:NS].unsqueeze(1).to_broadcast([P, NT, NS]), ALU.is_equal))
                step(v.tensor_tensor(is_tile[:], is_tile[:], sh.token[:].unsqueeze(2).to_broadcast([P, NT, NS]),
                                     ALU.mult))
                step(v.tensor_tensor(is_row[:], row_of[:].unsqueeze(2).to_broadcast([P, NT, P]),
                                     sh.count[:].unsqueeze(1).to_broadcast([P, NT, P]), ALU.is_equal))
                assert n[0] == STEPS_TO_ROWS
                for e in range(1, E):
                    s = v.tensor_scalar(kind[:, e - 1, :], sh.count[:, 0:NS], first[:, e:e + 1], None, ALU.is_ge)
                step(s)
                step(v.tensor_tensor(kind[:, 0, :], kind[:, 0, :], kind[:, 1, :], ALU.add))
                step(v.tensor_tensor(expert[:], kind[0:1, 0, :], kind[0:1, 2, :], ALU.add))
                dve.wait_ge(did_inverse, 1)
                step(v.tensor_scalar(index[:], pi[:], float(NONE), None, ALU.add))


STEPS_TO_ROWS = 16


def ffn(sh, src, dst, index, expert):
    nc = sh.nc
    with ExitStack() as own:
        a = lambda name, shape, dt=F32: sh.sb(name, shape, dt, ctx=own)
        two = lambda name, shape, dt=F32: [a(name, shape, dt) for _ in range(2)]
        gi = two("gather_index", [P, 1], U32)
        si = two("scatter_index", [P, 1], U32)
        x = two("x_slot", [P, C])
        xn = two("xn_slot", [P, C])
        xn_bo = a("xn_plus_bo", [P, NS, C])
        x_beta = a("x_plus_beta", [P, NS, C])
        xt = two("xn_slot_t", [P, CC, P])
        hb = two("hidden_biased", [P, I])
        hg = two("hidden", [P, I])
        ht = two("hidden_t", [P, IC, P])
        z = a("z", [P, C])
        zn = a("zn", [P, C])
        zg = a("zg", [P, C])
        out = two("out_rows", [P, C])
        st = [a("stats", [P, 6]) for _ in range(2)]
        mv = [a("mean_var", [P, 2]) for _ in range(2)]
        ve = [a("var_eps", [P, 1]) for _ in range(2)]
        rs = [a("rstd", [P, 1]) for _ in range(2)]
        p_xt = sh.ps("ps_xt", [P, HB], ctx=own)
        p_h = sh.ps("ps_h", [P, NH, HB], ctx=own)
        p_ht = sh.ps("ps_ht", [P, 2, HB], ctx=own)
        p_y = sh.ps("ps_y", [P, HB], ctx=own)

        halved = sh.sem("halved")
        cleared = sh.sem("cleared")
        got_x = [sh.sem("got_x") for _ in range(2)]
        stored = [sh.sem("stored") for _ in range(2)]
        names = ("x_aggr x_var x_rstd xn_made x_beta_made xn_bo_made xt_ps xt_made h_ps h_biased h_made "
                 "ht_ps ht_made y_ps z_made z_aggr z_var z_rstd zn_made zg_made out_made")
        s = {k: sh.sem(k) for k in names.split()}

        with nc.Block() as block:

            @block.gpsimd
            def _(pool):
                g = nc.gpsimd
                last_token = pool.to_reg(NTOK - 1)

                def gather(j, u):
                    g.tensor_copy(gi[u][:], index[:, ds(j)])
                    pool.drain()
                    g.indirect_dma_start(out=x[u][:], out_offset=None, in_=src,
                                         in_offset=bass.IndirectOffsetOnAxis(ap=gi[u][:, 0:1], axis=0),
                                         bounds_check=last_token, oob_is_err=False).then_inc(got_x[u], 16)

                def pre(j, u):
                    pool.wait_ge(s["x_var"], j + 1)
                    g.tensor_tensor(rs[0][:], ve[0][:], sh.lane[:, 0:1], ALU.pow).then_inc(s["x_rstd"], 1)
                    g.tensor_tensor(x_beta[:, ds(j), :], x[u][:].unsqueeze(1), sh.beta[:].unsqueeze(1), ALU.add
                                    ).then_inc(s["x_beta_made"], 1)
                    pool.wait_ge(s["xn_made"], j + 1)
                    g.tensor_tensor(xn_bo[:, ds(j), :], xn[u][:].unsqueeze(1), sh.bo[:].unsqueeze(1), ALU.add
                                    ).then_inc(s["xn_bo_made"], 1)

                g.memset(x[0][:], 0.0)
                g.memset(x[1][:], 0.0).then_inc(cleared, 1)
                pool.wait_ge(cleared, 1)
                gather(0, 0)
                gather(1, 1)
                pool.wait_ge(sh.ffn_in, FFN_LOADED)
                if not sh.halved:
                    pool.wait_ge(halved, 1)
                for j in range(2):
                    pre(j, j)
                    pool.wait_ge(s["x_beta_made"], j + 1)
                    gather(j + 2, j)

                def step(j, k, u):
                    if not isinstance(j, int) or j + 2 < NS:
                        pre(j + 2, u)
                    if not isinstance(j, int) or j + 4 < NS:
                        pool.wait_ge(s["x_beta_made"], j + 3)
                        gather(j + 4, u)
                    pool.wait_ge(s["z_var"], j + 1)
                    g.tensor_tensor(rs[1][:], ve[1][:], sh.lane[:, 0:1], ALU.pow).then_inc(s["z_rstd"], 1)
                    at_least(pool, stored[u], 16 * k)
                    pool.wait_ge(s["out_made"], j + 1)
                    g.tensor_copy(si[u][:], index[:, ds(j)])
                    pool.drain()
                    g.indirect_dma_start(out=dst, out_offset=bass.IndirectOffsetOnAxis(ap=si[u][:, 0:1], axis=0),
                                         in_=out[u][:], in_offset=None,
                                         bounds_check=last_token, oob_is_err=False).then_inc(stored[u], 16)

                over(pool, NS, step, tail=4)
                pool.wait_ge(stored[0], 16 * ((NS + 1) // 2))
                pool.wait_ge(stored[1], 16 * (NS // 2))

            @block.vector
            def _(dve):
                v = nc.vector
                reg = None

                def x_stats(j, k, u):
                    dve.wait_ge(got_x[u], 16 * k + 16)
                    at_least(dve, s["xn_made"], j)
                    v.bn_stats(st[0][:], x[u][:])
                    dve.drain()
                    v.bn_aggr(mv[0][:], st[0][:]).then_inc(s["x_aggr"], 1)
                    dve.wait_ge(s["x_aggr"], j + 1)
                    v.tensor_scalar(ve[0][:], mv[0][:, 1:2], LN_EPS, None, ALU.add).then_inc(s["x_var"], 1)

                def x_norm(j, u):
                    dve.wait_ge(s["x_rstd"], j + 1)
                    at_least(dve, s["xn_bo_made"], j - 1)
                    at_least(dve, s["xt_ps"], j - 1)
                    v.tensor_scalar(xn[u][:], x[u][:], mv[0][:, 0:1], rs[0][:], ALU.subtract, ALU.mult
                                    ).then_inc(s["xn_made"], 1)

                def bias(j, u):
                    e = dve.value_load(expert[0:1, ds(j)], min_val=0, max_val=E - 1)
                    for n in range(NH):
                        dve.wait_ge(s["h_ps"], NH * j + n + 1)
                        at_least(dve, s["h_made"], NH * (j - 2) + n + 1)
                        v.tensor_tensor(hb[u][:, n * HB:(n + 1) * HB].unsqueeze(1), p_h[:, n, :].unsqueeze(1),
                                        sh.b1[:, ds(e), n * HB:(n + 1) * HB], ALU.add).then_inc(s["h_biased"], 1)

                dve.wait_ge(sh.ffn_in, FFN_LOADED)
                if not sh.halved:
                    v.tensor_scalar(sh.gamma[:], sh.gamma[:], 0.5, None, ALU.mult)
                    v.tensor_scalar(sh.beta[:], sh.beta[:], 0.5, None, ALU.mult).then_inc(halved, 1)
                    dve.wait_ge(halved, 1)
                for j in range(2):
                    x_stats(j, 0, j)
                    x_norm(j, j)
                bias(0, 0)

                def step(j, k, u):
                    known = isinstance(j, int)
                    if not known or j + 2 < NS:
                        x_stats(j + 2, k + 1, u)
                    if not known or j + 1 < NS:
                        bias(j + 1, 1 - u)
                    if not known or j + 2 < NS:
                        x_norm(j + 2, u)
                    dve.wait_ge(s["y_ps"], j + 1)
                    dve.wait_ge(s["xn_bo_made"], j + 1)
                    v.tensor_tensor(z[:].unsqueeze(1), p_y[:, 0:C].unsqueeze(1), xn_bo[:, ds(j), :], ALU.add
                                    ).then_inc(s["z_made"], 1)
                    dve.wait_ge(s["z_made"], j + 1)
                    v.bn_stats(st[1][:], z[:])
                    dve.drain()
                    v.bn_aggr(mv[1][:], st[1][:]).then_inc(s["z_aggr"], 1)
                    dve.wait_ge(s["z_aggr"], j + 1)
                    v.tensor_scalar(ve[1][:], mv[1][:, 1:2], FFN_EPS, None, ALU.add).then_inc(s["z_var"], 1)
                    dve.wait_ge(s["z_rstd"], j + 1)
                    v.tensor_scalar(zn[:], z[:], mv[1][:, 0:1], rs[1][:], ALU.subtract, ALU.mult
                                    ).then_inc(s["zn_made"], 1)
                    dve.wait_ge(s["zn_made"], j + 1)
                    v.tensor_tensor(zg[:], zn[:], sh.gamma[:], ALU.mult).then_inc(s["zg_made"], 1)
                    dve.wait_ge(s["zg_made"], j + 1)
                    at_least(dve, stored[u], 16 * k)
                    v.tensor_tensor(out[u][:].unsqueeze(1), zg[:].unsqueeze(1), x_beta[:, ds(j), :], ALU.add
                                    ).then_inc(s["out_made"], 1)

                over(dve, NS, step, tail=4)

            @block.tensor
            def _(pe):
                mm = nc.tensor

                def xt_transposes(j, u):
                    pe.wait_ge(s["xn_made"], j + 1)
                    at_least(pe, s["xt_made"], j)
                    for c in range(CC):
                        m = mm.transpose(p_xt[:, c * P:(c + 1) * P], xn[u][:, c * P:(c + 1) * P], sh.ident[:])
                    m.then_inc(s["xt_ps"], 1)

                def hidden(j, u):
                    e = pe.value_load(expert[0:1, ds(j)], min_val=0, max_val=E - 1)
                    pe.wait_ge(s["xt_made"], j + 1)
                    for n in range(NH):
                        at_least(pe, s["h_biased"], NH * (j - 1) + n + 1)
                        for c in range(CC):
                            m = mm.matmul(p_h[:, n, :], xt[u][:, c, :],
                                          sh.w1[:, ds(e), c, n * HB:(n + 1) * HB].rearrange("p a i -> p (a i)"),
                                          start=(c == 0), stop=(c == CC - 1))
                        m.then_inc(s["h_ps"], 1)

                def hidden_transposes(j, u):
                    for n in range(2):
                        pe.wait_ge(s["h_made"], NH * j + n + 1)
                        at_least(pe, s["ht_made"], 2 * (j - 1) + n + 1)
                        for q in range(IC // 2):
                            k = n * IC // 2 + q
                            m = mm.transpose(p_ht[:, n, q * P:(q + 1) * P], hg[u][:, k * P:(k + 1) * P], sh.ident[:])
                        m.then_inc(s["ht_ps"], 1)

                def second(j, u):
                    at_least(pe, s["z_made"], j)
                    for k in range(IC):
                        if k % (IC // 2) == 0:
                            pe.wait_ge(s["ht_made"], 2 * j + k // (IC // 2) + 1)
                        m = mm.matmul(p_y[:, 0:C], ht[u][:, k, :], sh.wo[:, k, :], start=(k == 0), stop=(k == IC - 1))
                    m.then_inc(s["y_ps"], 1)

                pe.wait_ge(sh.ffn_in, FFN_LOADED)
                xt_transposes(0, 0)
                hidden(0, 0)

                def step(j, k, u):
                    more = not isinstance(j, int) or j + 1 < NS
                    if more:
                        xt_transposes(j + 1, 1 - u)
                    hidden_transposes(j, u)
                    if more:
                        hidden(j + 1, 1 - u)
                    second(j, u)

                over(pe, NS, step, tail=4)

            @block.scalar
            def _(act):
                def xt_copy(j, u):
                    act.wait_ge(s["xt_ps"], j + 1)
                    at_least(act, s["h_ps"], NH * (j - 1))
                    nc.scalar.activation(xt[u][:].rearrange("p c k -> p (c k)"), p_xt[:, 0:C], ACT.Copy
                                         ).then_inc(s["xt_made"], 1)

                def gelu(j, u):
                    for n in range(NH):
                        act.wait_ge(s["h_biased"], NH * j + n + 1)
                        at_least(act, s["ht_ps"], 2 * (j - 1))
                        nc.scalar.activation(hg[u][:, n * HB:(n + 1) * HB], hb[u][:, n * HB:(n + 1) * HB], ACT.Gelu
                                             ).then_inc(s["h_made"], 1)

                def ht_copy(j, u):
                    for n in range(2):
                        act.wait_ge(s["ht_ps"], 2 * j + n + 1)
                        at_least(act, s["y_ps"], j - 1)
                        h = IC // 2
                        nc.scalar.activation(ht[u][:, n * h:(n + 1) * h, :].rearrange("p k t -> p (k t)"),
                                             p_ht[:, n, :], ACT.Copy).then_inc(s["ht_made"], 1)

                xt_copy(0, 0)
                gelu(0, 0)

                def step(j, k, u):
                    more = not isinstance(j, int) or j + 1 < NS
                    if more:
                        xt_copy(j + 1, 1 - u)
                    ht_copy(j, u)
                    if more:
                        gelu(j + 1, 1 - u)

                over(act, NS, step, tail=4)
        sh.halved = True


MIXES = 5
W_, K_, V_, R_, G_ = range(MIXES)
LORA, DLORA = 32, 64
H, N = 4, 64
HP = C // P
QC = T // P
GN_EPS = 1e-5 * 8 ** 2
HALVES = [1, 2, 4, 8, 16]
LAST = 7


class Banks:

    def __init__(self, sh, own, fills):
        self.ps = [sh.ps("bank", [P, HB], ctx=own) for _ in range(8)]
        self.full = [sh.sem(f"bank_full{j}") for j in range(8)]
        self.free = [sh.sem(f"bank_free{j}") for j in range(8)]
        self.at = {name: (k % 8, k // 8) for k, name in enumerate(fills)}
        self.per = [len(fills[j::8]) for j in range(8)]

    def open(self, pe, name, b):
        j, n = self.at[name]
        at_least(pe, self.free[j], b * self.per[j] + n)
        return self.ps[j]

    def filled(self, eng, name, b):
        j, n = self.at[name]
        at_least(eng, self.full[j], b * self.per[j] + n + 1)
        return self.ps[j]

    def emptied(self, eng, name, b):
        j, n = self.at[name]
        at_least(eng, self.free[j], b * self.per[j] + n + 1)

    def f(self, name):
        return self.full[self.at[name][0]]

    def e(self, name):
        return self.free[self.at[name][0]]


def load_attention(sh, d):
    sh.maa = sh.sb("maa", [P, MIXES + 1, CC])
    sh.mix1 = sh.sb("mix_w1", [P, CC, MIXES * LORA])
    sh.mix2a = sh.sb("mix_w2a", [4 * LORA, C])
    sh.mix2b = sh.sb("mix_w2b", [LORA, C])
    sh.dw1 = sh.sb("decay_w1", [P, CC, DLORA])
    sh.dw2 = sh.sb("decay_w2", [DLORA, C])
    sh.vecs = sh.sb("vectors", [P, 4, CC])
    sh.wm = {k: sh.sb(k, [P, CC, C]) for k in ("Wr", "Wk", "Wv", "Wg", "Wo")}
    sh.att_in = sh.sem("attention_in")


def start_attention_loads(q, sh, d):
    flat = lambda a: a.rearrange("(c p) -> p c", p=P)
    loads = [(sh.maa[:, n, :], flat(d["time_maa_" + k])) for n, k in enumerate("wkvrgx")]
    loads += [(sh.vecs[:, 0, :], flat(d["time_decay"])),
              (sh.vecs[:, 1, :], d["time_faaaa"].rearrange("(c h) n -> (h n) c", c=CC)),
              (sh.vecs[:, 2, :], flat(d["ln_w"])), (sh.vecs[:, 3, :], flat(d["ln_b"])),
              (sh.mix1[:], d["time_maa_w1"].rearrange("(c p) n -> p c n", p=P)),
              (sh.mix2a[:], d["time_maa_w2"][0:4].rearrange("s d c -> (s d) c")),
              (sh.mix2b[:], d["time_maa_w2"][4]),
              (sh.dw1[:], d["time_decay_w1"].rearrange("(c p) n -> p c n", p=P)),
              (sh.dw2[:], d["time_decay_w2"])]
    loads += [(sh.wm[k][:], d[k].rearrange("(c p) n -> p c n", p=P)) for k in ("Wr", "Wk", "Wv", "Wg", "Wo")]
    for to, of in loads:
        q.dma_start(to, of).then_inc(sh.att_in, 16)
    assert len(loads) == ATT_LOADS


ATT_LOADS = 20


def attention(sh, src, dst):
    nc = sh.nc
    src_v = src.rearrange("(b t p) c -> b p t c", p=P, t=TB)
    dst_v = dst.rearrange("(b t p) c -> b p t c", p=P, t=TB)
    quads = [(qp, hl) for qp in range(QC // 2) for hl in range(2)]
    mixing = [(s, c) for c in range(CC) for s in (W_, K_, R_, V_)] + [(G_, 0), (G_, 1)]
    levels = ["u"] + HALVES
    fills = ["xt0", "xt1", "mixa", "mixb"]
    fills += [f"m{s}{c}" for s, c in mixing]
    fills += ["d1", "k0", "k1", "r0", "r1", "d20", "d21", "v0", "v1", "g0", "g1"]
    fills += [f"a{m}{qp}{hl}" for m in levels for qp, hl in quads]
    fills += ["b0", "b1", "c0", "c1", "kt0", "kt1", "kv0", "kv1", "y0", "y1", "y2", "y3", "yt0", "yt1", "o0", "o1"]

    with ExitStack() as own:
        a = lambda name, shape, dt=F32: sh.sb(name, shape, dt, ctx=own)
        x = a("x_in", [P, TB, C])
        x_res = a("x_residual", [P, TB, C])
        out = a("x_out", [P, TB, C])
        mv = a("mean_var", [P, TB, 2])
        st = a("stats", [P, TB, 6])
        ve = a("var_eps", [P, TB])
        rs = a("rstd", [P, TB])
        xn = a("xn", [P, TB, C])
        xt = a("xn_t", [P, CC, T + 1])
        xx = a("shift_less_x", [P, CC, T])
        xxx = a("xxx", [P, CC, T])
        mixa = a("mix_a", [4 * LORA, T])
        mixb = a("mix_b", [LORA, T])
        xs = [a("x_mixed", [P, CC, T]) for _ in range(MIXES)]
        d1 = a("decay_hidden", [DLORA, T])
        ew = a("exp_w", [P, HP, T])
        tot = [a("block_decay", [P, HP, T >> m]) for m in range(LAST + 1)]
        ks = [a("K", [P, HP, T]) for _ in range(2)]
        rr = [a("R", [P, HP, T]) for _ in range(2)]
        ru = a("R_u", [P, HP, T])
        vv = a("v", [P, QC, C])
        gt = a("g_tanh", [P, CC, T])
        gh = a("g_half", [P, CC, T])
        wt = a("weights", [P, QC // 2, 2, 2 * HP, P])
        kt = a("K_rows", [P, QC - 1, HP, P])
        ss = a("state", [P, QC, HP, P])
        y = a("y", [P, QC, C])
        gst = a("y_stats", [P, QC * H, 6])
        gm = a("y_mean", [P, QC * H])
        gd = a("y_dif", [P, QC * H])
        gv = a("y_var", [P, QC * H])
        gr = a("y_rstd", [P, QC * H])
        yn = a("yn", [P, QC, C])
        yt = a("yn_t", [P, CC, T])
        diag = a("mask_diagonal", [P, P])
        mf = a("mask_float", [P, P])
        masks = {m: a(f"mask{m}", [P, P], U8) for m in HALVES}

        touched = {nc.vector: a("touched_dve", [P, 16]), nc.gpsimd: a("touched_pool", [P, 16])}
        touches = {nc.vector: 0, nc.gpsimd: 0}

        bk = Banks(sh, own, fills)
        names = ("x_var x_rstd xn_made xx_made xxx_made xs_made decay_made gate_made multiplied copied tot_made "
                 "s_made y_var y_rstd yn_made gated")
        s = {k: sh.sem(k) for k in names.split()}
        x_got = sh.sem("x_got")
        res_got = sh.sem("residual_got")
        stored = sh.sem("x_stored")
        masks_made = sh.sem("masks_made")
        mask_step = sh.sem("mask_step")
        zeroed = sh.sem("zeroed")

        def upto(eng, name, count):
            at_least(eng, s[name], count)

        def touch(eng, e):
            n = touches[eng] = touches[eng] + 1
            e.tensor_tensor(touched[eng][:, n:n + 1], sh.ones[:, 0:1], sh.ones[:, 0:1], ALU.mult)

        def over_b(eng, step):
            step(0)
            with eng.Fori(1, B) as b:
                step(b)

        def state_before(eng, q, b):
            if q == 1:
                eng.wait_ge(s["s_made"], b + 1)
            else:
                bk.emptied(eng, f"kv{q - 2}", b)

        def blocks(t, m):
            return t[:].rearrange("p h (n two m) -> p (h n) two m", two=2, m=m)

        with nc.Block() as block:

            @block.sync
            def _(sp):
                def load(b):
                    upto(sp, "xn_made", b)
                    sp.dma_start(x[:], src_v[ds(b)].rearrange("a p t c -> (a p) t c")).then_inc(x_got, 16)

                def step(b, last=False):
                    bk.emptied(sp, "o1", b - 1)
                    sp.dma_start(x_res[:], src_v[ds(b)].rearrange("a p t c -> (a p) t c")).then_inc(res_got, 16)
                    if not last:
                        load(b + 1)
                    bk.emptied(sp, "o1", b)
                    sp.dma_start(dst_v[ds(b)].rearrange("a p t c -> (a p) t c"), out[:]).then_inc(stored, 16)

                load(0)
                step(0)
                with sp.Fori(1, B - 1) as b:
                    step(b)
                step(B - 1, last=True)
                sp.wait_ge(stored, 16 * B)

            @block.gpsimd
            def _(pool):
                g = nc.gpsimd
                g.memset(xt[:, :, 0:1], 0.0)
                g.memset(ss[:], 0.0).then_inc(zeroed, 1)
                n = 0
                for m in HALVES:
                    v4 = lambda z: z.rearrange("p (b h m) -> p b h m", h=2, m=m)
                    nb = P // (2 * m)
                    g.memset(mf[:], 1.0).then_inc(mask_step, 1)
                    pool.wait_ge(mask_step, n + 1)
                    g.affine_select(out=v4(mf[:]), in_=v4(mf[:]), compare_op=ALU.is_gt, fill=0.0, base=0,
                                    pattern=[[0, nb], [1, 2], [0, m]], channel_multiplier=0).then_inc(mask_step, 1)
                    pool.wait_ge(mask_step, n + 2)
                    g.affine_select(out=v4(mf[:]), in_=v4(mf[:]), compare_op=ALU.is_ge, fill=0.0, base=0,
                                    pattern=[[-2 * m, nb], [0, 2], [0, m]], channel_multiplier=1
                                    ).then_inc(mask_step, 1)
                    pool.wait_ge(mask_step, n + 3)
                    g.affine_select(out=v4(mf[:]), in_=v4(mf[:]), compare_op=ALU.is_gt, fill=0.0, base=m,
                                    pattern=[[2 * m, nb], [0, 2], [0, m]], channel_multiplier=-1
                                    ).then_inc(mask_step, 1)
                    pool.wait_ge(mask_step, n + 4)
                    g.tensor_copy(masks[m][:], mf[:]).then_inc(mask_step, 1)
                    pool.wait_ge(mask_step, n + 5)
                    n += 5
                g.tensor_copy(diag[:], sh.ident[:]).then_inc(masks_made, 1)

                def step(b):
                    touches[pool] = 0
                    upto(pool, "x_var", b + 1)
                    upto(pool, "xn_made", b)
                    g.tensor_tensor(rs[:], ve[:], sh.lane[:, 0:TB], ALU.pow).then_inc(s["x_rstd"], 1)
                    for i, c in mixing:
                        bk.emptied(pool, f"m{i}{c}", b)
                        g.tensor_tensor(xs[i][:, c, :], xs[i][:, c, :], xt[:, c, 1:T + 1], ALU.add
                                        ).then_inc(s["xs_made"], 1)
                    bk.emptied(pool, "r1", b)
                    for n in range(LAST):
                        m = 1 << n
                        old, new = n % 2, (n + 1) % 2
                        upto(pool, "multiplied", LAST * b + n)
                        if n:
                            bk.filled(pool, f"a{levels[n]}11", b) if n <= 5 else bk.filled(pool, "b1", b)
                        else:
                            bk.filled(pool, "y3", b - 1)
                            bk.filled(pool, "kt1", b - 1)
                        touch(pool, g)
                        g.tensor_copy(blocks(ks[new], m)[:, :, 1, :], blocks(ks[old], m)[:, :, 1, :])
                        g.tensor_copy(blocks(rr[new], m)[:, :, 0, :], blocks(rr[old], m)[:, :, 0, :]
                                      ).then_inc(s["copied"], 1)
                        pool.wait_ge(s["copied"], LAST * b + n + 1)
                    upto(pool, "y_var", b + 1)
                    upto(pool, "yn_made", b)
                    g.tensor_tensor(gr[:], gv[:], sh.lane[:, 0:QC * H], ALU.pow).then_inc(s["y_rstd"], 1)

                over_b(pool, step)

            @block.vector
            def _(dve):
                v = nc.vector
                dve.wait_ge(zeroed, 1)
                dve.wait_ge(masks_made, 1)
                dve.wait_ge(sh.att_in, 16 * ATT_LOADS)

                def double(b, n):
                    m = 1 << n
                    old, new = n % 2, (n + 1) % 2
                    if n == 0:
                        bk.emptied(dve, "r1", b)
                        upto(dve, "decay_made", b + 1)
                        bk.filled(dve, "y3", b - 1)
                        bk.filled(dve, "kt1", b - 1)
                    else:
                        upto(dve, "copied", LAST * b + n)
                        bk.filled(dve, f"a{levels[n]}11" if n <= 5 else "b1", b)
                        dve.wait_ge(s["tot_made"], LAST * b + n)
                    t2 = tot[n][:].rearrange("p h (n two) -> p (h n) two", two=2)
                    shape = [P, HP * T // (2 * m), m]
                    v.tensor_tensor(blocks(ks[new], m)[:, :, 0, :], blocks(ks[old], m)[:, :, 0, :],
                                    t2[:, :, 1:2].to_broadcast(shape), ALU.mult)
                    v.tensor_tensor(blocks(rr[new], m)[:, :, 1, :], blocks(rr[old], m)[:, :, 1, :],
                                    t2[:, :, 0:1].to_broadcast(shape), ALU.mult).then_inc(s["multiplied"], 1)
                    v.tensor_tensor(tot[n + 1][:].rearrange("p h n -> p (h n)"), t2[:, :, 0], t2[:, :, 1], ALU.mult
                                    ).then_inc(s["tot_made"], 1)
                    dve.wait_ge(s["multiplied"], LAST * b + n + 1)

                def masked(b, n):
                    m = levels[n]
                    for qp in range(QC // 2):
                        both = [f"a{m}{qp}{hl}" for hl in range(2)]
                        ps = [bk.filled(dve, name, b)[:].rearrange("p (n t) -> p n t", t=P) for name in both]
                        if n == 0:
                            for hl in range(2):
                                v.tensor_tensor(wt[:, qp, hl, :, :], ps[hl],
                                                diag[:].unsqueeze(1).to_broadcast([P, 2 * HP, P]), ALU.mult
                                                ).then_inc(bk.e(both[hl]), 1)
                        else:
                            bk.emptied(dve, f"a{levels[n - 1]}{qp}0", b)
                            bk.emptied(dve, f"a{levels[n - 1]}{qp}1", b)
                            touch(dve, v)
                            for hl in range(2):
                                v.copy_predicated(wt[:, qp, hl, :, :],
                                                  masks[m][:].unsqueeze(1).to_broadcast([P, 2 * HP, P]), ps[hl]
                                                  ).then_inc(bk.e(both[hl]), 1)

                def step(b):
                    touches[dve] = 0
                    dve.wait_ge(x_got, 16 * b + 16)
                    for t in range(TB):
                        v.bn_stats(st[:, t, :], x[:, t, :])
                    dve.drain()
                    for t in range(TB):
                        v.bn_aggr(mv[:, t, :], st[:, t, :])
                    dve.drain()
                    v.tensor_scalar(ve[:], mv[:, :, 1], LN_EPS, None, ALU.add).then_inc(s["x_var"], 1)
                    dve.wait_ge(s["x_rstd"], b + 1)
                    bk.filled(dve, "xt1", b - 1)
                    for t in range(TB):
                        i = v.tensor_scalar(xn[:, t, :], x[:, t, :], mv[:, t, 0:1], rs[:, t:t + 1],
                                            ALU.subtract, ALU.mult)
                    i.then_inc(s["xn_made"], 1)
                    bk.emptied(dve, "xt1", b)
                    v.tensor_tensor(xx[:], xt[:, :, 0:T], xt[:, :, 1:T + 1], ALU.subtract).then_inc(s["xx_made"], 1)
                    dve.wait_ge(s["xx_made"], b + 1)
                    bk.filled(dve, "mixb", b - 1)
                    for c in range(CC):
                        i = v.scalar_tensor_tensor(xxx[:, c, :], xx[:, c, :], sh.maa[:, MIXES, c:c + 1],
                                                   xt[:, c, 1:T + 1], ALU.mult, ALU.add)
                    i.then_inc(s["xxx_made"], 1)
                    bk.filled(dve, "g1", b - 1)
                    for i_, c in mixing:
                        ps = bk.filled(dve, f"m{i_}{c}", b)
                        v.scalar_tensor_tensor(xs[i_][:, c, :], ps[:], sh.maa[:, i_, c:c + 1], xx[:, c, :],
                                               ALU.add, ALU.mult).then_inc(bk.e(f"m{i_}{c}"), 1)
                    double(b, 0)
                    bk.emptied(dve, "g1", b)
                    v.scalar_tensor_tensor(gt[:], gt[:], 1.0, gh[:], ALU.add, ALU.mult).then_inc(s["gate_made"], 1)
                    for n in range(1, LAST):
                        masked(b, n - 1)
                        double(b, n)
                    for q in range(QC - 1):
                        ps = bk.filled(dve, f"kv{q // 2}", b)
                        if q == 0:
                            bk.filled(dve, "y3", b - 1)
                            dve.wait_ge(s["tot_made"], LAST * b + LAST)
                        else:
                            state_before(dve, q, b)
                        for hp in range(HP):
                            for hl in range(2):
                                r_ = slice(hl * N, hl * N + N)
                                col = (q % 2) * C + hp * P + hl * N
                                i = v.scalar_tensor_tensor(ss[r_, q + 1, hp, r_], ss[r_, q, hp, r_],
                                                           tot[LAST][r_, hp, q:q + 1], ps[r_, col:col + N],
                                                           ALU.mult, ALU.add)
                        i.then_inc(s["s_made"] if q == 0 else bk.e(f"kv{q - 1}"), 1)
                    bk.emptied(dve, "y3", b)
                    for q in range(QC):
                        for h in range(H):
                            v.bn_stats(gst[:, q * H + h, :], y[:, q, h * N:(h + 1) * N])
                    dve.drain()
                    v.tensor_tensor(gm[:], gst[:, :, 1], gst[:, :, 4], ALU.add)
                    v.tensor_tensor(gd[:], gst[:, :, 1], gst[:, :, 4], ALU.subtract)
                    v.tensor_tensor(gv[:], gst[:, :, 2], gst[:, :, 5], ALU.add)
                    dve.drain()
                    v.tensor_scalar(gm[:], gm[:], 0.5, None, ALU.mult)
                    v.tensor_tensor(gd[:], gd[:], gd[:], ALU.mult)
                    dve.drain()
                    v.scalar_tensor_tensor(gv[:], gd[:], N / 4.0, gv[:], ALU.mult, ALU.add)
                    dve.drain()
                    v.tensor_scalar(gv[:], gv[:], 1.0 / N, GN_EPS, ALU.mult, ALU.add).then_inc(s["y_var"], 1)
                    dve.wait_ge(s["y_rstd"], b + 1)
                    bk.filled(dve, "yt1", b - 1)
                    for q in range(QC):
                        for h in range(H):
                            k = q * H + h
                            i = v.tensor_scalar(yn[:, q, h * N:(h + 1) * N], y[:, q, h * N:(h + 1) * N],
                                                gm[:, k:k + 1], gr[:, k:k + 1], ALU.subtract, ALU.mult)
                    i.then_inc(s["yn_made"], 1)
                    dve.wait_ge(s["gate_made"], b + 1)
                    bk.emptied(dve, "yt1", b)
                    v.tensor_tensor(yt[:], yt[:], gt[:], ALU.mult).then_inc(s["gated"], 1)
                    dve.wait_ge(res_got, 16 * b + 16)
                    at_least(dve, stored, 16 * b)
                    for n in range(2):
                        ps = bk.filled(dve, f"o{n}", b)
                        v.tensor_tensor(out[:, 2 * n:2 * n + 2, :].rearrange("p t c -> p (t c)"), ps[:],
                                        x_res[:, 2 * n:2 * n + 2, :].rearrange("p t c -> p (t c)"), ALU.add
                                        ).then_inc(bk.e(f"o{n}"), 1)

                over_b(dve, step)

            @block.tensor
            def _(pe):
                mm = nc.tensor
                pe.wait_ge(sh.att_in, 16 * ATT_LOADS)

                def project(name, b, w, xin, cols, m0=0, m1=P):
                    ps = bk.open(pe, name, b)
                    for c in range(CC):
                        i = mm.matmul(ps[m0:m1, :], w[:, c, cols], xin[:, c, :], start=(c == 0), stop=(c == CC - 1))
                    i.then_inc(bk.f(name), 1)

                def step(b):
                    pe.wait_ge(s["xn_made"], b + 1)
                    for c in range(CC):
                        ps = bk.open(pe, f"xt{c}", b)
                        for t in range(TB):
                            i = mm.transpose(ps[:, t * P:(t + 1) * P], xn[:, t, c * P:(c + 1) * P], sh.ident[:])
                        i.then_inc(bk.f(f"xt{c}"), 1)
                    pe.wait_ge(s["xxx_made"], b + 1)
                    project("mixa", b, sh.mix1, xxx, slice(0, 4 * LORA))
                    project("mixb", b, sh.mix1, xxx, slice(4 * LORA, 5 * LORA), 0, LORA)
                    bk.emptied(pe, "mixb", b)
                    for i_, c in mixing:
                        ps = bk.open(pe, f"m{i_}{c}", b)
                        rows = slice(i_ * LORA, (i_ + 1) * LORA) if i_ < 4 else slice(0, LORA)
                        w, mx = (sh.mix2a, mixa) if i_ < 4 else (sh.mix2b, mixb)
                        mm.matmul(ps[:], w[rows, c * P:(c + 1) * P], mx[rows, :], start=True, stop=True
                                  ).then_inc(bk.f(f"m{i_}{c}"), 1)
                    pe.wait_ge(s["xs_made"], 10 * b + 5)
                    project("d1", b, sh.dw1, xs[W_], slice(0, DLORA), 0, DLORA)
                    pe.wait_ge(s["xs_made"], 10 * b + 6)
                    for c in range(CC):
                        project(f"k{c}", b, sh.wm["Wk"], xs[K_], slice(c * P, (c + 1) * P))
                    pe.wait_ge(s["xs_made"], 10 * b + 7)
                    for c in range(CC):
                        project(f"r{c}", b, sh.wm["Wr"], xs[R_], slice(c * P, (c + 1) * P))
                    bk.emptied(pe, "d1", b)
                    for c in range(CC):
                        ps = bk.open(pe, f"d2{c}", b)
                        mm.matmul(ps[:], sh.dw2[:, c * P:(c + 1) * P], d1[:], start=True, stop=True
                                  ).then_inc(bk.f(f"d2{c}"), 1)
                    pe.wait_ge(s["xs_made"], 10 * b + 8)
                    for n in range(2):
                        ps = bk.open(pe, f"v{n}", b)
                        for q in (0, 1):
                            t = 2 * n + q
                            for c in range(CC):
                                i = mm.matmul(ps[:, q * C:(q + 1) * C], xs[V_][:, c, t * P:(t + 1) * P],
                                              sh.wm["Wv"][:, c, :], start=(c == 0), stop=(c == CC - 1))
                        i.then_inc(bk.f(f"v{n}"), 1)
                    pe.wait_ge(s["xs_made"], 10 * b + 10)
                    for c in range(CC):
                        project(f"g{c}", b, sh.wm["Wg"], xs[G_], slice(c * P, (c + 1) * P))

                    bk.emptied(pe, "r1", b)
                    for n, m in enumerate(levels):
                        buf = max(n - 1, 0) % 2
                        if n >= 2:
                            pe.wait_ge(s["multiplied"], LAST * b + n - 1)
                            pe.wait_ge(s["copied"], LAST * b + n - 1)
                        rhs = ru if m == "u" else rr[buf]
                        for qp in range(QC // 2):
                            ps = [bk.open(pe, f"a{m}{qp}{hl}", b) for hl in range(2)]
                            for q2 in range(2):
                                for hp in range(HP):
                                    t0 = (2 * qp + q2) * P
                                    col = (q2 * HP + hp) * P
                                    for hl in range(2):
                                        r_ = slice(hl * N, hl * N + N)
                                        i = mm.matmul(ps[hl][:, col:col + P], ks[buf][r_, hp, t0:t0 + P],
                                                      rhs[r_, hp, t0:t0 + P], start=True, stop=True)
                                        if q2 and hp == HP - 1:
                                            i.then_inc(bk.f(f"a{m}{qp}{hl}"), 1)
                    for name, lvl, m, r0s in (("b", 6, 32, (0, 64)), ("c", 7, 64, (0,))):
                        buf = (lvl - 1) % 2
                        pe.wait_ge(s["multiplied"], LAST * b + lvl - 1)
                        pe.wait_ge(s["copied"], LAST * b + lvl - 1)
                        ps = [bk.open(pe, f"{name}{hl}", b) for hl in range(2)]
                        for q in range(QC):
                            for hp in range(HP):
                                col = (q * HP + hp) * m
                                for r0 in r0s:
                                    for hl in range(2):
                                        r_ = slice(hl * N, hl * N + N)
                                        t0 = q * P + r0
                                        w = P if (q, hp, r0, hl) == (0, 0, 0, 0) else m
                                        i = mm.matmul(ps[hl][r0:r0 + w, col:col + m], ks[buf][r_, hp, t0:t0 + w],
                                                      rr[buf][r_, hp, t0 + m:t0 + 2 * m], start=True, stop=True)
                                        if (q, hp, r0) == (QC - 1, HP - 1, r0s[-1]):
                                            i.then_inc(bk.f(f"{name}{hl}"), 1)
                    pe.wait_ge(s["multiplied"], LAST * b + LAST)
                    pe.wait_ge(s["copied"], LAST * b + LAST)
                    buf = LAST % 2
                    for n in range(2):
                        ps = bk.open(pe, f"kt{n}", b)
                        for q in range(2 * n, min(2 * n + 2, QC - 1)):
                            for hp in range(HP):
                                col = ((q % 2) * HP + hp) * P
                                i = mm.transpose(ps[:, col:col + P], ks[buf][:, hp, q * P:(q + 1) * P], sh.ident[:])
                        i.then_inc(bk.f(f"kt{n}"), 1)
                    bk.emptied(pe, "v1", b)
                    for n in range(2):
                        bk.emptied(pe, f"kt{n}", b)
                        ps = bk.open(pe, f"kv{n}", b)
                        for q in range(2 * n, min(2 * n + 2, QC - 1)):
                            for hp in range(HP):
                                col = (q % 2) * C + hp * P
                                i = mm.matmul(ps[:, col:col + P], kt[:, q, hp, :], vv[:, q, hp * P:(hp + 1) * P],
                                              start=True, stop=True)
                        i.then_inc(bk.f(f"kv{n}"), 1)
                    bk.emptied(pe, "c1", b)
                    for q in range(QC):
                        ps = bk.open(pe, f"y{q}", b)
                        if q:
                            state_before(pe, q, b)
                        for hp in range(HP):
                            for hl in range(2):
                                col = hp * P + hl * N
                                if q:
                                    mm.matmul(ps[:, col:col + N], rr[buf][:, hp, q * P:(q + 1) * P],
                                              ss[:, q, hp, hl * N:(hl + 1) * N], start=True, stop=False)
                                i = mm.matmul(ps[:, col:col + N], wt[:, q // 2, hl, (q % 2) * HP + hp, :],
                                              vv[:, q, col:col + N], start=(q == 0), stop=True)
                        i.then_inc(bk.f(f"y{q}"), 1)
                    pe.wait_ge(s["yn_made"], b + 1)
                    for c in range(CC):
                        ps = bk.open(pe, f"yt{c}", b)
                        for q in range(QC):
                            i = mm.transpose(ps[:, q * P:(q + 1) * P], yn[:, q, c * P:(c + 1) * P], sh.ident[:])
                        i.then_inc(bk.f(f"yt{c}"), 1)
                    pe.wait_ge(s["gated"], b + 1)
                    for n in range(2):
                        ps = bk.open(pe, f"o{n}", b)
                        for q in (0, 1):
                            t = 2 * n + q
                            for c in range(CC):
                                i = mm.matmul(ps[:, q * C:(q + 1) * C], yt[:, c, t * P:(t + 1) * P],
                                              sh.wm["Wo"][:, c, :], start=(c == 0), stop=(c == CC - 1))
                        i.then_inc(bk.f(f"o{n}"), 1)

                over_b(pe, step)

            @block.scalar
            def _(act):
                ac = nc.scalar.activation
                act.wait_ge(sh.att_in, 16 * ATT_LOADS)

                def step(b):
                    upto(act, "xs_made", 10 * b)
                    for c in range(CC):
                        ps = bk.filled(act, f"xt{c}", b)
                        ac(xt[:, c, 1:T + 1], ps[:], ACT.Copy).then_inc(bk.e(f"xt{c}"), 1)
                    bk.filled(act, "m41", b - 1)
                    ac(mixa[:], bk.filled(act, "mixa", b)[:], ACT.Tanh).then_inc(bk.e("mixa"), 1)
                    ac(mixb[:], bk.filled(act, "mixb", b)[0:LORA, :], ACT.Tanh).then_inc(bk.e("mixb"), 1)
                    bk.filled(act, "d21", b - 1)
                    ac(d1[:], bk.filled(act, "d1", b)[0:DLORA, :], ACT.Tanh).then_inc(bk.e("d1"), 1)
                    bk.filled(act, "c1", b - 1)
                    upto(act, "multiplied", LAST * b)
                    upto(act, "copied", LAST * b)
                    for c in range(CC):
                        ac(ks[0][:, c, :], bk.filled(act, f"k{c}", b)[:], ACT.Copy).then_inc(bk.e(f"k{c}"), 1)
                    for c in range(CC):
                        ps = bk.filled(act, f"r{c}", b)
                        ac(rr[0][:, c, :], ps[:], ACT.Copy)
                        ac(ru[:, c, :], ps[:], ACT.Copy, scale=sh.vecs[:, 1, c:c + 1]).then_inc(bk.e(f"r{c}"), 1)
                    for c in range(CC):
                        ac(ew[:, c, :], bk.filled(act, f"d2{c}", b)[:], ACT.Exp, bias=sh.vecs[:, 0, c:c + 1]
                           ).then_inc(bk.e(f"d2{c}"), 1)
                    bk.emptied(act, "d21", b)
                    upto(act, "tot_made", LAST * b)
                    ac(tot[0][:], ew[:], ACT.Exp, scale=-1.0).then_inc(s["decay_made"], 1)
                    bk.filled(act, "y3", b - 1)
                    for n in range(2):
                        ac(vv[:, 2 * n:2 * n + 2, :].rearrange("p q c -> p (q c)"), bk.filled(act, f"v{n}", b)[:],
                           ACT.Copy).then_inc(bk.e(f"v{n}"), 1)
                    upto(act, "gated", b)
                    for c in range(CC):
                        ps = bk.filled(act, f"g{c}", b)
                        ac(gt[:, c, :], ps[:], ACT.Tanh, scale=0.5)
                        ac(gh[:, c, :], ps[:], ACT.Copy, scale=0.5).then_inc(bk.e(f"g{c}"), 1)
                    bk.emptied(act, "a1611", b)
                    for hl in range(2):
                        ps = bk.filled(act, f"b{hl}", b)
                        for i, r0 in enumerate((0, 64)):
                            ins = ac(wt[r0:r0 + 32, :, hl, :, r0 + 32:r0 + 64],
                                     ps[r0:r0 + 32, 0:256].rearrange("p (q n t) -> p q n t", q=QC // 2, t=32), ACT.Copy)
                        ins.then_inc(bk.e(f"b{hl}"), 1)
                    for hl in range(2):
                        ps = bk.filled(act, f"c{hl}", b)
                        ac(wt[0:64, :, hl, :, 64:128], ps[0:64, :].rearrange("p (q n t) -> p q n t", q=QC // 2, t=64),
                           ACT.Copy).then_inc(bk.e(f"c{hl}"), 1)
                    for n, cols in ((0, 512), (1, 256)):
                        ps = bk.filled(act, f"kt{n}", b)
                        bk.filled(act, "kv1", b - 1)
                        ac(kt[:, 2 * n:min(2 * n + 2, QC - 1), :, :].rearrange("p q h s -> p (q h s)"),
                           ps[:, 0:cols], ACT.Copy).then_inc(bk.e(f"kt{n}"), 1)
                    upto(act, "yn_made", b)
                    for q in range(QC):
                        ac(y[:, q, :], bk.filled(act, f"y{q}", b)[:, 0:C], ACT.Copy).then_inc(bk.e(f"y{q}"), 1)
                    bk.filled(act, "o1", b - 1)
                    for c in range(CC):
                        ac(yt[:, c, :], bk.filled(act, f"yt{c}", b)[:], ACT.Identity, bias=sh.vecs[:, 3, c:c + 1],
                           scale=sh.vecs[:, 2, c:c + 1]).then_inc(bk.e(f"yt{c}"), 1)

                over_b(act, step)


def macaron(nc, x, attn, ffn_in, out):
    x1 = nc.dram_tensor("after_ffn1", [NTOK, C], F32, kind="Internal").ap()
    x2 = nc.dram_tensor("after_attention", [NTOK, C], F32, kind="Internal").ap()
    with ExitStack() as ctx:
        sh = Shared(nc, ctx)
        load_constants(sh, ffn_in)
        load_attention(sh, attn)
        onehot = sh.sb("onehot", [P, NT, E])
        index = sh.sb("index", [P, NS], U32)
        expert = sh.sb("expert", [1, NS], I32)

        def other_loads(sp):
            start_ffn_loads(sp, sh, ffn_in)
            with nc.allow_non_contiguous_dma(reason="vectors of 256 to 128 partitions"):
                start_attention_loads(sp, sh, attn)

        choose_experts(sh, x, onehot, other_loads)
        place_tokens(sh, onehot, index, expert)
        ffn(sh, x, x1, index, expert)
        attention(sh, x1, x2)
        choose_experts(sh, x2, onehot)
        place_tokens(sh, onehot, index, expert)
        ffn(sh, x2, out, index, expert)


_ATTN = ["time_maa_x", "time_maa_w", "time_maa_k", "time_maa_v", "time_maa_r", "time_maa_g", "time_maa_w1",
         "time_maa_w2", "time_decay", "time_decay_w1", "time_decay_w2", "time_faaaa", "Wr", "Wk", "Wv", "Wg", "Wo",
         "ln_w", "ln_b"]
_FFN = ["W_router", "W1", "b1", "Wo", "bo", "ln_gamma", "ln_beta"]


def kernel(**inputs):
    import numpy as _np
    import concourse.bacc as _bacc
    from concourse import mybir as _mybir
    from concourse.bass_utils import run_bass_kernel_spmd as _run

    nc = _bacc.Bacc("TRN2", target_bir_lowering=False, num_devices=1)
    arrays = {}

    def given(name):
        a = _np.ascontiguousarray(inputs[name])
        arrays[f"in_{name}"] = a
        return nc.dram_tensor(f"in_{name}", a.shape, _mybir.dt.from_np(a.dtype), kind="ExternalInput").ap()

    x = given("L0_attn_x")
    attn = {k: given("L0_attn_" + k) for k in _ATTN}
    ffn_in = {k: given("L0_ffn_" + k) for k in _FFN}
    out = nc.dram_tensor("out_0", x.shape, F32, kind="ExternalOutput").ap()
    macaron(nc, x.rearrange("b t c -> (b t) c"), attn, ffn_in, out.rearrange("b t c -> (b t) c"))
    r = _run(nc, [arrays], core_ids=[0])
    return r.results[0]["out_0"]
```

```python
from contextlib import ExitStack

import concourse.bass as bass
from concourse import mybir

F32 = mybir.dt.float32
U32 = mybir.dt.uint32
I32 = mybir.dt.int32
U8 = mybir.dt.uint8
ALU = mybir.AluOpType
ACT = mybir.ActivationFunctionType
AX = mybir.AxisListType

P = 128
B, T, C = 8, 512, 256
NTOK = B * T
NT = NTOK // P
TB = T // P
CC = C // P
E = 4
I = 1024
IC = I // P
HB = 512
NH = I // HB
NS = NT + E - 1
NONE = 2 * NTOK
LN_EPS = 1e-5
FFN_EPS = 1e-12


def ds(i, n=1):
    return bass.ds(i, n)


class Shared:

    def __init__(self, nc, ctx):
        self.nc, self.ctx, self.n = nc, ctx, 0

    def sem(self, name):
        self.n += 1
        return self.ctx.enter_context(self.nc.semaphore(f"{name}_{self.n}"))

    def sb(self, name, shape, dt=F32, ctx=None):
        self.n += 1
        return (ctx or self.ctx).enter_context(self.nc.sbuf_tensor(f"{name}_{self.n}", shape, dt))

    def ps(self, name, shape, dt=F32, ctx=None):
        self.n += 1
        return (ctx or self.ctx).enter_context(self.nc.psum_tensor(f"{name}_{self.n}", shape, dt))


def load_constants(sh, d):
    nc = sh.nc
    sh.ident = sh.sb("ident", [P, P])
    sh.ones = sh.sb("ones", [P, P])
    sh.before = sh.sb("before", [P, P])
    sh.count = sh.sb("count", [P, P])
    sh.token = sh.sb("token", [P, NT])
    sh.steps = sh.sb("steps", [P, NS + 1])
    sh.w_router = sh.sb("w_router", [P, CC, E])
    sh.lane = sh.sb("minus_half", [P, HB // 8])

    sh.router_in = sh.sem("router_in")
    sh.built = sh.sem("built")
    ready = sh.sem("constants_ready")

    with nc.Block() as block:

        @block.sync
        def _(sp):
            sp.dma_start(sh.w_router[:], d["W_router"].rearrange("(c p) e -> p c e", p=P)).then_inc(sh.router_in, 16)

        @block.gpsimd
        def _(pool):
            g = nc.gpsimd
            g.memset(sh.ident[:], 0.0).then_inc(sh.built, 1)
            g.memset(sh.before[:], 1.0).then_inc(sh.built, 1)
            g.memset(sh.ones[:], 1.0)
            g.memset(sh.lane[:], -0.5)
            for padded in (sh.mix1, sh.mix2, sh.dw1, sh.dw2):
                g.memset(padded[:], 0.0)
            pool.wait_ge(sh.built, 2)
            g.affine_select(out=sh.ident[:], in_=sh.ident[:], compare_op=ALU.not_equal, fill=1.0, base=0,
                            pattern=[[-1, P]], channel_multiplier=1)
            g.affine_select(out=sh.before[:], in_=sh.before[:], compare_op=ALU.is_gt, fill=0.0, base=0,
                            pattern=[[1, P]], channel_multiplier=-1)
            g.iota(sh.count[:], pattern=[[1, P]], base=0, channel_multiplier=0, allow_small_or_imprecise_dtypes=True)
            g.iota(sh.token[:], pattern=[[P, NT]], base=-NONE, channel_multiplier=1,
                   allow_small_or_imprecise_dtypes=True)
            g.iota(sh.steps[:], pattern=[[P, NS + 1]], base=0, channel_multiplier=0,
                   allow_small_or_imprecise_dtypes=True).then_inc(ready, 1)
            pool.wait_ge(ready, 1)


def place_ffn_weights(sh, ctx):
    sh.w1 = sh.sb("w1", [P, E, CC, I], ctx=ctx)
    sh.b1 = sh.sb("b1", [P, E, I], ctx=ctx)
    sh.wo = sh.sb("wo_ffn", [P, IC, C], ctx=ctx)
    sh.bo = sh.sb("bo", [P, C], ctx=ctx)
    sh.gamma = sh.sb("gamma", [P, C], ctx=ctx)
    sh.beta = sh.sb("beta", [P, C], ctx=ctx)
    sh.ffn_in = sh.sem("ffn_in")


def start_ffn_loads(sp, sh, d):
    sp.dma_start(sh.bo[:], d["bo"].partition_broadcast(P)).then_inc(sh.ffn_in, 16)
    sp.dma_start(sh.gamma[:], d["ln_gamma"].partition_broadcast(P)).then_inc(sh.ffn_in, 16)
    sp.dma_start(sh.beta[:], d["ln_beta"].partition_broadcast(P)).then_inc(sh.ffn_in, 16)
    for e in range(E):
        sp.dma_start(sh.b1[:, e, :], d["b1"][e].partition_broadcast(P)).then_inc(sh.ffn_in, 16)
        sp.dma_start(sh.w1[:, e, :, :], d["W1"][e].rearrange("(c p) i -> p c i", p=P)).then_inc(sh.ffn_in, 16)
    sp.dma_start(sh.wo[:], d["Wo"].rearrange("(c p) n -> p c n", p=P)).then_inc(sh.ffn_in, 16)


FFN_LOADED = 16 * (3 + 2 * E + 1)


def at_least(eng, sem, value):
    if not isinstance(value, int) or value > 0:
        eng.wait_ge(sem, value)


def over(eng, total, step, tail=0):
    pairs = (total - tail) // 2
    step(0, 0, 0)
    step(1, 0, 1)
    with eng.Fori(1, pairs) as k:
        for u in range(2):
            step(2 * k + u, k, u)
    for j in range(2 * pairs, total):
        step(j, j // 2, j % 2)


def choose_experts(sh, src, onehot, extra_loads=None):
    nc = sh.nc
    src_v = src.rearrange("(b t p) c -> b p t c", p=P, t=TB)
    with ExitStack() as own:
        two = lambda name, shape: [sh.sb(name, shape, ctx=own) for _ in range(2)]
        x = sh.sb("x_in", [P, NT, C], ctx=own)
        xn = two("xn", [P, TB, C])
        xt = two("xn_t", [P, CC, T])
        st = sh.sb("stats", [P, TB, 6], ctx=own)
        mv = two("mean_var", [P, TB, 2])
        ve = two("var_eps", [P, TB])
        rs = two("rstd", [P, TB])
        mx = sh.sb("top", [P, TB, 1], ctx=own)
        sc = sh.sb("score", [P, TB, E], ctx=own)
        rank = sh.sb("rank", [P, TB, E], ctx=own)
        pt = [sh.ps("ps_xt", [P, CC, T], ctx=own) for _ in range(2)]
        pl = [sh.ps("ps_logit", [P, HB], ctx=own) for _ in range(2)]

        x_in = [sh.sem("x_in") for _ in range(2)]
        did_aggr = sh.sem("did_aggr")
        did_var = sh.sem("did_var")
        did_rstd = sh.sem("did_rstd")
        did_xn = sh.sem("did_xn")
        did_pt = sh.sem("did_transposes")
        did_xt = sh.sem("did_xt")
        did_logit = sh.sem("did_logit")
        did_top = sh.sem("did_top")
        did_eq = sh.sem("did_eq")
        did_sc = sh.sem("did_score")
        did_best = sh.sem("did_best")
        did_hot = sh.sem("did_onehot")
        did_rank = sh.sem("did_rank")
        with nc.Block() as block:

            @block.sync
            def _(sp):
                sp.dma_start(x[:, 0:TB, :], src_v[0]).then_inc(x_in[0], 16)
                sp.dma_start(x[:, TB:2 * TB, :], src_v[1]).then_inc(x_in[1], 16)
                with sp.Fori(1, B // 2) as k:
                    for u in range(2):
                        sp.wait_ge(x_in[u], 16 * k)
                        sp.dma_start(x[:, ds(TB * (2 * k + u), TB), :],
                                     src_v[ds(2 * k + u)].rearrange("a p t c -> (a p) t c")).then_inc(x_in[u], 16)
                if extra_loads:
                    extra_loads(sp)

            @block.gpsimd
            def _(pool):
                g = nc.gpsimd
                g.iota(rank[:], pattern=[[0, TB], [-1, E]], base=E, channel_multiplier=0,
                       allow_small_or_imprecise_dtypes=True).then_inc(did_rank, 1)

                def step(b, k, u):
                    pool.wait_ge(did_var, b + 1)
                    at_least(pool, did_xn, b - 1)
                    g.tensor_tensor(rs[u][:], ve[u][:], sh.lane[:, 0:TB], ALU.pow).then_inc(did_rstd, 1)

                over(pool, B, step)

            @block.vector
            def _(dve):
                v = nc.vector
                dve.wait_ge(did_rank, 1)

                def rows(b, t):
                    return x[:, TB * b + t, :] if isinstance(b, int) else \
                        x[:, ds(TB * b + t), :].rearrange("p a c -> p (a c)")

                def statistics(b, k, u):
                    dve.wait_ge(x_in[u], 16 * k + 16)
                    for t in range(TB):
                        v.bn_stats(st[:, t, :], rows(b, t))
                    dve.drain()
                    for t in range(TB):
                        s = v.bn_aggr(mv[u][:, t, :], st[:, t, :])
                    s.then_inc(did_aggr, 1)
                    dve.wait_ge(did_aggr, b + 1)
                    at_least(dve, did_rstd, b - 1)
                    v.tensor_scalar(ve[u][:], mv[u][:, :, 1], LN_EPS, None, ALU.add).then_inc(did_var, 1)

                def normalise(b, u):
                    dve.wait_ge(did_rstd, b + 1)
                    at_least(dve, did_pt, b - 1)
                    for t in range(TB):
                        s = v.tensor_scalar(xn[u][:, t, :], rows(b, t), mv[u][:, t, 0:1], rs[u][:, t:t + 1],
                                            ALU.subtract, ALU.mult)
                    s.then_inc(did_xn, 1)

                def choose(b, u):
                    logits = pl[u][:, 0:TB * E].rearrange("p (t e) -> p t e", e=E)
                    dve.wait_ge(did_logit, b + 1)
                    v.tensor_reduce(mx[:], logits, AX.X, ALU.max).then_inc(did_top, 1)
                    dve.wait_ge(did_top, b + 1)
                    v.tensor_tensor(sc[:], logits, mx[:].to_broadcast([P, TB, E]), ALU.is_equal
                                    ).then_inc(did_eq, 1)
                    dve.wait_ge(did_eq, b + 1)
                    v.tensor_tensor(sc[:], sc[:], rank[:], ALU.mult).then_inc(did_sc, 1)
                    dve.wait_ge(did_sc, b + 1)
                    v.tensor_reduce(mx[:], sc[:], AX.X, ALU.max).then_inc(did_best, 1)
                    dve.wait_ge(did_best, b + 1)
                    v.tensor_tensor(onehot[:, ds(TB * b, TB), :], sc[:], mx[:].to_broadcast([P, TB, E]),
                                    ALU.is_equal).then_inc(did_hot, 1)
                    dve.wait_ge(did_hot, b + 1)

                statistics(0, 0, 0)

                def step(b, k, u):
                    if not isinstance(b, int) or b + 1 < B:
                        statistics(b + 1, k + u, 1 - u)
                    normalise(b, u)
                    if not isinstance(b, int) or b > 1:
                        choose(b - 2, u)

                over(dve, B, step, tail=2)
                choose(B - 2, 0)
                choose(B - 1, 1)

            @block.tensor
            def _(pe):
                pe.wait_ge(sh.router_in, 16)

                def transposes(b, u):
                    pe.wait_ge(did_xn, b + 1)
                    at_least(pe, did_xt, b - 1)
                    for c in range(CC):
                        for t in range(TB):
                            m = nc.tensor.transpose(pt[u][:, c, t * P:(t + 1) * P],
                                                    xn[u][:, t, c * P:(c + 1) * P], sh.ident[:])
                    m.then_inc(did_pt, 1)

                transposes(0, 0)

                def step(b, k, u):
                    if not isinstance(b, int) or b + 1 < B:
                        transposes(b + 1, 1 - u)
                    pe.wait_ge(did_xt, b + 1)
                    at_least(pe, did_eq, b - 1)
                    for t in range(TB):
                        for c in range(CC):
                            m = nc.tensor.matmul(pl[u][:, t * E:(t + 1) * E], xt[u][:, c, t * P:(t + 1) * P],
                                                 sh.w_router[:, c, :], start=(c == 0), stop=(c == CC - 1))
                    m.then_inc(did_logit, 1)

                over(pe, B, step, tail=2)

            @block.scalar
            def _(act):

                def step(b, k, u):
                    act.wait_ge(did_pt, b + 1)
                    at_least(act, did_logit, b - 1)
                    for c in range(CC):
                        s = nc.scalar.activation(xt[u][:, c, :], pt[u][:, c, :], ACT.Copy)
                    s.then_inc(did_xt, 1)

                over(act, B, step)


def place_tokens(sh, onehot, index, expert, loads=None):
    nc = sh.nc
    with ExitStack() as own:
        a = lambda name, shape, dt=F32: sh.sb(name, shape, dt, ctx=own)
        upto = a("upto", [P, E, NT])
        more = a("more", [P, E, NT])
        tiles = a("tiles", [P, E])
        ends = a("ends", [P, E])
        first = a("first", [P, E])
        slots = a("slots", [P, NT, E])
        slots2 = a("slots2", [P, NT, E])
        slot = a("slot", [P, NT])
        beyond = a("beyond", [P, NT, NS])
        tile_of = a("tile_of", [P, NT])
        row_of = a("row_of", [P, NT])
        is_row = a("is_row", [P, NT, P])
        is_tile = a("is_tile", [P, NT, NS])
        kind = a("kind", [P, 3, NS])
        pp = sh.ps("ps_prefix", [P, 2, NT, E], ctx=own)
        pi = sh.ps("ps_index", [P, NS], ctx=own)
        did_sums = sh.sem("did_sums")
        did_inverse = sh.sem("did_inverse")
        did = sh.sem("placing")
        with nc.Block() as block:

            if loads:
                @block.sync
                def _(sp):
                    loads(sp)

            @block.tensor
            def _(pe):
                flat = onehot[:].rearrange("p t e -> p (t e)")
                nc.tensor.matmul(pp[:, 0, :, :].rearrange("p t e -> p (t e)"), sh.before[:], flat,
                                 start=True, stop=True)
                nc.tensor.matmul(pp[:, 1, :, :].rearrange("p t e -> p (t e)"), sh.ones[:], flat,
                                 start=True, stop=True).then_inc(did_sums, 1)
                pe.wait_ge(did, STEPS_TO_ROWS)
                for t in range(NT):
                    m = nc.tensor.matmul(pi[:], is_row[:, t, :], is_tile[:, t, :], start=(t == 0), stop=(t == NT - 1))
                m.then_inc(did_inverse, 1)

            @block.vector
            def _(dve):
                v = nc.vector
                n = [0]

                def step(ins):
                    n[0] += 1
                    ins.then_inc(did, 1)
                    dve.wait_ge(did, n[0])

                dve.wait_ge(did_sums, 1)
                for e in range(E):
                    s = v.tensor_tensor_scan(upto[:, e, :], sh.ones[:, 0:NT], pp[:, 1, :, e], 0.0, ALU.mult, ALU.add)
                step(s)
                step(v.tensor_tensor(more[:], upto[:, :, NT - 1:NT].to_broadcast([P, E, NT]),
                                     sh.steps[:, 0:NT].unsqueeze(1).to_broadcast([P, E, NT]), ALU.is_gt))
                step(v.tensor_reduce(tiles[:].unsqueeze(2), more[:], AX.X, ALU.add))
                step(v.tensor_tensor_scan(ends[:], sh.ones[:, 0:E], tiles[:], 0.0, ALU.mult, ALU.add))
                step(v.tensor_tensor(first[:], ends[:], tiles[:], ALU.subtract))
                step(v.tensor_tensor(slots[:], upto[:].rearrange("p e t -> p t e"), pp[:, 1, :, :], ALU.subtract))
                step(v.tensor_tensor(slots[:], slots[:], pp[:, 0, :, :], ALU.add))
                for e in range(E):
                    s = v.scalar_tensor_tensor(slots2[:, :, e], first[:, e:e + 1].to_broadcast([P, NT]), float(P),
                                               slots[:, :, e], ALU.mult, ALU.add)
                step(s)
                step(v.tensor_tensor(slots2[:], slots2[:], onehot[:], ALU.mult))
                step(v.tensor_reduce(slot[:].unsqueeze(2), slots2[:], AX.X, ALU.add))
                step(v.tensor_tensor(beyond[:], slot[:].unsqueeze(2).to_broadcast([P, NT, NS]),
                                     sh.steps[:, 1:NS + 1].unsqueeze(1).to_broadcast([P, NT, NS]), ALU.is_ge))
                step(v.tensor_reduce(tile_of[:].unsqueeze(2), beyond[:], AX.X, ALU.add))
                step(v.scalar_tensor_tensor(row_of[:], tile_of[:], -float(P), slot[:], ALU.mult, ALU.add))
                step(v.tensor_tensor(is_tile[:], tile_of[:].unsqueeze(2).to_broadcast([P, NT, NS]),
                                     sh.count[:, 0:NS].unsqueeze(1).to_broadcast([P, NT, NS]), ALU.is_equal))
                step(v.tensor_tensor(is_tile[:], is_tile[:], sh.token[:].unsqueeze(2).to_broadcast([P, NT, NS]),
                                     ALU.mult))
                step(v.tensor_tensor(is_row[:], row_of[:].unsqueeze(2).to_broadcast([P, NT, P]),
                                     sh.count[:].unsqueeze(1).to_broadcast([P, NT, P]), ALU.is_equal))
                assert n[0] == STEPS_TO_ROWS
                for e in range(1, E):
                    s = v.tensor_scalar(kind[:, e - 1, :], sh.count[:, 0:NS], first[:, e:e + 1], None, ALU.is_ge)
                step(s)
                step(v.tensor_tensor(kind[:, 0, :], kind[:, 0, :], kind[:, 1, :], ALU.add))
                step(v.tensor_tensor(expert[:], kind[0:1, 0, :], kind[0:1, 2, :], ALU.add))
                dve.wait_ge(did_inverse, 1)
                step(v.tensor_scalar(index[:], pi[:], float(NONE), None, ALU.add))


STEPS_TO_ROWS = 16


def ffn(sh, src, dst, index, expert):
    nc = sh.nc
    with ExitStack() as own:
        a = lambda name, shape, dt=F32: sh.sb(name, shape, dt, ctx=own)
        two = lambda name, shape, dt=F32: [a(name, shape, dt) for _ in range(2)]
        gi = two("gather_index", [P, 1], U32)
        si = two("scatter_index", [P, 1], U32)
        x = two("x_slot", [P, C])
        xn = two("xn_slot", [P, C])
        xn_bo = a("xn_plus_bo", [P, NS, C])
        x_beta = a("x_plus_beta", [P, NS, C])
        xt = two("xn_slot_t", [P, CC, P])
        hb = two("hidden_biased", [P, I])
        hg = two("hidden", [P, I])
        ht = two("hidden_t", [P, IC, P])
        z = a("z", [P, C])
        zn = a("zn", [P, C])
        zg = a("zg", [P, C])
        out = two("out_rows", [P, C])
        st = [a("stats", [P, 6]) for _ in range(2)]
        mv = [a("mean_var", [P, 2]) for _ in range(2)]
        ve = [a("var_eps", [P, 1]) for _ in range(2)]
        rs = [a("rstd", [P, 1]) for _ in range(2)]
        p_xt = sh.ps("ps_xt", [P, HB], ctx=own)
        p_h = sh.ps("ps_h", [P, NH, HB], ctx=own)
        p_ht = sh.ps("ps_ht", [P, 2, HB], ctx=own)
        p_y = sh.ps("ps_y", [P, HB], ctx=own)

        halved = sh.sem("halved")
        cleared = sh.sem("cleared")
        got_x = [sh.sem("got_x") for _ in range(2)]
        stored = [sh.sem("stored") for _ in range(2)]
        names = ("x_aggr x_var x_rstd xn_made x_beta_made xn_bo_made xt_ps xt_made h_ps h_biased h_made "
                 "ht_ps ht_made y_ps z_made z_aggr z_var z_rstd zn_made zg_made out_made")
        s = {k: sh.sem(k) for k in names.split()}

        with nc.Block() as block:

            @block.gpsimd
            def _(pool):
                g = nc.gpsimd
                last_token = pool.to_reg(NTOK - 1)

                def gather(j, u):
                    g.tensor_copy(gi[u][:], index[:, ds(j)])
                    pool.drain()
                    g.indirect_dma_start(out=x[u][:], out_offset=None, in_=src,
                                         in_offset=bass.IndirectOffsetOnAxis(ap=gi[u][:, 0:1], axis=0),
                                         bounds_check=last_token, oob_is_err=False).then_inc(got_x[u], 16)

                def pre(j, u):
                    pool.wait_ge(s["x_var"], j + 1)
                    g.tensor_tensor(rs[0][:], ve[0][:], sh.lane[:, 0:1], ALU.pow).then_inc(s["x_rstd"], 1)
                    g.tensor_tensor(x_beta[:, ds(j), :], x[u][:].unsqueeze(1), sh.beta[:].unsqueeze(1), ALU.add
                                    ).then_inc(s["x_beta_made"], 1)
                    pool.wait_ge(s["xn_made"], j + 1)
                    g.tensor_tensor(xn_bo[:, ds(j), :], xn[u][:].unsqueeze(1), sh.bo[:].unsqueeze(1), ALU.add
                                    ).then_inc(s["xn_bo_made"], 1)

                g.memset(x[0][:], 0.0)
                g.memset(x[1][:], 0.0).then_inc(cleared, 1)
                pool.wait_ge(cleared, 1)
                gather(0, 0)
                gather(1, 1)
                pool.wait_ge(sh.ffn_in, FFN_LOADED)
                pool.wait_ge(halved, 1)
                for j in range(2):
                    pre(j, j)
                    pool.wait_ge(s["x_beta_made"], j + 1)
                    gather(j + 2, j)

                def step(j, k, u):
                    if not isinstance(j, int) or j + 2 < NS:
                        pre(j + 2, u)
                    if not isinstance(j, int) or j + 4 < NS:
                        pool.wait_ge(s["x_beta_made"], j + 3)
                        gather(j + 4, u)
                    pool.wait_ge(s["z_var"], j + 1)
                    g.tensor_tensor(rs[1][:], ve[1][:], sh.lane[:, 0:1], ALU.pow).then_inc(s["z_rstd"], 1)
                    at_least(pool, stored[u], 16 * k)
                    pool.wait_ge(s["out_made"], j + 1)
                    g.tensor_copy(si[u][:], index[:, ds(j)])
                    pool.drain()
                    g.indirect_dma_start(out=dst, out_offset=bass.IndirectOffsetOnAxis(ap=si[u][:, 0:1], axis=0),
                                         in_=out[u][:], in_offset=None,
                                         bounds_check=last_token, oob_is_err=False).then_inc(stored[u], 16)

                over(pool, NS, step, tail=4)
                pool.wait_ge(stored[0], 16 * ((NS + 1) // 2))
                pool.wait_ge(stored[1], 16 * (NS // 2))

            @block.vector
            def _(dve):
                v = nc.vector
                reg = None

                def x_stats(j, k, u):
                    dve.wait_ge(got_x[u], 16 * k + 16)
                    at_least(dve, s["xn_made"], j)
                    v.bn_stats(st[0][:], x[u][:])
                    dve.drain()
                    v.bn_aggr(mv[0][:], st[0][:]).then_inc(s["x_aggr"], 1)
                    dve.wait_ge(s["x_aggr"], j + 1)
                    v.tensor_scalar(ve[0][:], mv[0][:, 1:2], LN_EPS, None, ALU.add).then_inc(s["x_var"], 1)

                def x_norm(j, u):
                    dve.wait_ge(s["x_rstd"], j + 1)
                    at_least(dve, s["xn_bo_made"], j - 1)
                    at_least(dve, s["xt_ps"], j - 1)
                    v.tensor_scalar(xn[u][:], x[u][:], mv[0][:, 0:1], rs[0][:], ALU.subtract, ALU.mult
                                    ).then_inc(s["xn_made"], 1)

                def bias(j, u):
                    e = dve.value_load(expert[0:1, ds(j)], min_val=0, max_val=E - 1)
                    for n in range(NH):
                        dve.wait_ge(s["h_ps"], NH * j + n + 1)
                        at_least(dve, s["h_made"], NH * (j - 2) + n + 1)
                        v.tensor_tensor(hb[u][:, n * HB:(n + 1) * HB].unsqueeze(1), p_h[:, n, :].unsqueeze(1),
                                        sh.b1[:, ds(e), n * HB:(n + 1) * HB], ALU.add).then_inc(s["h_biased"], 1)

                dve.wait_ge(sh.ffn_in, FFN_LOADED)
                v.tensor_scalar(sh.gamma[:], sh.gamma[:], 0.5, None, ALU.mult)
                v.tensor_scalar(sh.beta[:], sh.beta[:], 0.5, None, ALU.mult).then_inc(halved, 1)
                dve.wait_ge(halved, 1)
                for j in range(2):
                    x_stats(j, 0, j)
                    x_norm(j, j)
                bias(0, 0)

                def step(j, k, u):
                    known = isinstance(j, int)
                    if not known or j + 2 < NS:
                        x_stats(j + 2, k + 1, u)
                    if not known or j + 1 < NS:
                        bias(j + 1, 1 - u)
                    if not known or j + 2 < NS:
                        x_norm(j + 2, u)
                    dve.wait_ge(s["y_ps"], j + 1)
                    dve.wait_ge(s["xn_bo_made"], j + 1)
                    v.tensor_tensor(z[:].unsqueeze(1), p_y[:, 0:C].unsqueeze(1), xn_bo[:, ds(j), :], ALU.add
                                    ).then_inc(s["z_made"], 1)
                    dve.wait_ge(s["z_made"], j + 1)
                    v.bn_stats(st[1][:], z[:])
                    dve.drain()
                    v.bn_aggr(mv[1][:], st[1][:]).then_inc(s["z_aggr"], 1)
                    dve.wait_ge(s["z_aggr"], j + 1)
                    v.tensor_scalar(ve[1][:], mv[1][:, 1:2], FFN_EPS, None, ALU.add).then_inc(s["z_var"], 1)
                    dve.wait_ge(s["z_rstd"], j + 1)
                    v.tensor_scalar(zn[:], z[:], mv[1][:, 0:1], rs[1][:], ALU.subtract, ALU.mult
                                    ).then_inc(s["zn_made"], 1)
                    dve.wait_ge(s["zn_made"], j + 1)
                    v.tensor_tensor(zg[:], zn[:], sh.gamma[:], ALU.mult).then_inc(s["zg_made"], 1)
                    dve.wait_ge(s["zg_made"], j + 1)
                    at_least(dve, stored[u], 16 * k)
                    v.tensor_tensor(out[u][:].unsqueeze(1), zg[:].unsqueeze(1), x_beta[:, ds(j), :], ALU.add
                                    ).then_inc(s["out_made"], 1)

                over(dve, NS, step, tail=4)

            @block.tensor
            def _(pe):
                mm = nc.tensor

                def xt_transposes(j, u):
                    pe.wait_ge(s["xn_made"], j + 1)
                    at_least(pe, s["xt_made"], j)
                    for c in range(CC):
                        m = mm.transpose(p_xt[:, c * P:(c + 1) * P], xn[u][:, c * P:(c + 1) * P], sh.ident[:])
                    m.then_inc(s["xt_ps"], 1)

                def hidden(j, u):
                    e = pe.value_load(expert[0:1, ds(j)], min_val=0, max_val=E - 1)
                    pe.wait_ge(s["xt_made"], j + 1)
                    for n in range(NH):
                        at_least(pe, s["h_biased"], NH * (j - 1) + n + 1)
                        for c in range(CC):
                            m = mm.matmul(p_h[:, n, :], xt[u][:, c, :],
                                          sh.w1[:, ds(e), c, n * HB:(n + 1) * HB].rearrange("p a i -> p (a i)"),
                                          start=(c == 0), stop=(c == CC - 1))
                        m.then_inc(s["h_ps"], 1)

                def hidden_transposes(j, u):
                    for n in range(2):
                        pe.wait_ge(s["h_made"], NH * j + n + 1)
                        at_least(pe, s["ht_made"], 2 * (j - 1) + n + 1)
                        for q in range(IC // 2):
                            k = n * IC // 2 + q
                            m = mm.transpose(p_ht[:, n, q * P:(q + 1) * P], hg[u][:, k * P:(k + 1) * P], sh.ident[:])
                        m.then_inc(s["ht_ps"], 1)

                def second(j, u):
                    at_least(pe, s["z_made"], j)
                    for k in range(IC):
                        if k % (IC // 2) == 0:
                            pe.wait_ge(s["ht_made"], 2 * j + k // (IC // 2) + 1)
                        m = mm.matmul(p_y[:, 0:C], ht[u][:, k, :], sh.wo[:, k, :], start=(k == 0), stop=(k == IC - 1))
                    m.then_inc(s["y_ps"], 1)

                pe.wait_ge(sh.ffn_in, FFN_LOADED)
                xt_transposes(0, 0)
                hidden(0, 0)

                def step(j, k, u):
                    more = not isinstance(j, int) or j + 1 < NS
                    if more:
                        xt_transposes(j + 1, 1 - u)
                    hidden_transposes(j, u)
                    if more:
                        hidden(j + 1, 1 - u)
                    second(j, u)

                over(pe, NS, step, tail=4)

            @block.scalar
            def _(act):
                def xt_copy(j, u):
                    act.wait_ge(s["xt_ps"], j + 1)
                    at_least(act, s["h_ps"], NH * (j - 1))
                    nc.scalar.activation(xt[u][:].rearrange("p c k -> p (c k)"), p_xt[:, 0:C], ACT.Copy
                                         ).then_inc(s["xt_made"], 1)

                def gelu(j, u):
                    for n in range(NH):
                        act.wait_ge(s["h_biased"], NH * j + n + 1)
                        at_least(act, s["ht_ps"], 2 * (j - 1))
                        nc.scalar.activation(hg[u][:, n * HB:(n + 1) * HB], hb[u][:, n * HB:(n + 1) * HB], ACT.Gelu
                                             ).then_inc(s["h_made"], 1)

                def ht_copy(j, u):
                    for n in range(2):
                        act.wait_ge(s["ht_ps"], 2 * j + n + 1)
                        at_least(act, s["y_ps"], j - 1)
                        h = IC // 2
                        nc.scalar.activation(ht[u][:, n * h:(n + 1) * h, :].rearrange("p k t -> p (k t)"),
                                             p_ht[:, n, :], ACT.Copy).then_inc(s["ht_made"], 1)

                xt_copy(0, 0)
                gelu(0, 0)

                def step(j, k, u):
                    more = not isinstance(j, int) or j + 1 < NS
                    if more:
                        xt_copy(j + 1, 1 - u)
                    ht_copy(j, u)
                    if more:
                        gelu(j + 1, 1 - u)

                over(act, NS, step, tail=4)


MIXES = 5
W_, K_, V_, R_, G_ = range(MIXES)
LORA, DLORA = 32, 64
H, N = 4, 64
HP = C // P
QC = T // P
GN_EPS = 1e-5 * 8 ** 2
HALVES = [1, 2, 4, 8, 16]
LEVELS = ["u"] + HALVES
LAST = 7

MIXING = [(s, c) for c in range(CC) for s in (W_, K_, R_, V_)] + [(G_, 0), (G_, 1)]
FILLS = [("b", f"au{q}") for q in range(QC)] + [("b", f"a1{q}") for q in range(QC)]
FILLS += [("a", f"xt{c}") for c in range(CC)]
FILLS += [("b", f"a2{q}") for q in range(QC)] + [("c", f"yt{c}") for c in range(CC)]
FILLS += [("a", "mixa"), ("a", "mixb"), ("b", "g0"), ("b", "g1"), ("c", "o0"), ("c", "o1")]
FILLS += [("b", f"a4{q}") for q in range(QC)]
FILLS += [("a", f"m{s}{c}") for s, c in MIXING[:8]]
FILLS += [("b", f"a8{q}") for q in range(QC)]
FILLS += [("c", f"zt{c}") for c in range(CC)] + [("a", "m40"), ("a", "m41"), ("a", "d1")]
FILLS += [("b", f"a16{q}") for q in range(QC)] + [("c", "lg")]
FILLS += [("a", "k0"), ("a", "k1"), ("a", "r0"), ("a", "r1")]
FILLS += [("b", "b"), ("b", "c0"), ("b", "c1"), ("a", "d20"), ("a", "d21"), ("b", "kt0"), ("b", "kt1")]
FILLS += [("a", "v0"), ("a", "v1"), ("b", "kv0"), ("b", "kv1")] + [("b", f"y{q}") for q in range(QC)]
HEAD, TAIL = 2, 3


class Banks:

    SHIFT = {"a": -1, "b": 0, "c": 1}

    def __init__(self, sh, own):
        self.ps = [sh.ps("bank", [P, HB], ctx=own) for _ in range(8)]
        self.full = [sh.sem(f"bank_full{j}") for j in range(8)]
        self.free = [sh.sem(f"bank_free{j}") for j in range(8)]
        self.bank = {name: (k % 8, kind) for k, (kind, name) in enumerate(FILLS)}
        self.before = {}
        self.per = [len(FILLS[j::8]) for j in range(8)]
        n = [0] * 8
        for i in range(-1, B + 1):
            for kind, name in FILLS:
                seq = i - self.SHIFT[kind]
                if 0 <= seq < B:
                    j = self.bank[name][0]
                    self.before[name, i] = n[j]
                    n[j] += 1

    def count(self, name, seq):
        j, kind = self.bank[name]
        if isinstance(seq, int):
            return self.before[name, seq + self.SHIFT[kind]]
        i = seq + self.SHIFT[kind]
        return i * self.per[j] + (self.before[name, HEAD] - HEAD * self.per[j])

    def open(self, pe, name, seq):
        j = self.bank[name][0]
        at_least(pe, self.free[j], self.count(name, seq))
        return self.ps[j]

    def filled(self, eng, name, seq):
        j = self.bank[name][0]
        if not (isinstance(seq, int) and seq < 0):
            eng.wait_ge(self.full[j], self.count(name, seq) + 1)
        return self.ps[j]

    def emptied(self, eng, name, seq):
        j = self.bank[name][0]
        if not (isinstance(seq, int) and seq < 0):
            eng.wait_ge(self.free[j], self.count(name, seq) + 1)

    def f(self, name):
        return self.full[self.bank[name][0]]

    def e(self, name):
        return self.free[self.bank[name][0]]


def load_attention(sh):
    sh.maa = sh.sb("maa", [P, MIXES + 1, CC])
    sh.mix1 = sh.sb("mix_w1", [P, CC, 2 * P])
    sh.mix2 = sh.sb("mix_w2", [P, MIXES, C])
    sh.dw1 = sh.sb("decay_w1", [P, CC, P])
    sh.dw2 = sh.sb("decay_w2", [P, C])
    sh.vecs = sh.sb("vectors", [P, 4, CC])
    sh.wm = {k: sh.sb(k, [P, CC, C]) for k in ("Wr", "Wk", "Wv", "Wg", "Wo")}
    sh.att_in = sh.sem("attention_in")


def start_attention_loads(q, sh, d):
    flat = lambda a: a.rearrange("(c p) -> p c", p=P)
    loads = [(sh.maa[:, n, :], flat(d["time_maa_" + k])) for n, k in enumerate("wkvrgx")]
    loads += [(sh.vecs[:, 0, :], flat(d["time_decay"])),
              (sh.vecs[:, 1, :], d["time_faaaa"].rearrange("(c h) n -> (h n) c", c=CC)),
              (sh.vecs[:, 2, :], flat(d["ln_w"])), (sh.vecs[:, 3, :], flat(d["ln_b"])),
              (sh.mix1[:, :, 0:MIXES * LORA], d["time_maa_w1"].rearrange("(c p) n -> p c n", p=P)),
              (sh.dw1[:, :, 0:DLORA], d["time_decay_w1"].rearrange("(c p) n -> p c n", p=P)),
              (sh.dw2[0:DLORA, :], d["time_decay_w2"])]
    loads += [(sh.mix2[i % 4 * LORA:(i % 4 + 1) * LORA, i, :], d["time_maa_w2"][i]) for i in range(MIXES)]
    loads += [(sh.wm[k][:], d[k].rearrange("(c p) n -> p c n", p=P)) for k in ("Wr", "Wk", "Wv", "Wg", "Wo")]
    for to, of in loads:
        q.dma_start(to, of).then_inc(sh.att_in, 16)
    assert len(loads) == ATT_LOADS


ATT_LOADS = 23


def attention(sh, src, dst, onehot):
    nc = sh.nc
    src_v = src.rearrange("(b t p) c -> b p t c", p=P, t=TB)
    dst_v = dst.rearrange("(b t p) c -> b p t c", p=P, t=TB)
    row = lambda ap: ap.rearrange("a p t c -> (a p) t c")

    with ExitStack() as own:
        a_ = lambda name, shape, dt=F32: sh.sb(name, shape, dt, ctx=own)
        x = a_("x_in", [P, TB, C])
        xr = a_("x_out", [P, TB, C])
        mv = [a_("mean_var", [P, TB, 2]) for _ in range(2)]
        st = [a_("stats", [P, TB, 6]) for _ in range(2)]
        ve = [a_("var_eps", [P, TB]) for _ in range(2)]
        rs = [a_("rstd", [P, TB]) for _ in range(2)]
        xn = a_("xn", [P, TB, C])
        xt = a_("xn_t", [P, CC, T + 1])
        xx = a_("shift_less_x", [P, CC, T])
        xxx = a_("xxx", [P, CC, T])
        mixa = a_("mix_a", [P, T])
        mixb = a_("mix_b", [P, T])
        xs = [a_("x_mixed", [P, CC, T]) for _ in range(MIXES)]
        d1 = a_("decay_hidden", [P, T])
        tot = [a_("block_decay", [P, HP, T >> m]) for m in range(LAST + 1)]
        ks = [a_("K", [P, HP, T]) for _ in range(3)]
        rx = [a_("R", [P, 2, HP, T]) for _ in range(3)]
        ku = a_("K_u", [P, HP, T])
        vv = a_("v", [P, QC, C])
        gt = a_("g_tanh", [P, CC, T])
        gh = a_("g_half", [P, CC, T])
        wt = a_("weights", [P, QC, HP, 2, P])
        kt = a_("K_rows", [P, QC - 1, HP, P])
        ss = a_("state", [P, QC, HP, N])
        y = a_("y", [P, QC, C])
        gst = a_("y_stats", [P, QC * H, 6])
        gm = a_("y_mean", [P, QC * H])
        gd = a_("y_dif", [P, QC * H])
        gv = a_("y_var", [P, QC * H])
        gr = a_("y_rstd", [P, QC * H])
        yn = a_("yn", [P, QC, C])
        yt = a_("yn_t", [P, CC, T])
        zn = a_("zn", [P, TB, C])
        zt = a_("zn_t", [P, CC, T])
        top = a_("top", [P, TB, 1])
        sc = a_("score", [P, TB, E])
        rank = a_("rank", [P, TB, E])
        mf = {m: a_(f"mask_float{m}", [P, P]) for m in HALVES}
        masks = {m: a_(f"mask{m}", [P, P], U8) for m in HALVES}
        touched = a_("touched", [P, 32])

        bk = Banks(sh, own)
        names = ("x_var x_rstd xn_made xx_made xxx_made xs_made decay_made gate_made multiplied multiplied1 copied "
                 "tot_made s_made y_var y_rstd y_centred yn_made gated z_var z_rstd zn_made top_made eq_made sc_made best_made "
                 "hot_made")
        s = {k: sh.sem(k) for k in names.split()}
        x_got = sh.sem("x_got")
        res_got = sh.sem("residual_got")
        stored = sh.sem("x_stored")
        masks_made = sh.sem("masks_made")
        zeros_made = sh.sem("zeros_made")
        r_zeros_made = sh.sem("r_zeros_made")
        mask_step = sh.sem("mask_step")

        def upto(eng, name, count):
            at_least(eng, s[name], count)

        def buf(n):
            return 0 if n == 0 else 2 - n % 2

        def level_ready(eng, n, b):
            if n == 0:
                bk.emptied(eng, "r1", b)
            else:
                for name in ("multiplied", "multiplied1", "copied"):
                    eng.wait_ge(s[name], LAST * b + n)

        def level_read(eng, n, b):
            names = {1: "a23", 2: "a43", 3: "a83", 4: "a163", 5: "b", 6: "c1", 7: "y3"}
            bk.filled(eng, names[n], b)

        def blocks(t, m):
            return t.rearrange("p h (n two m) -> p (h n) two m", two=2, m=m)

        def state_before(eng, q, b):
            if q == 1:
                eng.wait_ge(s["s_made"], b + 1)
            else:
                bk.emptied(eng, f"kv{q - 2}", b)

        def has_next(i):
            return not isinstance(i, int) or i + 2 < B

        def rounds(eng, step):
            step(-1, True, False, False)
            step(0, True, True, False)
            step(1, True, True, True)
            with eng.Fori(HEAD, B + 1 - TAIL) as i:
                step(i, True, True, True)
            for i in range(B + 1 - TAIL, B + 1):
                step(i, i + 1 < B, i < B, True)

        with nc.Block() as block:

            @block.sync
            def _(sp):
                sp.dma_start(x[:], src_v[0]).then_inc(x_got, 16)

                def step(i, a, b, c):
                    if a and (not isinstance(i, int) or i + 2 < B):
                        upto(sp, "xn_made", i + 2)
                        sp.dma_start(x[:], row(src_v[ds(i + 2)])).then_inc(x_got, 16)
                    if c:
                        bk.emptied(sp, "o1", i - 1)
                        sp.dma_start(row(dst_v[ds(i - 1)]), xr[:]).then_inc(stored, 16)
                    if b:
                        at_least(sp, stored, 16 * i)
                        upto(sp, "zn_made", i)
                        sp.dma_start(xr[:], row(src_v[ds(i)])).then_inc(res_got, 16)

                step(-1, True, False, False)
                step(0, True, True, False)
                step(1, True, True, True)
                with sp.Fori(HEAD, B - 2) as i:
                    step(i, True, True, True)
                step(B - 2, True, True, True)
                step(B - 1, False, True, True)
                step(B, False, False, True)
                sp.wait_ge(stored, 16 * B)

            @block.gpsimd
            def _(pool):
                g = nc.gpsimd
                g.iota(rank[:], pattern=[[0, TB], [-1, E]], base=E, channel_multiplier=0,
                       allow_small_or_imprecise_dtypes=True)
                g.memset(xt[:, :, 0:1], 0.0)
                g.memset(ss[:], 0.0).then_inc(zeros_made, 1)

                def make_masks():
                    for m in HALVES:
                        i = g.memset(mf[m][:], 1.0)
                    i.then_inc(mask_step, 1)
                    for n, (op, rows) in enumerate(((ALU.is_gt, 0), (ALU.is_ge, 1), (ALU.is_gt, -1))):
                        pool.wait_ge(mask_step, n + 1)
                        for m in HALVES:
                            blocks_of_2m = mf[m][:].rearrange("p (b h m) -> p b h m", h=2, m=m)
                            pattern = [[-2 * m * rows, P // (2 * m)], [0 if rows else 1, 2], [0, m]]
                            i = g.affine_select(out=blocks_of_2m, in_=blocks_of_2m, compare_op=op, fill=0.0,
                                                base=m if rows < 0 else 0, pattern=pattern, channel_multiplier=rows)
                        i.then_inc(mask_step, 1)
                    pool.wait_ge(mask_step, 4)
                    for m in HALVES:
                        i = g.tensor_copy(masks[m][:], mf[m][:])
                    i.then_inc(masks_made, 1)

                def add_x(seq, pairs):
                    for i, c in pairs:
                        bk.emptied(pool, f"m{i}{c}", seq)
                        g.tensor_tensor(xs[i][:, c, :], xs[i][:, c, :], xt[:, c, 1:T + 1], ALU.add
                                        ).then_inc(s["xs_made"], 1)

                def double(b, n):
                    pool.drain()
                    level_ready(pool, n, b)
                    if n == 0:
                        pool.wait_ge(s["decay_made"], b + 1)
                        if not (isinstance(b, int) and b == 0):
                            level_read(pool, 7, b - 1)
                    elif n == 1:
                        if not (isinstance(b, int) and b == 0):
                            level_read(pool, 6, b - 1)
                        pool.wait_ge(s["tot_made"], LAST * b + n)
                    else:
                        level_read(pool, n - 1, b)
                        pool.wait_ge(s["tot_made"], LAST * b + n)
                    m = 1 << n
                    t2 = tot[n][N:P].rearrange("p h (n two) -> p (h n) two", two=2)
                    g.tensor_tensor(blocks(rx[buf(n + 1)][N:P, 1], m)[:, :, 1, :],
                                    blocks(rx[buf(n)][N:P, 1], m)[:, :, 1, :],
                                    t2[:, :, 0:1].to_broadcast([N, HP * T // (2 * m), m]), ALU.mult
                                    ).then_inc(s["multiplied1"], 1)
                    pool.drain()

                def x_rstd(seq):
                    upto(pool, "x_var", seq + 1)
                    upto(pool, "xn_made", seq)
                    g.tensor_tensor(rs[0][:], ve[0][:], sh.lane[:, 0:TB], ALU.pow).then_inc(s["x_rstd"], 1)

                def group_normalise(seq):
                    heads = lambda z: z[:].rearrange("p q (h n) -> p (q h) n", n=N)
                    each = lambda z: z[:].unsqueeze(2).to_broadcast([P, QC * H, N])
                    upto(pool, "y_var", seq + 1)
                    g.tensor_tensor(gr[:], gv[:], sh.lane[:, 0:QC * H], ALU.pow).then_inc(s["y_rstd"], 1)
                    bk.filled(pool, "yt1", seq - 1)
                    g.tensor_tensor(heads(yn), heads(y), each(gm), ALU.subtract).then_inc(s["y_centred"], 1)
                    upto(pool, "y_rstd", seq + 1)
                    upto(pool, "y_centred", seq + 1)
                    g.tensor_tensor(heads(yn), heads(yn), each(gr), ALU.mult).then_inc(s["yn_made"], 1)

                def step(i, a, b, c):
                    if b:
                        double(i, 1)
                    if c:
                        upto(pool, "z_var", i)
                        upto(pool, "zn_made", i - 1)
                        g.tensor_tensor(rs[1][:], ve[1][:], sh.lane[:, 0:TB], ALU.pow).then_inc(s["z_rstd"], 1)
                    if b:
                        double(i, 2)
                        double(i, 3)
                    if a:
                        add_x(i + 1, MIXING[:8])
                    if b:
                        double(i, 4)
                    if a:
                        add_x(i + 1, MIXING[8:])
                    if b:
                        double(i, 5)
                        double(i, 6)
                    if has_next(i):
                        x_rstd(i + 2)
                    if a:
                        double(i + 1, 0)
                    if a and not b:
                        make_masks()
                    if b:
                        group_normalise(i)

                x_rstd(0)
                rounds(pool, step)

            @block.vector
            def _(dve):
                v = nc.vector
                for r in rx:
                    v.memset(r[N:P, 0, :, :], 0.0)
                    i = v.memset(r[0:N, 1, :, :], 0.0)
                i.then_inc(r_zeros_made, 1)
                dve.wait_ge(zeros_made, 1)
                dve.wait_ge(sh.att_in, 16 * ATT_LOADS)
                touches = [0]

                def normalise(k, xin, out_, var, rstd, made, seq):
                    for t in range(TB):
                        v.bn_stats(st[k][:, t, :], xin[:, t, :])
                    dve.drain()
                    for t in range(TB):
                        v.bn_aggr(mv[k][:, t, :], st[k][:, t, :])
                    dve.drain()
                    v.tensor_scalar(ve[k][:], mv[k][:, :, 1], LN_EPS, None, ALU.add).then_inc(s[var], 1)
                    dve.wait_ge(s[rstd], seq + 1)
                    bk.filled(dve, "zt1" if k else "xt1", seq - 1)
                    for t in range(TB):
                        i = v.tensor_scalar(out_[:, t, :], xin[:, t, :], mv[k][:, t, 0:1], rs[k][:, t:t + 1],
                                            ALU.subtract, ALU.mult)
                    i.then_inc(s[made], 1)

                def normalise_x(seq):
                    dve.wait_ge(x_got, 16 * seq + 16)
                    normalise(0, x, xn, "x_var", "x_rstd", "xn_made", seq)

                def double(b, n):
                    level_ready(dve, n, b)
                    if n == 0:
                        dve.wait_ge(s["decay_made"], b + 1)
                        if not (isinstance(b, int) and b == 0):
                            level_read(dve, 7, b - 1)
                    elif n == 1:
                        if not (isinstance(b, int) and b == 0):
                            level_read(dve, 6, b - 1)
                        dve.wait_ge(s["tot_made"], LAST * b + n)
                    else:
                        level_read(dve, n - 1, b)
                        dve.wait_ge(s["tot_made"], LAST * b + n)
                    m = 1 << n
                    t2 = tot[n][:].rearrange("p h (n two) -> p (h n) two", two=2)
                    nb = HP * T // (2 * m)
                    v.tensor_tensor(tot[n + 1][:].rearrange("p h n -> p (h n)"), t2[:, :, 0], t2[:, :, 1], ALU.mult
                                    ).then_inc(s["tot_made"], 1)
                    v.tensor_tensor(blocks(ks[buf(n + 1)][:], m)[:, :, 0, :], blocks(ks[buf(n)][:], m)[:, :, 0, :],
                                    t2[:, :, 1:2].to_broadcast([P, nb, m]), ALU.mult)
                    v.tensor_tensor(blocks(rx[buf(n + 1)][0:N, 0], m)[:, :, 1, :],
                                    blocks(rx[buf(n)][0:N, 0], m)[:, :, 1, :],
                                    t2[0:N, :, 0:1].to_broadcast([N, nb, m]), ALU.mult).then_inc(s["multiplied"], 1)

                def masked(b, n):
                    m = LEVELS[n]
                    for q in range(QC):
                        name = f"a{m}{q}"
                        ps = bk.filled(dve, name, b)[:].rearrange("p (n t) -> p n t", t=P)
                        w = wt[:, q].rearrange("p h l t -> p (h l) t")
                        shape = [P, 2 * HP, P]
                        if n == 0:
                            i = v.tensor_tensor(w, ps, sh.ident[:].unsqueeze(1).to_broadcast(shape), ALU.mult)
                        else:
                            bk.emptied(dve, f"a{LEVELS[n - 1]}{q}", b)
                            k = touches[0]
                            touches[0] += 1
                            v.tensor_copy(touched[:, k:k + 1], sh.ones[:, 0:1])
                            i = v.copy_predicated(w, masks[m][:].unsqueeze(1).to_broadcast(shape), ps)
                        i.then_inc(bk.e(name), 1)

                def mix(seq, pairs):
                    for i, c in pairs:
                        ps = bk.filled(dve, f"m{i}{c}", seq)
                        v.scalar_tensor_tensor(xs[i][:, c, :], ps[:], sh.maa[:, i, c:c + 1], xx[:, c, :],
                                               ALU.add, ALU.mult).then_inc(bk.e(f"m{i}{c}"), 1)

                def states(b):
                    for q in range(QC - 1):
                        ps = bk.filled(dve, f"kv{q // 2}", b)
                        if q == 0:
                            bk.filled(dve, "y3", b - 1)
                            dve.wait_ge(s["tot_made"], LAST * b + LAST)
                        else:
                            state_before(dve, q, b)
                        for hp in range(HP):
                            for hl in range(2):
                                r_ = slice(hl * N, hl * N + N)
                                col = (q % 2) * C + hp * P + hl * N
                                i = v.scalar_tensor_tensor(ss[r_, q + 1, hp, :], ss[r_, q, hp, :],
                                                           tot[LAST][r_, hp, q:q + 1], ps[r_, col:col + N],
                                                           ALU.mult, ALU.add)
                        i.then_inc(s["s_made"] if q == 0 else bk.e(f"kv{q - 1}"), 1)

                def group_statistics(b):
                    bk.emptied(dve, "y3", b)
                    upto(dve, "yn_made", b)
                    for q in range(QC):
                        for h in range(H):
                            v.bn_stats(gst[:, q * H + h, :], y[:, q, h * N:(h + 1) * N])
                    dve.drain()
                    v.tensor_tensor(gm[:], gst[:, :, 1], gst[:, :, 4], ALU.add)
                    v.tensor_tensor(gd[:], gst[:, :, 1], gst[:, :, 4], ALU.subtract)
                    v.tensor_tensor(gv[:], gst[:, :, 2], gst[:, :, 5], ALU.add)
                    dve.drain()
                    v.tensor_scalar(gm[:], gm[:], 0.5, None, ALU.mult)
                    v.tensor_tensor(gd[:], gd[:], gd[:], ALU.mult)
                    dve.drain()
                    v.scalar_tensor_tensor(gv[:], gd[:], N / 4.0, gv[:], ALU.mult, ALU.add)
                    dve.drain()
                    v.tensor_scalar(gv[:], gv[:], 1.0 / N, GN_EPS, ALU.mult, ALU.add).then_inc(s["y_var"], 1)

                def choose(seq):
                    lg = bk.filled(dve, "lg", seq)[:, 0:TB * E].rearrange("p (t e) -> p t e", e=E)
                    v.tensor_reduce(top[:], lg, AX.X, ALU.max).then_inc(s["top_made"], 1)
                    dve.wait_ge(s["top_made"], seq + 1)
                    v.tensor_tensor(sc[:], lg, top[:].to_broadcast([P, TB, E]), ALU.is_equal).then_inc(bk.e("lg"), 1)
                    bk.emptied(dve, "lg", seq)
                    v.tensor_tensor(sc[:], sc[:], rank[:], ALU.mult).then_inc(s["sc_made"], 1)
                    dve.wait_ge(s["sc_made"], seq + 1)
                    v.tensor_reduce(top[:], sc[:], AX.X, ALU.max).then_inc(s["best_made"], 1)
                    dve.wait_ge(s["best_made"], seq + 1)
                    v.tensor_tensor(onehot[:, ds(TB * seq, TB), :], sc[:], top[:].to_broadcast([P, TB, E]),
                                    ALU.is_equal).then_inc(s["hot_made"], 1)

                def step(i, a, b, c):
                    touches[0] = 0
                    if b:
                        masked(i, 0)
                        double(i, 1)
                        if isinstance(i, int) and i == 0:
                            dve.wait_ge(masks_made, 1)
                        masked(i, 1)
                    if a:
                        bk.emptied(dve, "xt1", i + 1)
                        v.tensor_tensor(xx[:], xt[:, :, 0:T], xt[:, :, 1:T + 1], ALU.subtract
                                        ).then_inc(s["xx_made"], 1)
                        dve.wait_ge(s["xx_made"], i + 2)
                        bk.filled(dve, "mixb", i)
                        for k in range(CC):
                            ins = v.scalar_tensor_tensor(xxx[:, k, :], xx[:, k, :], sh.maa[:, MIXES, k:k + 1],
                                                         xt[:, k, 1:T + 1], ALU.mult, ALU.add)
                        ins.then_inc(s["xxx_made"], 1)
                    if b:
                        double(i, 2)
                    if c:
                        dve.wait_ge(s["gate_made"], i)
                        bk.emptied(dve, "yt1", i - 1)
                        v.tensor_tensor(yt[:], yt[:], gt[:], ALU.mult).then_inc(s["gated"], 1)
                    if b:
                        masked(i, 2)
                    if c:
                        dve.wait_ge(res_got, 16 * i)
                        for n in range(2):
                            ps = bk.filled(dve, f"o{n}", i - 1)
                            half = xr[:, 2 * n:2 * n + 2, :].rearrange("p t c -> p (t c)")
                            v.tensor_tensor(half, ps[:], half, ALU.add).then_inc(bk.e(f"o{n}"), 1)
                        bk.emptied(dve, "o0", i - 1)
                        bk.emptied(dve, "o1", i - 1)
                        normalise(1, xr, zn, "z_var", "z_rstd", "zn_made", i - 1)
                    if b:
                        double(i, 3)
                        masked(i, 3)
                    if a:
                        bk.filled(dve, "v1", i)
                        bk.filled(dve, "g1", i)
                        mix(i + 1, MIXING[:8])
                    if b:
                        double(i, 4)
                        masked(i, 4)
                    if a:
                        mix(i + 1, MIXING[8:])
                    if b:
                        double(i, 5)
                        masked(i, 5)
                    if c:
                        choose(i - 1)
                    if b:
                        double(i, 6)
                        bk.emptied(dve, "g1", i)
                        v.scalar_tensor_tensor(gt[:], gt[:], 1.0, gh[:], ALU.add, ALU.mult).then_inc(s["gate_made"], 1)
                        states(i)
                    if has_next(i):
                        normalise_x(i + 2)
                    if a:
                        double(i + 1, 0)
                    if b:
                        group_statistics(i)

                normalise_x(0)
                rounds(dve, step)
                dve.wait_ge(s["hot_made"], B)

            @block.tensor
            def _(pe):
                mm = nc.tensor
                pe.wait_ge(sh.att_in, 16 * ATT_LOADS)

                def transposes(name, c, of, seq):
                    ps = bk.open(pe, f"{name}{c}", seq)
                    for t in range(TB):
                        i = mm.transpose(ps[:, t * P:(t + 1) * P], of[:, t, c * P:(c + 1) * P], sh.ident[:])
                    i.then_inc(bk.f(f"{name}{c}"), 1)

                def project(name, seq, w, xin, cols):
                    ps = bk.open(pe, name, seq)
                    for c in range(CC):
                        i = mm.matmul(ps[:], w[:, c, cols], xin[:, c, :], start=(c == 0), stop=(c == CC - 1))
                    i.then_inc(bk.f(name), 1)

                def project_rows(name, seq, xin, w):
                    for n in range(2):
                        ps = bk.open(pe, f"{name}{n}", seq)
                        for q in (0, 1):
                            t = 2 * n + q
                            for c in range(CC):
                                i = mm.matmul(ps[:, q * C:(q + 1) * C], xin[:, c, t * P:(t + 1) * P], w[:, c, :],
                                              start=(c == 0), stop=(c == CC - 1))
                        i.then_inc(bk.f(f"{name}{n}"), 1)

                def one(name, seq, w, xin):
                    ps = bk.open(pe, name, seq)
                    mm.matmul(ps[:], w, xin, start=True, stop=True).then_inc(bk.f(name), 1)

                def mixes(seq, pairs):
                    for i, c in pairs:
                        one(f"m{i}{c}", seq, sh.mix2[:, i, c * P:(c + 1) * P], (mixa if i < 4 else mixb)[:])

                def level(b, n):
                    m, l = LEVELS[n], max(n - 1, 0)
                    level_ready(pe, l, b)
                    k = ku if m == "u" else ks[buf(l)]
                    for q in range(QC):
                        ps = bk.open(pe, f"a{m}{q}", b)
                        t_ = slice(q * P, (q + 1) * P)
                        for hp in range(HP):
                            i = mm.matmul(ps[:, hp * C:(hp + 1) * C].rearrange("p (l t) -> p l t", t=P),
                                          k[:, hp, t_], rx[buf(l)][:, :, hp, t_], start=True, stop=True)
                        i.then_inc(bk.f(f"a{m}{q}"), 1)

                def wide_levels(b):
                    for l, m, r0s in ((5, 32, (0, 64)), (6, 64, (0,))):
                        level_ready(pe, l, b)
                        for q in range(QC):
                            name, at = ("b", q * 4 * m) if m == 32 else (f"c{q // 2}", q % 2 * 4 * m)
                            if at == 0:
                                ps = bk.open(pe, name, b)
                            for hp in range(HP):
                                for r0 in r0s:
                                    t0 = q * P + r0
                                    col = at + hp * 2 * m
                                    i = mm.matmul(ps[r0:r0 + m, col:col + 2 * m].rearrange("p (l t) -> p l t", t=m),
                                                  ks[buf(l)][:, hp, t0:t0 + m],
                                                  rx[buf(l)][:, :, hp, t0 + m:t0 + 2 * m], start=True, stop=True)
                            if at + 4 * m == HB:
                                i.then_inc(bk.f(name), 1)

                def k_rows(b):
                    level_ready(pe, LAST, b)
                    for n in range(2):
                        ps = bk.open(pe, f"kt{n}", b)
                        for q in range(2 * n, min(2 * n + 2, QC - 1)):
                            for hp in range(HP):
                                col = ((q % 2) * HP + hp) * P
                                i = mm.transpose(ps[:, col:col + P], ks[buf(LAST)][:, hp, q * P:(q + 1) * P],
                                                 sh.ident[:])
                        i.then_inc(bk.f(f"kt{n}"), 1)

                def kv(b):
                    bk.emptied(pe, "v1", b)
                    for n in range(2):
                        bk.emptied(pe, f"kt{n}", b)
                        ps = bk.open(pe, f"kv{n}", b)
                        for q in range(2 * n, min(2 * n + 2, QC - 1)):
                            for hp in range(HP):
                                col = (q % 2) * C + hp * P
                                i = mm.matmul(ps[:, col:col + P], kt[:, q, hp, :], vv[:, q, hp * P:(hp + 1) * P],
                                              start=True, stop=True)
                        i.then_inc(bk.f(f"kv{n}"), 1)

                def outputs(b):
                    bk.emptied(pe, "c1", b)
                    for q in range(QC):
                        ps = bk.open(pe, f"y{q}", b)
                        if q:
                            state_before(pe, q, b)
                        for hp in range(HP):
                            for hl in range(2):
                                col = hp * P + hl * N
                                i = mm.matmul(ps[:, col:col + N], wt[:, q, hp, hl, :], vv[:, q, col:col + N],
                                              start=True, stop=(q == 0))
                                if q:
                                    i = mm.matmul(ps[:, col:col + N], rx[buf(LAST)][:, hl, hp, q * P:(q + 1) * P],
                                                  ss[:, q, hp, :], start=False, stop=True)
                        i.then_inc(bk.f(f"y{q}"), 1)

                def step(i, a, b, c):
                    if b:
                        level(i, 0)
                        level(i, 1)
                    if a:
                        pe.wait_ge(s["xn_made"], i + 2)
                        for k in range(CC):
                            transposes("xt", k, xn, i + 1)
                    if b:
                        level(i, 2)
                    if c:
                        pe.wait_ge(s["yn_made"], i)
                        for k in range(CC):
                            transposes("yt", k, yn, i - 1)
                    if a:
                        pe.wait_ge(s["xxx_made"], i + 2)
                        project("mixa", i + 1, sh.mix1, xxx, slice(0, P))
                        project("mixb", i + 1, sh.mix1, xxx, slice(P, 2 * P))
                    if b:
                        for k in range(CC):
                            project(f"g{k}", i, sh.wm["Wg"], xs[G_], slice(k * P, (k + 1) * P))
                    if c:
                        pe.wait_ge(s["gated"], i)
                        project_rows("o", i - 1, yt, sh.wm["Wo"])
                    if b:
                        level(i, 3)
                    if a:
                        bk.emptied(pe, "mixb", i + 1)
                        mixes(i + 1, MIXING[:8])
                    if b:
                        level(i, 4)
                    if c:
                        pe.wait_ge(s["zn_made"], i)
                        for k in range(CC):
                            transposes("zt", k, zn, i - 1)
                    if a:
                        mixes(i + 1, MIXING[8:])
                        pe.wait_ge(s["xs_made"], 10 * i + 15)
                        project("d1", i + 1, sh.dw1, xs[W_], slice(0, P))
                    if b:
                        level(i, 5)
                    if c:
                        bk.emptied(pe, "zt1", i - 1)
                        ps = bk.open(pe, "lg", i - 1)
                        for t in range(TB):
                            for k in range(CC):
                                ins = mm.matmul(ps[:, t * E:(t + 1) * E], zt[:, k, t * P:(t + 1) * P],
                                                sh.w_router[:, k, :], start=(k == 0), stop=(k == CC - 1))
                        ins.then_inc(bk.f("lg"), 1)
                    if a:
                        pe.wait_ge(s["xs_made"], 10 * i + 17)
                        for name, w, xin in (("k", "Wk", K_), ("r", "Wr", R_)):
                            for k in range(CC):
                                project(f"{name}{k}", i + 1, sh.wm[w], xs[xin], slice(k * P, (k + 1) * P))
                    if b:
                        wide_levels(i)
                    if a:
                        bk.emptied(pe, "d1", i + 1)
                        for k in range(CC):
                            one(f"d2{k}", i + 1, sh.dw2[:, k * P:(k + 1) * P], d1[:])
                    if b:
                        k_rows(i)
                    if a:
                        pe.wait_ge(s["xs_made"], 10 * i + 20)
                        project_rows("v", i + 1, xs[V_], sh.wm["Wv"])
                    if b:
                        kv(i)
                        outputs(i)

                rounds(pe, step)

            @block.scalar
            def _(act):
                ac = nc.scalar.activation
                act.wait_ge(sh.att_in, 16 * ATT_LOADS)
                act.wait_ge(r_zeros_made, 1)

                def keep(b, n):
                    level_ready(act, n, b)
                    if n == 0:
                        if not (isinstance(b, int) and b == 0):
                            level_read(act, 7, b - 1)
                    elif n == 1:
                        if not (isinstance(b, int) and b == 0):
                            level_read(act, 6, b - 1)
                    else:
                        level_read(act, n - 1, b)
                    m = 1 << n
                    ac(blocks(ks[buf(n + 1)][:], m)[:, :, 1, :], blocks(ks[buf(n)][:], m)[:, :, 1, :], ACT.Copy)
                    for hl in range(2):
                        r_ = slice(hl * N, hl * N + N)
                        i = ac(blocks(rx[buf(n + 1)][r_, hl], m)[:, :, 0, :], blocks(rx[buf(n)][r_, hl], m)[:, :, 0, :],
                               ACT.Copy)
                    i.then_inc(s["copied"], 1)

                def step(i, a, b, c):
                    if b:
                        keep(i, 1)
                    if a:
                        upto(act, "xs_made", 10 * (i + 1))
                        for k in range(CC):
                            ps = bk.filled(act, f"xt{k}", i + 1)
                            ac(xt[:, k, 1:T + 1], ps[:], ACT.Copy).then_inc(bk.e(f"xt{k}"), 1)
                    if b:
                        keep(i, 2)
                    if c:
                        bk.filled(act, "o1", i - 2)
                        for k in range(CC):
                            ac(yt[:, k, :], bk.filled(act, f"yt{k}", i - 1)[:], ACT.Identity,
                               bias=sh.vecs[:, 3, k:k + 1], scale=sh.vecs[:, 2, k:k + 1]).then_inc(bk.e(f"yt{k}"), 1)
                    if a:
                        bk.filled(act, "m41", i)
                        for name, to in (("mixa", mixa), ("mixb", mixb)):
                            ac(to[:], bk.filled(act, name, i + 1)[:], ACT.Tanh).then_inc(bk.e(name), 1)
                    if b:
                        upto(act, "gated", i)
                        for k in range(CC):
                            ps = bk.filled(act, f"g{k}", i)
                            ac(gt[:, k, :], ps[:], ACT.Tanh, scale=0.5)
                            ac(gh[:, k, :], ps[:], ACT.Copy, scale=0.5).then_inc(bk.e(f"g{k}"), 1)
                    if b:
                        keep(i, 3)
                    if c:
                        bk.filled(act, "lg", i - 2)
                        for k in range(CC):
                            ac(zt[:, k, :], bk.filled(act, f"zt{k}", i - 1)[:], ACT.Copy).then_inc(bk.e(f"zt{k}"), 1)
                    if b:
                        keep(i, 4)
                    if a:
                        bk.filled(act, "d21", i)
                        ac(d1[:], bk.filled(act, "d1", i + 1)[:], ACT.Tanh).then_inc(bk.e("d1"), 1)
                    if b:
                        keep(i, 5)
                        level_ready(act, 1, i)
                        bk.filled(act, "a13", i)
                    if a:
                        for k in range(CC):
                            ps = bk.filled(act, f"k{k}", i + 1)
                            ac(ks[0][:, k, :], ps[:], ACT.Copy)
                            ac(ku[:, k, :], ps[:], ACT.Copy, scale=sh.vecs[:, 1, k:k + 1]).then_inc(bk.e(f"k{k}"), 1)
                        for k in range(CC):
                            ps = bk.filled(act, f"r{k}", i + 1)
                            ac(rx[0][0:N, 0, k, :], ps[0:N, :], ACT.Copy)
                            ac(rx[0][N:P, 1, k, :], ps[N:P, :], ACT.Copy).then_inc(bk.e(f"r{k}"), 1)
                    if b:
                        bk.emptied(act, "a163", i)
                        ps = bk.filled(act, "b", i)
                        for r0 in (0, 64):
                            ins = ac(wt[r0:r0 + 32, :, :, :, r0 + 32:r0 + 64].rearrange("p q h l t -> p (q h l) t"),
                                     ps[r0:r0 + 32, :].rearrange("p (n t) -> p n t", t=32), ACT.Copy)
                        ins.then_inc(bk.e("b"), 1)
                        keep(i, 6)
                        for n in range(2):
                            ac(wt[0:64, 2 * n:2 * n + 2, :, :, 64:128].rearrange("p q h l t -> p (q h l) t"),
                               bk.filled(act, f"c{n}", i)[0:64, :].rearrange("p (n t) -> p n t", t=64),
                               ACT.Copy).then_inc(bk.e(f"c{n}"), 1)
                    if a:
                        if b:
                            act.wait_ge(s["multiplied"], LAST * i + 1)
                            act.wait_ge(s["multiplied1"], LAST * i + 1)
                        for k in range(CC):
                            ac(tot[0][:, k, :], bk.filled(act, f"d2{k}", i + 1)[:], ACT.Exp,
                               bias=sh.vecs[:, 0, k:k + 1]).then_inc(bk.e(f"d2{k}"), 1)
                    if b:
                        for n, cols in ((0, 512), (1, 256)):
                            bk.filled(act, "kv1", i - 1)
                            ps = bk.filled(act, f"kt{n}", i)
                            ac(kt[:, 2 * n:min(2 * n + 2, QC - 1), :, :].rearrange("p q h s -> p (q h s)"),
                               ps[:, 0:cols], ACT.Copy).then_inc(bk.e(f"kt{n}"), 1)
                    if a:
                        bk.emptied(act, "d20", i + 1)
                        bk.emptied(act, "d21", i + 1)
                        ac(tot[0][:], tot[0][:], ACT.Exp, scale=-1.0).then_inc(s["decay_made"], 1)
                    if b:
                        upto(act, "yn_made", i)
                        for q in range(QC):
                            ac(y[:, q, :], bk.filled(act, f"y{q}", i)[:, 0:C], ACT.Copy).then_inc(bk.e(f"y{q}"), 1)
                    if a:
                        for n in range(2):
                            ac(vv[:, 2 * n:2 * n + 2, :].rearrange("p q c -> p (q c)"),
                               bk.filled(act, f"v{n}", i + 1)[:], ACT.Copy).then_inc(bk.e(f"v{n}"), 1)
                        keep(i + 1, 0)

                rounds(act, step)


def macaron(nc, x, attn, ffn_in, out):
    x1 = nc.dram_tensor("after_ffn1", [NTOK, C], F32, kind="Internal").ap()
    x2 = nc.dram_tensor("after_attention", [NTOK, C], F32, kind="Internal").ap()
    with ExitStack() as ctx:
        sh = Shared(nc, ctx)
        load_attention(sh)
        load_constants(sh, ffn_in)
        onehot = sh.sb("onehot", [P, NT, E])
        index = sh.sb("index", [P, NS], U32)
        expert = sh.sb("expert", [1, NS], I32)

        def ffn_loads(sp):
            start_ffn_loads(sp, sh, ffn_in)

        def all_loads(sp):
            ffn_loads(sp)
            with nc.allow_non_contiguous_dma(reason="vectors of 256 to 128 partitions"):
                start_attention_loads(sp, sh, attn)

        with ExitStack() as weights:
            place_ffn_weights(sh, weights)
            choose_experts(sh, x, onehot, all_loads)
            place_tokens(sh, onehot, index, expert)
            ffn(sh, x, x1, index, expert)
        attention(sh, x1, x2, onehot)
        with ExitStack() as weights:
            place_ffn_weights(sh, weights)
            place_tokens(sh, onehot, index, expert, ffn_loads)
            ffn(sh, x2, out, index, expert)


_ATTN = ["time_maa_x", "time_maa_w", "time_maa_k", "time_maa_v", "time_maa_r", "time_maa_g", "time_maa_w1",
         "time_maa_w2", "time_decay", "time_decay_w1", "time_decay_w2", "time_faaaa", "Wr", "Wk", "Wv", "Wg", "Wo",
         "ln_w", "ln_b"]
_FFN = ["W_router", "W1", "b1", "Wo", "bo", "ln_gamma", "ln_beta"]


def kernel(**inputs):
    import numpy as _np
    import concourse.bacc as _bacc
    from concourse import mybir as _mybir
    from concourse.bass_utils import run_bass_kernel_spmd as _run

    nc = _bacc.Bacc("TRN2", target_bir_lowering=False, num_devices=1)
    arrays = {}

    def given(name):
        a = _np.ascontiguousarray(inputs[name])
        arrays[f"in_{name}"] = a
        return nc.dram_tensor(f"in_{name}", a.shape, _mybir.dt.from_np(a.dtype), kind="ExternalInput").ap()

    x = given("L0_attn_x")
    attn = {k: given("L0_attn_" + k) for k in _ATTN}
    ffn_in = {k: given("L0_ffn_" + k) for k in _FFN}
    out = nc.dram_tensor("out_0", x.shape, F32, kind="ExternalOutput").ap()
    macaron(nc, x.rearrange("b t c -> (b t) c"), attn, ffn_in, out.rearrange("b t c -> (b t) c"))
    r = _run(nc, [arrays], core_ids=[0])
    return r.results[0]["out_0"]
```

```python
from contextlib import ExitStack

import concourse.bass as bass
from concourse import mybir

F32 = mybir.dt.float32
F32R = mybir.dt.float32r
U32 = mybir.dt.uint32
I32 = mybir.dt.int32
U8 = mybir.dt.uint8
ALU = mybir.AluOpType
ACT = mybir.ActivationFunctionType
AX = mybir.AxisListType

P = 128
B, T, C = 8, 512, 256
NTOK = B * T
NT = NTOK // P
TB = T // P
CC = C // P
E = 4
I = 1024
IC = I // P
HB = 512
NH = I // HB
NS = NT + E - 1
NONE = 2 * NTOK
LN_EPS = 1e-5
FFN_EPS = 1e-12


def ds(i, n=1):
    return bass.ds(i, n)


class Shared:

    def __init__(self, nc, ctx):
        self.nc, self.ctx, self.n = nc, ctx, 0

    def sem(self, name):
        self.n += 1
        return self.ctx.enter_context(self.nc.semaphore(f"{name}_{self.n}"))

    def sb(self, name, shape, dt=F32, ctx=None):
        self.n += 1
        return (ctx or self.ctx).enter_context(self.nc.sbuf_tensor(f"{name}_{self.n}", shape, dt))

    def ps(self, name, shape, dt=F32, ctx=None):
        self.n += 1
        return (ctx or self.ctx).enter_context(self.nc.psum_tensor(f"{name}_{self.n}", shape, dt))


def load_constants(sh, d):
    nc = sh.nc
    sh.ident = sh.sb("ident", [P, P])
    sh.ones = sh.sb("ones", [P, P])
    sh.before = sh.sb("before", [P, P])
    sh.count = sh.sb("count", [P, P])
    sh.token = sh.sb("token", [P, NT])
    sh.steps = sh.sb("steps", [P, NS + 1])
    sh.w_router = sh.sb("w_router", [P, CC, E])
    sh.lane = sh.sb("minus_half", [P, HB // 8])

    sh.router_in = sh.sem("router_in")
    sh.built = sh.sem("built")
    ready = sh.sem("constants_ready")

    with nc.Block() as block:

        @block.sync
        def _(sp):
            sp.dma_start(sh.w_router[:], d["W_router"].rearrange("(c p) e -> p c e", p=P)).then_inc(sh.router_in, 16)

        @block.gpsimd
        def _(pool):
            g = nc.gpsimd
            g.memset(sh.ident[:], 0.0).then_inc(sh.built, 1)
            g.memset(sh.before[:], 1.0).then_inc(sh.built, 1)
            g.memset(sh.ones[:], 1.0)
            g.memset(sh.lane[:], -0.5)
            for padded in (sh.mix1, sh.mix2, sh.dw1, sh.dw2):
                g.memset(padded[:], 0.0)
            pool.wait_ge(sh.built, 2)
            g.affine_select(out=sh.ident[:], in_=sh.ident[:], compare_op=ALU.not_equal, fill=1.0, base=0,
                            pattern=[[-1, P]], channel_multiplier=1)
            g.affine_select(out=sh.before[:], in_=sh.before[:], compare_op=ALU.is_gt, fill=0.0, base=0,
                            pattern=[[1, P]], channel_multiplier=-1)
            g.iota(sh.count[:], pattern=[[1, P]], base=0, channel_multiplier=0, allow_small_or_imprecise_dtypes=True)
            g.iota(sh.token[:], pattern=[[P, NT]], base=-NONE, channel_multiplier=1,
                   allow_small_or_imprecise_dtypes=True)
            g.iota(sh.steps[:], pattern=[[P, NS + 1]], base=0, channel_multiplier=0,
                   allow_small_or_imprecise_dtypes=True).then_inc(ready, 1)
            pool.wait_ge(ready, 1)


def place_ffn_weights(sh, ctx):
    sh.stage = sh.sb("stage", [P, (E * CC + CC) * I], ctx=ctx)
    sh.w1 = sh.stage[:, 0:E * CC * I].rearrange("p (e c i) -> p e c i", e=E, c=CC)
    sh.wo = sh.stage[:, E * CC * I:(E * CC + CC) * I]
    sh.b1 = sh.sb("b1", [P, E, I], ctx=ctx)
    sh.bo = sh.sb("bo", [P, C], ctx=ctx)
    sh.gamma = sh.sb("gamma", [P, C], ctx=ctx)
    sh.beta = sh.sb("beta", [P, C], ctx=ctx)
    sh.w1_in = [sh.sem(f"w1_in{e}") for e in range(E)]
    sh.wo_in = sh.sem("wo_in")
    sh.ffn_in = sh.sem("ffn_in")


def place_split_weights(sh, ctx):
    sh.w1_high = sh.sb("w1_high", [P, E, CC, I], F32R, ctx=ctx)
    sh.w1_low = sh.sb("w1_low", [P, E, CC, I], F32R, ctx=ctx)
    sh.wo_high = sh.sb("wo_high", [P, IC, C], F32R, ctx=ctx)
    sh.wo_low = sh.sb("wo_low", [P, IC, C], F32R, ctx=ctx)


def start_ffn_loads(sp, sh, d):
    for e in range(E):
        sp.dma_start(sh.w1[:, e, :, :], d["W1"][e].rearrange("(c p) i -> p c i", p=P)).then_inc(sh.w1_in[e], 16)
    sp.dma_start(sh.wo.rearrange("p (c n) -> p c n", n=C), d["Wo"].rearrange("(c p) n -> p c n", p=P)
                 ).then_inc(sh.wo_in, 16)
    for to, name in ((sh.bo, "bo"), (sh.gamma, "ln_gamma"), (sh.beta, "ln_beta")):
        sp.dma_start(to[:], d[name].partition_broadcast(P)).then_inc(sh.ffn_in, 16)
    for e in range(E):
        sp.dma_start(sh.b1[:, e, :], d["b1"][e].partition_broadcast(P)).then_inc(sh.ffn_in, 16)


FFN_LOADED = 16 * (3 + E)


def at_least(eng, sem, value):
    if not isinstance(value, int) or value > 0:
        eng.wait_ge(sem, value)


def over(eng, total, step, tail=0):
    pairs = (total - tail) // 2
    step(0, 0, 0)
    step(1, 0, 1)
    with eng.Fori(1, pairs) as k:
        for u in range(2):
            step(2 * k + u, k, u)
    for j in range(2 * pairs, total):
        step(j, j // 2, j % 2)


def over4(eng, total, step, tail=0):
    fours = (total - tail) // 4
    for j in range(4):
        step(j, j // 2, j)
    with eng.Fori(1, fours) as q:
        for u in range(4):
            step(4 * q + u, 2 * q + u // 2, u)
    for j in range(4 * fours, total):
        step(j, j // 2, j % 4)


def choose_experts(sh, src, onehot, extra_loads=None):
    nc = sh.nc
    src_v = src.rearrange("(b t p) c -> b p t c", p=P, t=TB)
    with ExitStack() as own:
        two = lambda name, shape: [sh.sb(name, shape, ctx=own) for _ in range(2)]
        x = sh.sb("x_in", [P, NT, C], ctx=own)
        xn = two("xn", [P, TB, C])
        xt = two("xn_t", [P, CC, T])
        st = sh.sb("stats", [P, TB, 6], ctx=own)
        mv = two("mean_var", [P, TB, 2])
        ve = two("var_eps", [P, TB])
        rs = two("rstd", [P, TB])
        mx = sh.sb("top", [P, TB, 1], ctx=own)
        sc = sh.sb("score", [P, TB, E], ctx=own)
        rank = sh.sb("rank", [P, TB, E], ctx=own)
        pt = [sh.ps("ps_xt", [P, CC, T], ctx=own) for _ in range(2)]
        pl = [sh.ps("ps_logit", [P, HB], ctx=own) for _ in range(2)]

        x_in = [sh.sem("x_in") for _ in range(2)]
        did_aggr = sh.sem("did_aggr")
        did_var = sh.sem("did_var")
        did_rstd = sh.sem("did_rstd")
        did_xn = sh.sem("did_xn")
        did_pt = sh.sem("did_transposes")
        did_xt = sh.sem("did_xt")
        did_logit = sh.sem("did_logit")
        did_top = sh.sem("did_top")
        did_eq = sh.sem("did_eq")
        did_sc = sh.sem("did_score")
        did_best = sh.sem("did_best")
        did_hot = sh.sem("did_onehot")
        did_rank = sh.sem("did_rank")
        with nc.Block() as block:

            @block.sync
            def _(sp):
                sp.dma_start(x[:, 0:TB, :], src_v[0]).then_inc(x_in[0], 16)
                sp.dma_start(x[:, TB:2 * TB, :], src_v[1]).then_inc(x_in[1], 16)
                with sp.Fori(1, B // 2) as k:
                    for u in range(2):
                        sp.wait_ge(x_in[u], 16 * k)
                        sp.dma_start(x[:, ds(TB * (2 * k + u), TB), :],
                                     src_v[ds(2 * k + u)].rearrange("a p t c -> (a p) t c")).then_inc(x_in[u], 16)
                if extra_loads:
                    extra_loads(sp)

            @block.gpsimd
            def _(pool):
                g = nc.gpsimd
                g.iota(rank[:], pattern=[[0, TB], [-1, E]], base=E, channel_multiplier=0,
                       allow_small_or_imprecise_dtypes=True).then_inc(did_rank, 1)

                def step(b, k, u):
                    pool.wait_ge(did_var, b + 1)
                    at_least(pool, did_xn, b - 1)
                    g.tensor_tensor(rs[u][:], ve[u][:], sh.lane[:, 0:TB], ALU.pow).then_inc(did_rstd, 1)

                over(pool, B, step)

            @block.vector
            def _(dve):
                v = nc.vector
                dve.wait_ge(did_rank, 1)

                def rows(b, t):
                    return x[:, TB * b + t, :] if isinstance(b, int) else \
                        x[:, ds(TB * b + t), :].rearrange("p a c -> p (a c)")

                def statistics(b, k, u):
                    dve.wait_ge(x_in[u], 16 * k + 16)
                    for t in range(TB):
                        v.bn_stats(st[:, t, :], rows(b, t))
                    dve.drain()
                    for t in range(TB):
                        s = v.bn_aggr(mv[u][:, t, :], st[:, t, :])
                    s.then_inc(did_aggr, 1)
                    dve.wait_ge(did_aggr, b + 1)
                    at_least(dve, did_rstd, b - 1)
                    v.tensor_scalar(ve[u][:], mv[u][:, :, 1], LN_EPS, None, ALU.add).then_inc(did_var, 1)

                def normalise(b, u):
                    dve.wait_ge(did_rstd, b + 1)
                    at_least(dve, did_pt, b - 1)
                    for t in range(TB):
                        s = v.tensor_scalar(xn[u][:, t, :], rows(b, t), mv[u][:, t, 0:1], rs[u][:, t:t + 1],
                                            ALU.subtract, ALU.mult)
                    s.then_inc(did_xn, 1)

                def choose(b, u):
                    logits = pl[u][:, 0:TB * E].rearrange("p (t e) -> p t e", e=E)
                    dve.wait_ge(did_logit, b + 1)
                    v.tensor_reduce(mx[:], logits, AX.X, ALU.max).then_inc(did_top, 1)
                    dve.wait_ge(did_top, b + 1)
                    v.tensor_tensor(sc[:], logits, mx[:].to_broadcast([P, TB, E]), ALU.is_equal
                                    ).then_inc(did_eq, 1)
                    dve.wait_ge(did_eq, b + 1)
                    v.tensor_tensor(sc[:], sc[:], rank[:], ALU.mult).then_inc(did_sc, 1)
                    dve.wait_ge(did_sc, b + 1)
                    v.tensor_reduce(mx[:], sc[:], AX.X, ALU.max).then_inc(did_best, 1)
                    dve.wait_ge(did_best, b + 1)
                    v.tensor_tensor(onehot[:, ds(TB * b, TB), :], sc[:], mx[:].to_broadcast([P, TB, E]),
                                    ALU.is_equal).then_inc(did_hot, 1)
                    dve.wait_ge(did_hot, b + 1)

                statistics(0, 0, 0)

                def step(b, k, u):
                    if not isinstance(b, int) or b + 1 < B:
                        statistics(b + 1, k + u, 1 - u)
                    normalise(b, u)
                    if not isinstance(b, int) or b > 1:
                        choose(b - 2, u)

                over(dve, B, step, tail=2)
                choose(B - 2, 0)
                choose(B - 1, 1)

            @block.tensor
            def _(pe):
                pe.wait_ge(sh.router_in, 16)

                def transposes(b, u):
                    pe.wait_ge(did_xn, b + 1)
                    at_least(pe, did_xt, b - 1)
                    for c in range(CC):
                        for t in range(TB):
                            m = nc.tensor.transpose(pt[u][:, c, t * P:(t + 1) * P],
                                                    xn[u][:, t, c * P:(c + 1) * P], sh.ident[:])
                    m.then_inc(did_pt, 1)

                transposes(0, 0)

                def step(b, k, u):
                    if not isinstance(b, int) or b + 1 < B:
                        transposes(b + 1, 1 - u)
                    pe.wait_ge(did_xt, b + 1)
                    at_least(pe, did_eq, b - 1)
                    for t in range(TB):
                        for c in range(CC):
                            m = nc.tensor.matmul(pl[u][:, t * E:(t + 1) * E], xt[u][:, c, t * P:(t + 1) * P],
                                                 sh.w_router[:, c, :], start=(c == 0), stop=(c == CC - 1))
                    m.then_inc(did_logit, 1)

                over(pe, B, step, tail=2)

            @block.scalar
            def _(act):

                def step(b, k, u):
                    act.wait_ge(did_pt, b + 1)
                    at_least(act, did_logit, b - 1)
                    for c in range(CC):
                        s = nc.scalar.activation(xt[u][:, c, :], pt[u][:, c, :], ACT.Copy)
                    s.then_inc(did_xt, 1)

                over(act, B, step)


def place_tokens(sh, onehot, index, expert, loads=None):
    nc = sh.nc
    with ExitStack() as own:
        a = lambda name, shape, dt=F32: sh.sb(name, shape, dt, ctx=own)
        upto = a("upto", [P, E, NT])
        more = a("more", [P, E, NT])
        tiles = a("tiles", [P, E])
        ends = a("ends", [P, E])
        first = a("first", [P, E])
        slots = a("slots", [P, NT, E])
        slots2 = a("slots2", [P, NT, E])
        slot = a("slot", [P, NT])
        beyond = a("beyond", [P, NT, NS])
        tile_of = a("tile_of", [P, NT])
        row_of = a("row_of", [P, NT])
        is_row = a("is_row", [P, NT, P])
        is_tile = a("is_tile", [P, NT, NS])
        kind = a("kind", [P, 3, NS])
        pp = sh.ps("ps_prefix", [P, 2, NT, E], ctx=own)
        pi = sh.ps("ps_index", [P, NS], ctx=own)
        did_sums = sh.sem("did_sums")
        did_inverse = sh.sem("did_inverse")
        did_high = sh.sem("did_high")
        did = sh.sem("placing")
        with nc.Block() as block:

            if loads:
                @block.sync
                def _(sp):
                    loads(sp)

            parts = [(sh.w1[:, e], sh.w1_high[:, e], sh.w1_low[:, e], sh.w1_in[e]) for e in range(E)]
            parts += [(sh.wo.rearrange("p (c n) -> p c n", n=C), sh.wo_high[:], sh.wo_low[:], sh.wo_in)]

            @block.scalar
            def _(act):
                for whole, high, low, loaded in parts:
                    act.wait_ge(loaded, 16)
                    nc.scalar.activation(high, whole, ACT.Copy).then_inc(did_high, 1)

            @block.gpsimd
            def _(pool):
                for n, (whole, high, low, loaded) in enumerate(parts):
                    pool.wait_ge(did_high, n + 1)
                    nc.gpsimd.tensor_tensor(low, whole, high, ALU.subtract)

            @block.tensor
            def _(pe):
                flat = onehot[:].rearrange("p t e -> p (t e)")
                nc.tensor.matmul(pp[:, 0, :, :].rearrange("p t e -> p (t e)"), sh.before[:], flat,
                                 start=True, stop=True)
                nc.tensor.matmul(pp[:, 1, :, :].rearrange("p t e -> p (t e)"), sh.ones[:], flat,
                                 start=True, stop=True).then_inc(did_sums, 1)
                for t in range(NT):
                    if t % ROWS_AT_ONCE == 0:
                        pe.wait_ge(did, STEPS_TO_ROWS + t // ROWS_AT_ONCE + 1)
                    m = nc.tensor.matmul(pi[:], is_row[:, t, :], is_tile[:, t, :], start=(t == 0), stop=(t == NT - 1))
                m.then_inc(did_inverse, 1)

            @block.vector
            def _(dve):
                v = nc.vector
                n = [0]

                def step(ins):
                    n[0] += 1
                    ins.then_inc(did, 1)
                    dve.wait_ge(did, n[0])

                dve.wait_ge(did_sums, 1)
                for e in range(E):
                    s = v.tensor_tensor_scan(upto[:, e, :], sh.ones[:, 0:NT], pp[:, 1, :, e], 0.0, ALU.mult, ALU.add)
                step(s)
                step(v.tensor_tensor(more[:], upto[:, :, NT - 1:NT].to_broadcast([P, E, NT]),
                                     sh.steps[:, 0:NT].unsqueeze(1).to_broadcast([P, E, NT]), ALU.is_gt))
                step(v.tensor_reduce(tiles[:].unsqueeze(2), more[:], AX.X, ALU.add))
                step(v.tensor_tensor_scan(ends[:], sh.ones[:, 0:E], tiles[:], 0.0, ALU.mult, ALU.add))
                step(v.tensor_tensor(first[:], ends[:], tiles[:], ALU.subtract))
                step(v.tensor_tensor(slots[:], upto[:].rearrange("p e t -> p t e"), pp[:, 1, :, :], ALU.subtract))
                step(v.tensor_tensor(slots[:], slots[:], pp[:, 0, :, :], ALU.add))
                for e in range(E):
                    s = v.scalar_tensor_tensor(slots2[:, :, e], first[:, e:e + 1].to_broadcast([P, NT]), float(P),
                                               slots[:, :, e], ALU.mult, ALU.add)
                step(s)
                step(v.tensor_tensor(slots2[:], slots2[:], onehot[:], ALU.mult))
                step(v.tensor_reduce(slot[:].unsqueeze(2), slots2[:], AX.X, ALU.add))
                step(v.tensor_tensor(beyond[:], slot[:].unsqueeze(2).to_broadcast([P, NT, NS]),
                                     sh.steps[:, 1:NS + 1].unsqueeze(1).to_broadcast([P, NT, NS]), ALU.is_ge))
                step(v.tensor_reduce(tile_of[:].unsqueeze(2), beyond[:], AX.X, ALU.add))
                step(v.scalar_tensor_tensor(row_of[:], tile_of[:], -float(P), slot[:], ALU.mult, ALU.add))
                step(v.tensor_tensor(is_tile[:], tile_of[:].unsqueeze(2).to_broadcast([P, NT, NS]),
                                     sh.count[:, 0:NS].unsqueeze(1).to_broadcast([P, NT, NS]), ALU.is_equal))
                step(v.tensor_tensor(is_tile[:], is_tile[:], sh.token[:].unsqueeze(2).to_broadcast([P, NT, NS]),
                                     ALU.mult))
                assert n[0] == STEPS_TO_ROWS
                for t in range(0, NT, ROWS_AT_ONCE):
                    t_, shape = slice(t, t + ROWS_AT_ONCE), [P, ROWS_AT_ONCE, P]
                    step(v.tensor_tensor(is_row[:, t_, :], row_of[:, t_].unsqueeze(2).to_broadcast(shape),
                                         sh.count[:].unsqueeze(1).to_broadcast(shape), ALU.is_equal))
                for e in range(1, E):
                    s = v.tensor_scalar(kind[:, e - 1, :], sh.count[:, 0:NS], first[:, e:e + 1], None, ALU.is_ge)
                step(s)
                step(v.tensor_tensor(kind[:, 0, :], kind[:, 0, :], kind[:, 1, :], ALU.add))
                step(v.tensor_tensor(expert[:], kind[0:1, 0, :], kind[0:1, 2, :], ALU.add))
                dve.wait_ge(did_inverse, 1)
                step(v.tensor_scalar(index[:], pi[:], float(NONE), None, ALU.add))


STEPS_TO_ROWS = 15
ROWS_AT_ONCE = NT // 4


def ffn(sh, src, dst, index, expert):
    nc = sh.nc
    with ExitStack() as own:
        a = lambda name, shape, dt=F32: sh.sb(name, shape, dt, ctx=own)
        two = lambda name, shape, dt=F32: [a(name, shape, dt) for _ in range(2)]
        used = [0]

        def staged(n):
            used[0] += n
            return sh.stage[:, used[0] - n:used[0]]

        gi = two("gather_index", [P, 1], U32)
        si = two("scatter_index", [P, 1], U32)
        x = [staged(C) for _ in range(2)]
        xn = [staged(C) for _ in range(2)]
        xn_bo = [staged(C) for _ in range(4)]
        x_beta = [staged(C) for _ in range(4)]
        hb = [staged(I) for _ in range(2)]
        hg = [staged(I) for _ in range(2)]
        z = [staged(C) for _ in range(2)]
        zg = staged(C)
        out = [staged(C) for _ in range(2)]
        xt_high = two("xn_t_high", [P, CC, P], F32R)
        xt_low = two("xn_t_low", [P, CC, P], F32R)
        ht_high = two("hidden_t_high", [P, IC, P], F32R)
        ht_low = two("hidden_t_low", [P, IC, P], F32R)
        st = [a("stats", [P, 6]) for _ in range(2)]
        mv_x, ve_x, rs_x = a("mean_var", [P, 2]), a("var_eps", [P, 1]), a("rstd", [P, 1])
        mv_z, ve_z, rs_z = two("z_mean_var", [P, 2]), two("z_var_eps", [P, 1]), two("z_rstd", [P, 1])
        p_xt = [sh.ps("ps_xt", [P, HB], ctx=own) for _ in range(2)]
        p_h = sh.ps("ps_h", [P, NH, HB], ctx=own)
        p_ht = sh.ps("ps_ht", [P, 2, HB], ctx=own)
        p_y = [sh.ps("ps_y", [P, HB], ctx=own) for _ in range(2)]

        halved = sh.sem("halved")
        cleared = sh.sem("cleared")
        got_x = [sh.sem("got_x") for _ in range(2)]
        stored = [sh.sem("stored") for _ in range(2)]
        names = ("x_aggr x_var x_rstd xn_made x_beta_made xn_bo_made xt_ps xt_high_made xt_made h_ps h_biased h_made "
                 "ht_ps ht_high_made ht_made y_ps z_made z_aggr z_var z_rstd zg_made out_made")
        s = {k: sh.sem(k) for k in names.split()}

        def there(j):
            return not isinstance(j, int) or 0 <= j < NS

        with nc.Block() as block:

            @block.gpsimd
            def _(pool):
                g = nc.gpsimd
                last_token = pool.to_reg(NTOK - 1)

                def gather(j, p):
                    g.tensor_copy(gi[p][:], index[:, ds(j)])
                    pool.drain()
                    g.indirect_dma_start(out=x[p], out_offset=None, in_=src,
                                         in_offset=bass.IndirectOffsetOnAxis(ap=gi[p][:, 0:1], axis=0),
                                         bounds_check=last_token, oob_is_err=False).then_inc(got_x[p], 16)

                def x_rstd(j):
                    pool.wait_ge(s["x_var"], j + 1)
                    at_least(pool, s["xn_made"], j)
                    g.tensor_tensor(rs_x[:], ve_x[:], sh.lane[:, 0:1], ALU.pow).then_inc(s["x_rstd"], 1)

                def x_plus_beta(j, p, r):
                    at_least(pool, s["out_made"], j - 3)
                    g.tensor_tensor(x_beta[r], x[p], sh.beta[:], ALU.add).then_inc(s["x_beta_made"], 1)

                def xn_plus_bo(j, p, r):
                    pool.wait_ge(s["xn_made"], j + 1)
                    at_least(pool, s["z_made"], j - 3)
                    g.tensor_tensor(xn_bo[r], xn[p], sh.bo[:], ALU.add).then_inc(s["xn_bo_made"], 1)

                def z_rstd(j, p):
                    pool.wait_ge(s["z_var"], j + 1)
                    at_least(pool, s["out_made"], j - 1)
                    g.tensor_tensor(rs_z[p][:], ve_z[p][:], sh.lane[:, 0:1], ALU.pow).then_inc(s["z_rstd"], 1)

                def scatter(j, k, p):
                    at_least(pool, stored[p], 16 * k)
                    pool.wait_ge(s["out_made"], j + 1)
                    g.tensor_copy(si[p][:], index[:, ds(j)])
                    pool.drain()
                    g.indirect_dma_start(out=dst, out_offset=bass.IndirectOffsetOnAxis(ap=si[p][:, 0:1], axis=0),
                                         in_=out[p], in_offset=None,
                                         bounds_check=last_token, oob_is_err=False).then_inc(stored[p], 16)

                g.memset(x[0], 0.0)
                g.memset(x[1], 0.0).then_inc(cleared, 1)
                pool.wait_ge(cleared, 1)
                gather(0, 0)
                gather(1, 1)
                pool.wait_ge(sh.ffn_in, FFN_LOADED)
                pool.wait_ge(halved, 1)
                for j in range(2):
                    x_rstd(j)
                    x_plus_beta(j, j, j)
                    xn_plus_bo(j, j, j)
                    pool.wait_ge(s["x_beta_made"], j + 1)
                    gather(j + 2, j)

                def step(j, k, u):
                    p, r = u % 2, (u + 2) % 4
                    if there(j + 2):
                        x_rstd(j + 2)
                    if there(j - 2):
                        scatter(j - 2, k - 1, p)
                    if there(j - 1):
                        z_rstd(j - 1, 1 - p)
                    if there(j + 2):
                        x_plus_beta(j + 2, p, r)
                        xn_plus_bo(j + 2, p, r)
                    if there(j + 4):
                        pool.wait_ge(s["x_beta_made"], j + 3)
                        gather(j + 4, p)

                over4(pool, NS, step, tail=4)
                z_rstd(NS - 1, (NS - 1) % 2)
                for j in (NS - 2, NS - 1):
                    scatter(j, j // 2, j % 2)
                pool.wait_ge(stored[0], 16 * ((NS + 1) // 2))
                pool.wait_ge(stored[1], 16 * (NS // 2))

            @block.vector
            def _(dve):
                v = nc.vector

                def x_stats(j, k, p):
                    dve.wait_ge(got_x[p], 16 * k + 16)
                    at_least(dve, s["xn_made"], j)
                    v.bn_stats(st[0][:], x[p])
                    dve.drain()
                    v.bn_aggr(mv_x[:], st[0][:]).then_inc(s["x_aggr"], 1)
                    dve.wait_ge(s["x_aggr"], j + 1)
                    v.tensor_scalar(ve_x[:], mv_x[:, 1:2], LN_EPS, None, ALU.add).then_inc(s["x_var"], 1)

                def x_norm(j, p):
                    dve.wait_ge(s["x_rstd"], j + 1)
                    at_least(dve, s["xn_bo_made"], j - 1)
                    at_least(dve, s["xt_ps"], j - 1)
                    v.tensor_scalar(xn[p], x[p], mv_x[:, 0:1], rs_x[:], ALU.subtract, ALU.mult
                                    ).then_inc(s["xn_made"], 1)

                def xt_rest(j, p):
                    dve.wait_ge(s["xt_high_made"], j + 1)
                    at_least(dve, s["h_ps"], NH * (j - 1))
                    v.tensor_tensor(xt_low[p][:].rearrange("p c k -> p (c k)"), p_xt[p][:, 0:C],
                                    xt_high[p][:].rearrange("p c k -> p (c k)"), ALU.subtract
                                    ).then_inc(s["xt_made"], 1)

                def ht_rest(j, p):
                    h = IC // 2
                    for n in range(2):
                        dve.wait_ge(s["ht_high_made"], 2 * j + n + 1)
                        at_least(dve, s["y_ps"], j - 1)
                        v.tensor_tensor(ht_low[p][:, n * h:(n + 1) * h, :].rearrange("p k t -> p (k t)"),
                                        p_ht[:, n, :],
                                        ht_high[p][:, n * h:(n + 1) * h, :].rearrange("p k t -> p (k t)"),
                                        ALU.subtract).then_inc(s["ht_made"], 1)

                def its_expert(j):
                    return dve.value_load(expert[0:1, ds(j)], min_val=0, max_val=E - 1)

                def bias(j, p, e):
                    for n in range(NH):
                        dve.wait_ge(s["h_ps"], NH * j + n + 1)
                        at_least(dve, s["h_made"], NH * (j - 2) + n + 1)
                        v.tensor_tensor(hb[p][:, n * HB:(n + 1) * HB].unsqueeze(1), p_h[:, n, :].unsqueeze(1),
                                        sh.b1[:, ds(e), n * HB:(n + 1) * HB], ALU.add).then_inc(s["h_biased"], 1)

                def z_stats(j, p, r):
                    dve.wait_ge(s["y_ps"], j + 1)
                    dve.wait_ge(s["xn_bo_made"], j + 1)
                    v.tensor_tensor(z[p], p_y[p][:, 0:C], xn_bo[r], ALU.add).then_inc(s["z_made"], 1)
                    dve.wait_ge(s["z_made"], j + 1)
                    v.bn_stats(st[1][:], z[p])
                    dve.drain()
                    v.bn_aggr(mv_z[p][:], st[1][:]).then_inc(s["z_aggr"], 1)
                    dve.wait_ge(s["z_aggr"], j + 1)
                    v.tensor_scalar(ve_z[p][:], mv_z[p][:, 1:2], FFN_EPS, None, ALU.add).then_inc(s["z_var"], 1)

                def z_norm(j, k, p, r):
                    v.scalar_tensor_tensor(zg, z[p], mv_z[p][:, 0:1], sh.gamma[:], ALU.subtract, ALU.mult
                                           ).then_inc(s["zg_made"], 1)
                    dve.wait_ge(s["z_rstd"], j + 1)
                    at_least(dve, stored[p], 16 * k)
                    dve.wait_ge(s["zg_made"], j + 1)
                    v.scalar_tensor_tensor(out[p], zg, rs_z[p][:], x_beta[r], ALU.mult, ALU.add
                                           ).then_inc(s["out_made"], 1)

                dve.wait_ge(sh.ffn_in, FFN_LOADED)
                v.tensor_scalar(sh.gamma[:], sh.gamma[:], 0.5, None, ALU.mult)
                v.tensor_scalar(sh.beta[:], sh.beta[:], 0.5, None, ALU.mult).then_inc(halved, 1)
                dve.wait_ge(halved, 1)
                for j in range(2):
                    x_stats(j, 0, j)
                    x_norm(j, j)
                    xt_rest(j, j)
                bias(0, 0, its_expert(0))

                def step(j, k, u):
                    p = u % 2
                    if there(j + 1):
                        e = its_expert(j + 1)
                    if there(j + 2):
                        x_stats(j + 2, k + 1, p)
                    ht_rest(j, p)
                    if there(j + 2):
                        x_norm(j + 2, p)
                    if there(j - 1):
                        z_stats(j - 1, 1 - p, (u - 1) % 4)
                    if there(j + 1):
                        bias(j + 1, 1 - p, e)
                    if there(j - 1):
                        z_norm(j - 1, k - 1 + p, 1 - p, (u - 1) % 4)
                    if there(j + 2):
                        xt_rest(j + 2, p)

                over4(dve, NS, step, tail=4)
                z_stats(NS - 1, (NS - 1) % 2, (NS - 1) % 4)
                z_norm(NS - 1, (NS - 1) // 2, (NS - 1) % 2, (NS - 1) % 4)

            @block.tensor
            def _(pe):
                mm = nc.tensor

                def products(out_, pairs, first, last):
                    n = 0
                    for (a_high, a_low), (b_high, b_low) in pairs:
                        for lhs, rhs in ((a_high, b_high), (a_high, b_low), (a_low, b_high)):
                            m = mm.matmul(out_, lhs, rhs, start=first and n == 0,
                                          stop=last and n == 3 * len(pairs) - 1)
                            n += 1
                    return m

                def xt_transposes(j, p):
                    pe.wait_ge(s["xn_made"], j + 1)
                    at_least(pe, s["xt_made"], j - 1)
                    for c in range(CC):
                        m = mm.transpose(p_xt[p][:, c * P:(c + 1) * P], xn[p][:, c * P:(c + 1) * P], sh.ident[:])
                    m.then_inc(s["xt_ps"], 1)

                def its_expert(j):
                    return pe.value_load(expert[0:1, ds(j)], min_val=0, max_val=E - 1)

                def hidden(j, p, e):
                    pe.wait_ge(s["xt_made"], j + 1)
                    for n in range(NH):
                        at_least(pe, s["h_biased"], NH * (j - 1) + n + 1)
                        w = lambda t, c: t[:, ds(e), c, n * HB:(n + 1) * HB].rearrange("p a i -> p (a i)")
                        products(p_h[:, n, :], [((xt_high[p][:, c, :], xt_low[p][:, c, :]),
                                                 (w(sh.w1_high, c), w(sh.w1_low, c))) for c in range(CC)],
                                 True, True).then_inc(s["h_ps"], 1)

                def hidden_transposes(j, p):
                    for n in range(2):
                        pe.wait_ge(s["h_made"], NH * j + n + 1)
                        at_least(pe, s["ht_made"], 2 * (j - 1) + n + 1)
                        for q in range(IC // 2):
                            k = n * IC // 2 + q
                            m = mm.transpose(p_ht[:, n, q * P:(q + 1) * P], hg[p][:, k * P:(k + 1) * P], sh.ident[:])
                        m.then_inc(s["ht_ps"], 1)

                def second(j, p):
                    at_least(pe, s["z_made"], j - 1)
                    h = IC // 2
                    for n in range(2):
                        pe.wait_ge(s["ht_made"], 2 * j + n + 1)
                        m = products(p_y[p][:, 0:C], [((ht_high[p][:, k, :], ht_low[p][:, k, :]),
                                                       (sh.wo_high[:, k, :], sh.wo_low[:, k, :]))
                                                      for k in range(n * h, (n + 1) * h)], n == 0, n == 1)
                    m.then_inc(s["y_ps"], 1)

                xt_transposes(0, 0)
                xt_transposes(1, 1)
                hidden(0, 0, its_expert(0))

                def step(j, k, u):
                    p = u % 2
                    if there(j + 1):
                        e = its_expert(j + 1)
                    hidden_transposes(j, p)
                    if there(j + 1):
                        hidden(j + 1, 1 - p, e)
                    if there(j + 2):
                        xt_transposes(j + 2, p)
                    second(j, p)

                over4(pe, NS, step, tail=4)

            @block.scalar
            def _(act):
                def xt_copy(j, p):
                    act.wait_ge(s["xt_ps"], j + 1)
                    at_least(act, s["h_ps"], NH * (j - 1))
                    nc.scalar.activation(xt_high[p][:].rearrange("p c k -> p (c k)"), p_xt[p][:, 0:C], ACT.Copy
                                         ).then_inc(s["xt_high_made"], 1)

                def gelu(j, p):
                    for n in range(NH):
                        act.wait_ge(s["h_biased"], NH * j + n + 1)
                        at_least(act, s["ht_ps"], 2 * (j - 1))
                        nc.scalar.activation(hg[p][:, n * HB:(n + 1) * HB], hb[p][:, n * HB:(n + 1) * HB], ACT.Gelu
                                             ).then_inc(s["h_made"], 1)

                def ht_copy(j, p):
                    h = IC // 2
                    for n in range(2):
                        act.wait_ge(s["ht_ps"], 2 * j + n + 1)
                        at_least(act, s["y_ps"], j - 1)
                        nc.scalar.activation(ht_high[p][:, n * h:(n + 1) * h, :].rearrange("p k t -> p (k t)"),
                                             p_ht[:, n, :], ACT.Copy).then_inc(s["ht_high_made"], 1)

                xt_copy(0, 0)
                xt_copy(1, 1)
                gelu(0, 0)

                def step(j, k, u):
                    p = u % 2
                    ht_copy(j, p)
                    if there(j + 1):
                        gelu(j + 1, 1 - p)
                    if there(j + 2):
                        xt_copy(j + 2, p)

                over4(act, NS, step, tail=4)


MIXES = 5
W_, K_, V_, R_, G_ = range(MIXES)
LORA, DLORA = 32, 64
H, N = 4, 64
HP = C // P
QC = T // P
GN_EPS = 1e-5 * 8 ** 2
HALVES = [1, 2, 4, 8, 16]
LEVELS = ["u"] + HALVES
LAST = 7

MIXING = [(s, c) for s in (W_, K_, R_, V_, G_) for c in range(CC)]
FILLS = [("b", f"au{q}") for q in range(QC)] + [("b", f"a1{q}") for q in range(QC)]
FILLS += [("a", f"xt{c}") for c in range(CC)]
FILLS += [("b", f"a2{q}") for q in range(QC)] + [("c", f"yt{c}") for c in range(CC)]
FILLS += [("a", "mixa"), ("a", "mixb")] + [("b", f"a4{q}") for q in range(QC)]
FILLS += [("b", "g0"), ("b", "g1"), ("c", "o0"), ("c", "o1")]
FILLS += [("a", f"m{s}{c}") for s, c in MIXING[:8]]
FILLS += [("b", f"a8{q}") for q in range(QC)]
FILLS += [("a", "m40"), ("a", "m41"), ("a", "d1")]
FILLS += [("b", f"a16{q}") for q in range(QC)]
FILLS += [("a", "k0"), ("a", "k1"), ("c", "zt0"), ("c", "zt1"), ("a", "r0"), ("a", "r1"), ("c", "lg")]
FILLS += [("b", "b"), ("b", "c0"), ("b", "c1"), ("a", "d20"), ("a", "d21"), ("b", "kt0"), ("b", "kt1")]
FILLS += [("a", "v0"), ("a", "v1"), ("b", "kv0"), ("b", "kv1")] + [("b", f"y{q}") for q in range(QC)]
HEAD, TAIL = 2, 3


class Banks:

    SHIFT = {"a": -1, "b": 0, "c": 1}

    def __init__(self, sh, own):
        self.ps = [sh.ps("bank", [P, HB], ctx=own) for _ in range(8)]
        self.full = [sh.sem(f"bank_full{j}") for j in range(8)]
        self.free = [sh.sem(f"bank_free{j}") for j in range(8)]
        self.bank = {name: (k % 8, kind) for k, (kind, name) in enumerate(FILLS)}
        self.before = {}
        self.per = [len(FILLS[j::8]) for j in range(8)]
        n = [0] * 8
        for i in range(-1, B + 1):
            for kind, name in FILLS:
                seq = i - self.SHIFT[kind]
                if 0 <= seq < B:
                    j = self.bank[name][0]
                    self.before[name, i] = n[j]
                    n[j] += 1

    def count(self, name, seq):
        j, kind = self.bank[name]
        if isinstance(seq, int):
            return self.before[name, seq + self.SHIFT[kind]]
        i = seq + self.SHIFT[kind]
        return i * self.per[j] + (self.before[name, HEAD] - HEAD * self.per[j])

    def open(self, pe, name, seq):
        j = self.bank[name][0]
        at_least(pe, self.free[j], self.count(name, seq))
        return self.ps[j]

    def filled(self, eng, name, seq):
        j = self.bank[name][0]
        if not (isinstance(seq, int) and seq < 0):
            eng.wait_ge(self.full[j], self.count(name, seq) + 1)
        return self.ps[j]

    def emptied(self, eng, name, seq):
        j = self.bank[name][0]
        if not (isinstance(seq, int) and seq < 0):
            eng.wait_ge(self.free[j], self.count(name, seq) + 1)

    def f(self, name):
        return self.full[self.bank[name][0]]

    def e(self, name):
        return self.free[self.bank[name][0]]


def slot(i, n):
    first = (i + n) % 4 * LORA
    return slice(first, first + LORA)


def load_attention(sh):
    sh.maa = sh.sb("maa", [P, MIXES + 1, CC])
    sh.mix1 = sh.sb("mix_w1", [P, CC, 2 * P])
    sh.mix2 = sh.sb("mix_w2", [P, MIXES, C])
    sh.dw1 = sh.sb("decay_w1", [P, CC, P])
    sh.dw2 = sh.sb("decay_w2", [P, C])
    sh.vecs = sh.sb("vectors", [P, 4, CC])
    sh.wm = {k: sh.sb(k, [P, CC, C]) for k in ("Wr", "Wk", "Wv", "Wg", "Wo")}
    sh.att_in = sh.sem("attention_in")


def start_attention_loads(q, sh, d):
    flat = lambda a: a.rearrange("(c p) -> p c", p=P)
    loads = [(sh.maa[:, n, :], flat(d["time_maa_" + k])) for n, k in enumerate("wkvrgx")]
    loads += [(sh.vecs[:, 0, :], flat(d["time_decay"])),
              (sh.vecs[:, 1, :], d["time_faaaa"].rearrange("(c h) n -> (h n) c", c=CC)),
              (sh.vecs[:, 2, :], flat(d["ln_w"])), (sh.vecs[:, 3, :], flat(d["ln_b"])),
              (sh.mix1[:, :, 0:MIXES * LORA], d["time_maa_w1"].rearrange("(c p) n -> p c n", p=P)),
              (sh.dw1[:, :, 0:DLORA], d["time_decay_w1"].rearrange("(c p) n -> p c n", p=P)),
              (sh.dw2[0:DLORA, :], d["time_decay_w2"])]
    loads += [(sh.mix2[slot(i, n), i, :], d["time_maa_w2"][i]) for i in range(MIXES) for n in range(3)]
    loads += [(sh.wm[k][:], d[k].rearrange("(c p) n -> p c n", p=P)) for k in ("Wr", "Wk", "Wv", "Wg", "Wo")]
    for to, of in loads:
        q.dma_start(to, of).then_inc(sh.att_in, 16)
    assert len(loads) == ATT_LOADS


ATT_LOADS = 33


def attention(sh, src, dst, onehot):
    nc = sh.nc
    src_v = src.rearrange("(b t p) c -> b p t c", p=P, t=TB)
    dst_v = dst.rearrange("(b t p) c -> b p t c", p=P, t=TB)
    row = lambda ap: ap.rearrange("a p t c -> (a p) t c")

    with ExitStack() as own:
        a_ = lambda name, shape, dt=F32: sh.sb(name, shape, dt, ctx=own)
        x = a_("x_in", [P, TB, C])
        xr = a_("x_out", [P, TB, C])
        mv = [a_("mean_var", [P, TB, 2]) for _ in range(2)]
        st = [a_("stats", [P, TB, 6]) for _ in range(2)]
        ve = [a_("var_eps", [P, TB]) for _ in range(2)]
        rs = [a_("rstd", [P, TB]) for _ in range(2)]
        xn = a_("xn", [P, TB, C])
        xt = a_("xn_t", [P, CC, T + 1])
        xx = a_("shift_less_x", [P, CC, T])
        xxx = a_("xxx", [P, CC, T])
        mixa = a_("mix_a", [P, T])
        mixb = a_("mix_b", [P, T])
        mix_parts = [a_("mix_parts", [P, T], F32R) for _ in range(MIXES)]
        mix_w = a_("mix_w2_parts", [P, MIXES, C], F32R)
        xs = [a_("x_mixed", [P, CC, T]) for _ in range(MIXES)]
        d1 = a_("decay_hidden", [P, T])
        tot = [a_("block_decay", [P, HP, T >> m]) for m in range(LAST + 1)]
        ks = [a_("K", [P, HP, T]) for _ in range(3)]
        rx = [a_("R", [P, 2, HP, T]) for _ in range(3)]
        ku = a_("K_u", [P, HP, T])
        vv = a_("v", [P, QC, C])
        gt = a_("g_tanh", [P, CC, T])
        gh = a_("g_half", [P, CC, T])
        wt = a_("weights", [P, QC, HP, 2, P])
        kt = a_("K_rows", [P, QC - 1, HP, P])
        ss = a_("state", [P, QC, HP, N])
        y = a_("y", [P, QC, C])
        gst = a_("y_stats", [P, QC * H, 6])
        gm = a_("y_mean", [P, QC * H])
        gd = a_("y_dif", [P, QC * H])
        gv = a_("y_var", [P, QC * H])
        gr = a_("y_rstd", [P, QC * H])
        yn = a_("yn", [P, QC, C])
        yt = a_("yn_t", [P, CC, T])
        zn = a_("zn", [P, TB, C])
        zt = a_("zn_t", [P, CC, T])
        top = a_("top", [P, TB, 1])
        sc = a_("score", [P, TB, E])
        rank = a_("rank", [P, TB, E])
        mf = {m: a_(f"mask_float{m}", [P, P]) for m in HALVES}
        masks = {m: a_(f"mask{m}", [P, P], U8) for m in HALVES}
        touched = a_("touched", [P, 32])

        bk = Banks(sh, own)
        names = ("x_var x_rstd xn_made xx_made xxx_made xs_made decay_made gate_made multiplied multiplied1 copied "
                 "tot_made s_made mix_high mix_ready y_var y_rstd y_centred yn_made gated z_var z_rstd zn_made top_made "
                 "sc_made best_made hot_made")
        s = {k: sh.sem(k) for k in names.split()}
        x_got = sh.sem("x_got")
        res_got = sh.sem("residual_got")
        stored = sh.sem("x_stored")
        masks_made = sh.sem("masks_made")
        zeros_made = sh.sem("zeros_made")
        mix_w_high = sh.sem("mix_w_high")
        mix_w_made = sh.sem("mix_w_made")
        r_zeros_made = sh.sem("r_zeros_made")
        mask_step = sh.sem("mask_step")

        def upto(eng, name, count):
            at_least(eng, s[name], count)

        def buf(n):
            return 0 if n == 0 else 2 - n % 2

        def level_ready(eng, n, b):
            if n == 0:
                bk.emptied(eng, "r1", b)
            else:
                for name in ("multiplied", "multiplied1", "copied"):
                    eng.wait_ge(s[name], LAST * b + n)

        def level_read(eng, n, b):
            names = {1: "a23", 2: "a43", 3: "a83", 4: "a163", 5: "b", 6: "c1", 7: "y3"}
            bk.filled(eng, names[n], b)

        def blocks(t, m):
            return t.rearrange("p h (n two m) -> p (h n) two m", two=2, m=m)

        def state_before(eng, q, b):
            if q == 1:
                eng.wait_ge(s["s_made"], b + 1)
            else:
                bk.emptied(eng, f"kv{q - 2}", b)

        def has_next(i):
            return not isinstance(i, int) or i + 2 < B

        def rounds(eng, step):
            step(-1, True, False, False)
            step(0, True, True, False)
            step(1, True, True, True)
            with eng.Fori(HEAD, B + 1 - TAIL) as i:
                step(i, True, True, True)
            for i in range(B + 1 - TAIL, B + 1):
                step(i, i + 1 < B, i < B, True)

        with nc.Block() as block:

            @block.sync
            def _(sp):
                sp.dma_start(x[:], src_v[0]).then_inc(x_got, 16)

                def step(i, a, b, c):
                    if a and (not isinstance(i, int) or i + 2 < B):
                        upto(sp, "xn_made", i + 2)
                        sp.dma_start(x[:], row(src_v[ds(i + 2)])).then_inc(x_got, 16)
                    if c:
                        bk.emptied(sp, "o1", i - 1)
                        sp.dma_start(row(dst_v[ds(i - 1)]), xr[:]).then_inc(stored, 16)
                    if b:
                        at_least(sp, stored, 16 * i)
                        upto(sp, "zn_made", i)
                        sp.dma_start(xr[:], row(src_v[ds(i)])).then_inc(res_got, 16)

                step(-1, True, False, False)
                step(0, True, True, False)
                step(1, True, True, True)
                with sp.Fori(HEAD, B - 2) as i:
                    step(i, True, True, True)
                step(B - 2, True, True, True)
                step(B - 1, False, True, True)
                step(B, False, False, True)
                sp.wait_ge(stored, 16 * B)

            @block.gpsimd
            def _(pool):
                g = nc.gpsimd
                g.iota(rank[:], pattern=[[0, TB], [-1, E]], base=E, channel_multiplier=0,
                       allow_small_or_imprecise_dtypes=True)
                g.memset(xt[:, :, 0:1], 0.0)
                g.memset(ss[:], 0.0).then_inc(zeros_made, 1)

                def make_masks():
                    for m in HALVES:
                        i = g.memset(mf[m][:], 1.0)
                    i.then_inc(mask_step, 1)
                    for n, (op, rows) in enumerate(((ALU.is_gt, 0), (ALU.is_ge, 1), (ALU.is_gt, -1))):
                        pool.wait_ge(mask_step, n + 1)
                        for m in HALVES:
                            blocks_of_2m = mf[m][:].rearrange("p (b h m) -> p b h m", h=2, m=m)
                            pattern = [[-2 * m * rows, P // (2 * m)], [0 if rows else 1, 2], [0, m]]
                            i = g.affine_select(out=blocks_of_2m, in_=blocks_of_2m, compare_op=op, fill=0.0,
                                                base=m if rows < 0 else 0, pattern=pattern, channel_multiplier=rows)
                        i.then_inc(mask_step, 1)
                    pool.wait_ge(mask_step, 4)
                    for m in HALVES:
                        i = g.tensor_copy(masks[m][:], mf[m][:])
                    i.then_inc(masks_made, 1)

                def add_x(seq, pairs):
                    for i, c in pairs:
                        bk.emptied(pool, f"m{i}{c}", seq)
                        g.tensor_tensor(xs[i][:, c, :], xs[i][:, c, :], xt[:, c, 1:T + 1], ALU.add
                                        ).then_inc(s["xs_made"], 1)

                def double(b, n):
                    pool.drain()
                    level_ready(pool, n, b)
                    if n == 0:
                        pool.wait_ge(s["decay_made"], b + 1)
                        if not (isinstance(b, int) and b == 0):
                            level_read(pool, 7, b - 1)
                    elif n == 1:
                        if not (isinstance(b, int) and b == 0):
                            level_read(pool, 6, b - 1)
                        pool.wait_ge(s["tot_made"], LAST * b + n)
                    else:
                        level_read(pool, n - 1, b)
                        pool.wait_ge(s["tot_made"], LAST * b + n)
                    m = 1 << n
                    t2 = tot[n][N:P].rearrange("p h (n two) -> p (h n) two", two=2)
                    g.tensor_tensor(blocks(rx[buf(n + 1)][N:P, 1], m)[:, :, 1, :],
                                    blocks(rx[buf(n)][N:P, 1], m)[:, :, 1, :],
                                    t2[:, :, 0:1].to_broadcast([N, HP * T // (2 * m), m]), ALU.mult
                                    ).then_inc(s["multiplied1"], 1)
                    pool.drain()

                def x_rstd(seq):
                    upto(pool, "x_var", seq + 1)
                    upto(pool, "xn_made", seq)
                    g.tensor_tensor(rs[0][:], ve[0][:], sh.lane[:, 0:TB], ALU.pow).then_inc(s["x_rstd"], 1)

                def group_normalise(seq):
                    heads = lambda z: z[:].rearrange("p q (h n) -> p (q h) n", n=N)
                    each = lambda z: z[:].unsqueeze(2).to_broadcast([P, QC * H, N])
                    upto(pool, "y_var", seq + 1)
                    g.tensor_tensor(gr[:], gv[:], sh.lane[:, 0:QC * H], ALU.pow).then_inc(s["y_rstd"], 1)
                    bk.filled(pool, "yt1", seq - 1)
                    g.tensor_tensor(heads(yn), heads(y), each(gm), ALU.subtract).then_inc(s["y_centred"], 1)
                    upto(pool, "y_rstd", seq + 1)
                    upto(pool, "y_centred", seq + 1)
                    g.tensor_tensor(heads(yn), heads(yn), each(gr), ALU.mult).then_inc(s["yn_made"], 1)

                def step(i, a, b, c):
                    if b:
                        double(i, 1)
                    if b:
                        double(i, 2)
                        double(i, 3)
                    if a:
                        add_x(i + 1, MIXING[:8])
                    if c:
                        upto(pool, "z_var", i)
                        upto(pool, "zn_made", i - 1)
                        g.tensor_tensor(rs[1][:], ve[1][:], sh.lane[:, 0:TB], ALU.pow).then_inc(s["z_rstd"], 1)
                    if b:
                        double(i, 4)
                    if a:
                        add_x(i + 1, MIXING[8:])
                    if b:
                        double(i, 5)
                        double(i, 6)
                    if has_next(i):
                        x_rstd(i + 2)
                    if a:
                        double(i + 1, 0)
                    if b:
                        group_normalise(i)

                x_rstd(0)
                make_masks()
                rounds(pool, step)

            @block.vector
            def _(dve):
                v = nc.vector
                dve.wait_ge(zeros_made, 1)
                dve.wait_ge(sh.att_in, 16 * ATT_LOADS)
                touches = [0]

                def statistics(k, xin, var):
                    for t in range(TB):
                        v.bn_stats(st[k][:, t, :], xin[:, t, :])
                    dve.drain()
                    for t in range(TB):
                        v.bn_aggr(mv[k][:, t, :], st[k][:, t, :])
                    dve.drain()
                    v.tensor_scalar(ve[k][:], mv[k][:, :, 1], LN_EPS, None, ALU.add).then_inc(s[var], 1)

                def normalise(k, xin, out_, rstd, made, seq):
                    dve.wait_ge(s[rstd], seq + 1)
                    bk.filled(dve, "zt1" if k else "xt1", seq - 1)
                    for t in range(TB):
                        i = v.tensor_scalar(out_[:, t, :], xin[:, t, :], mv[k][:, t, 0:1], rs[k][:, t:t + 1],
                                            ALU.subtract, ALU.mult)
                    i.then_inc(s[made], 1)

                def normalise_x(seq):
                    dve.wait_ge(x_got, 16 * seq + 16)
                    statistics(0, x, "x_var")
                    normalise(0, x, xn, "x_rstd", "xn_made", seq)

                def double(b, n):
                    level_ready(dve, n, b)
                    if n == 0:
                        dve.wait_ge(s["decay_made"], b + 1)
                        if not (isinstance(b, int) and b == 0):
                            level_read(dve, 7, b - 1)
                    elif n == 1:
                        if not (isinstance(b, int) and b == 0):
                            level_read(dve, 6, b - 1)
                        dve.wait_ge(s["tot_made"], LAST * b + n)
                    else:
                        level_read(dve, n - 1, b)
                        dve.wait_ge(s["tot_made"], LAST * b + n)
                    m = 1 << n
                    t2 = tot[n][:].rearrange("p h (n two) -> p (h n) two", two=2)
                    nb = HP * T // (2 * m)
                    v.tensor_tensor(tot[n + 1][:].rearrange("p h n -> p (h n)"), t2[:, :, 0], t2[:, :, 1], ALU.mult
                                    ).then_inc(s["tot_made"], 1)
                    v.tensor_tensor(blocks(ks[buf(n + 1)][:], m)[:, :, 0, :], blocks(ks[buf(n)][:], m)[:, :, 0, :],
                                    t2[:, :, 1:2].to_broadcast([P, nb, m]), ALU.mult)
                    v.tensor_tensor(blocks(rx[buf(n + 1)][0:N, 0], m)[:, :, 1, :],
                                    blocks(rx[buf(n)][0:N, 0], m)[:, :, 1, :],
                                    t2[0:N, :, 0:1].to_broadcast([N, nb, m]), ALU.mult).then_inc(s["multiplied"], 1)

                def masked(b, n):
                    m = LEVELS[n]
                    shape = [P, 2 * HP, P]
                    for q in range(QC):
                        ps = bk.ps[bk.bank[f"a{m}{q}"][0]][:].rearrange("p (n t) -> p n t", t=P)
                        w = wt[:, q].rearrange("p h l t -> p (h l) t")
                        if n == 0:
                            bk.filled(dve, f"a{m}{q}", b)
                            i = v.tensor_tensor(w, ps, sh.ident[:].unsqueeze(1).to_broadcast(shape), ALU.mult)
                        else:
                            if q % 2 == 0:
                                bk.filled(dve, f"a{m}{q + 1}", b)
                                bk.emptied(dve, f"a{LEVELS[n - 1]}{q + 1}", b)
                                k = touches[0]
                                touches[0] += 1
                                v.tensor_copy(touched[:, k:k + 1], sh.ones[:, 0:1])
                            i = v.copy_predicated(w, masks[m][:].unsqueeze(1).to_broadcast(shape), ps)
                        i.then_inc(bk.e(f"a{m}{q}"), 1)

                def mix(seq, pairs):
                    for i, c in pairs:
                        ps = bk.filled(dve, f"m{i}{c}", seq)
                        v.scalar_tensor_tensor(xs[i][:, c, :], ps[:], sh.maa[:, i, c:c + 1], xx[:, c, :],
                                               ALU.add, ALU.mult).then_inc(bk.e(f"m{i}{c}"), 1)

                def states(b):
                    for q in range(QC - 1):
                        ps = bk.filled(dve, f"kv{q // 2}", b)
                        if q == 0:
                            bk.filled(dve, "y3", b - 1)
                            dve.wait_ge(s["tot_made"], LAST * b + LAST)
                        else:
                            state_before(dve, q, b)
                        for hp in range(HP):
                            for hl in range(2):
                                r_ = slice(hl * N, hl * N + N)
                                col = (q % 2) * C + hp * P + hl * N
                                i = v.scalar_tensor_tensor(ss[r_, q + 1, hp, :], ss[r_, q, hp, :],
                                                           tot[LAST][r_, hp, q:q + 1], ps[r_, col:col + N],
                                                           ALU.mult, ALU.add)
                        i.then_inc(s["s_made"] if q == 0 else bk.e(f"kv{q - 1}"), 1)

                def group_statistics(b):
                    bk.emptied(dve, "y3", b)
                    upto(dve, "yn_made", b)
                    for q in range(QC):
                        for h in range(H):
                            v.bn_stats(gst[:, q * H + h, :], y[:, q, h * N:(h + 1) * N])
                    dve.drain()
                    v.tensor_tensor(gm[:], gst[:, :, 1], gst[:, :, 4], ALU.add)
                    v.tensor_tensor(gd[:], gst[:, :, 1], gst[:, :, 4], ALU.subtract)
                    v.tensor_tensor(gv[:], gst[:, :, 2], gst[:, :, 5], ALU.add)
                    dve.drain()
                    v.tensor_scalar(gm[:], gm[:], 0.5, None, ALU.mult)
                    v.tensor_tensor(gd[:], gd[:], gd[:], ALU.mult)
                    dve.drain()
                    v.scalar_tensor_tensor(gv[:], gd[:], N / 4.0, gv[:], ALU.mult, ALU.add)
                    dve.drain()
                    v.tensor_scalar(gv[:], gv[:], 1.0 / N, GN_EPS, ALU.mult, ALU.add).then_inc(s["y_var"], 1)

                def choose(seq):
                    lg = bk.filled(dve, "lg", seq)[:, 0:TB * E].rearrange("p (t e) -> p t e", e=E)
                    v.tensor_reduce(top[:], lg, AX.X, ALU.max).then_inc(s["top_made"], 1)
                    dve.wait_ge(s["top_made"], seq + 1)
                    v.tensor_tensor(sc[:], lg, top[:].to_broadcast([P, TB, E]), ALU.is_equal).then_inc(bk.e("lg"), 1)
                    bk.emptied(dve, "lg", seq)
                    v.tensor_tensor(sc[:], sc[:], rank[:], ALU.mult).then_inc(s["sc_made"], 1)
                    dve.wait_ge(s["sc_made"], seq + 1)
                    v.tensor_reduce(top[:], sc[:], AX.X, ALU.max).then_inc(s["best_made"], 1)
                    dve.wait_ge(s["best_made"], seq + 1)
                    v.tensor_tensor(onehot[:, ds(TB * seq, TB), :], sc[:], top[:].to_broadcast([P, TB, E]),
                                    ALU.is_equal).then_inc(s["hot_made"], 1)

                def step(i, a, b, c):
                    touches[0] = 0
                    if b:
                        masked(i, 0)
                        double(i, 1)
                        if isinstance(i, int) and i == 0:
                            dve.wait_ge(masks_made, 1)
                        masked(i, 1)
                    if a:
                        bk.emptied(dve, "xt1", i + 1)
                        v.tensor_tensor(xx[:], xt[:, :, 0:T], xt[:, :, 1:T + 1], ALU.subtract
                                        ).then_inc(s["xx_made"], 1)
                        dve.wait_ge(s["xx_made"], i + 2)
                        bk.filled(dve, "mixb", i)
                        for k in range(CC):
                            ins = v.scalar_tensor_tensor(xxx[:, k, :], xx[:, k, :], sh.maa[:, MIXES, k:k + 1],
                                                         xt[:, k, 1:T + 1], ALU.mult, ALU.add)
                        ins.then_inc(s["xxx_made"], 1)
                    if b:
                        double(i, 2)
                        masked(i, 2)
                    if c:
                        dve.wait_ge(s["gate_made"], i)
                        bk.emptied(dve, "yt1", i - 1)
                        v.tensor_tensor(yt[:], yt[:], gt[:], ALU.mult).then_inc(s["gated"], 1)
                    if b:
                        double(i, 3)
                    if a:
                        for m in range(MIXES):
                            dve.wait_ge(s["mix_high"], MIXES * (i + 1) + m + 1)
                            of = (mixa if m < 4 else mixb)[slot(m, 0), :]
                            ins = v.tensor_tensor(mix_parts[m][slot(m, 1), :], of, mix_parts[m][slot(m, 0), :],
                                                  ALU.subtract)
                        ins.then_inc(s["mix_ready"], 1)
                    if b:
                        masked(i, 3)
                    if c:
                        dve.wait_ge(res_got, 16 * i)
                        for n in range(2):
                            ps = bk.filled(dve, f"o{n}", i - 1)
                            half = xr[:, 2 * n:2 * n + 2, :].rearrange("p t c -> p (t c)")
                            v.tensor_tensor(half, ps[:], half, ALU.add).then_inc(bk.e(f"o{n}"), 1)
                    if a:
                        bk.filled(dve, "v1", i)
                        bk.filled(dve, "g1", i)
                        mix(i + 1, MIXING[:8])
                    if c:
                        bk.emptied(dve, "o0", i - 1)
                        bk.emptied(dve, "o1", i - 1)
                        statistics(1, xr, "z_var")
                    if b:
                        double(i, 4)
                        masked(i, 4)
                    if a:
                        mix(i + 1, MIXING[8:])
                    if c:
                        normalise(1, xr, zn, "z_rstd", "zn_made", i - 1)
                    if b:
                        double(i, 5)
                        masked(i, 5)
                        double(i, 6)
                        bk.emptied(dve, "g1", i)
                        v.scalar_tensor_tensor(gt[:], gt[:], 1.0, gh[:], ALU.add, ALU.mult).then_inc(s["gate_made"], 1)
                    if c:
                        choose(i - 1)
                    if b:
                        states(i)
                    if has_next(i):
                        normalise_x(i + 2)
                    if a:
                        double(i + 1, 0)
                    if b:
                        group_statistics(i)

                normalise_x(0)
                for r in rx:
                    v.memset(r[N:P, 0, :, :], 0.0)
                    i = v.memset(r[0:N, 1, :, :], 0.0)
                i.then_inc(r_zeros_made, 1)
                dve.wait_ge(mix_w_high, 1)
                for n in range(MIXES):
                    i = v.tensor_tensor(mix_w[slot(n, 2), n, :], sh.mix2[slot(n, 2), n, :], mix_w[slot(n, 2), n, :],
                                        ALU.subtract)
                i.then_inc(mix_w_made, 1)
                rounds(dve, step)
                dve.wait_ge(s["hot_made"], B)

            @block.tensor
            def _(pe):
                mm = nc.tensor
                pe.wait_ge(sh.att_in, 16 * ATT_LOADS)

                def transposes(name, c, of, seq):
                    ps = bk.open(pe, f"{name}{c}", seq)
                    for t in range(TB):
                        i = mm.transpose(ps[:, t * P:(t + 1) * P], of[:, t, c * P:(c + 1) * P], sh.ident[:])
                    i.then_inc(bk.f(f"{name}{c}"), 1)

                def project(name, seq, w, xin, cols):
                    ps = bk.open(pe, name, seq)
                    for c in range(CC):
                        i = mm.matmul(ps[:], w[:, c, cols], xin[:, c, :], start=(c == 0), stop=(c == CC - 1))
                    i.then_inc(bk.f(name), 1)

                def project_rows(name, seq, xin, w):
                    for n in range(2):
                        ps = bk.open(pe, f"{name}{n}", seq)
                        for q in (0, 1):
                            t = 2 * n + q
                            for c in range(CC):
                                i = mm.matmul(ps[:, q * C:(q + 1) * C], xin[:, c, t * P:(t + 1) * P], w[:, c, :],
                                              start=(c == 0), stop=(c == CC - 1))
                        i.then_inc(bk.f(f"{name}{n}"), 1)

                def one(name, seq, w, xin):
                    ps = bk.open(pe, name, seq)
                    mm.matmul(ps[:], w, xin, start=True, stop=True).then_inc(bk.f(name), 1)

                def mixes(seq, pairs):
                    for i, c in pairs:
                        one(f"m{i}{c}", seq, mix_w[:, i, c * P:(c + 1) * P], mix_parts[i][:])

                def level(b, n):
                    m, l = LEVELS[n], max(n - 1, 0)
                    level_ready(pe, l, b)
                    k = ku if m == "u" else ks[buf(l)]
                    for q in range(QC):
                        ps = bk.open(pe, f"a{m}{q}", b)
                        t_ = slice(q * P, (q + 1) * P)
                        for hp in range(HP):
                            i = mm.matmul(ps[:, hp * C:(hp + 1) * C].rearrange("p (l t) -> p l t", t=P),
                                          k[:, hp, t_], rx[buf(l)][:, :, hp, t_], start=True, stop=True)
                        i.then_inc(bk.f(f"a{m}{q}"), 1)

                def wide_levels(b):
                    for l, m, r0s in ((5, 32, (0, 64)), (6, 64, (0,))):
                        level_ready(pe, l, b)
                        for q in range(QC):
                            name, at = ("b", q * 4 * m) if m == 32 else (f"c{q // 2}", q % 2 * 4 * m)
                            if at == 0:
                                ps = bk.open(pe, name, b)
                            for hp in range(HP):
                                for r0 in r0s:
                                    t0 = q * P + r0
                                    col = at + hp * 2 * m
                                    i = mm.matmul(ps[r0:r0 + m, col:col + 2 * m].rearrange("p (l t) -> p l t", t=m),
                                                  ks[buf(l)][:, hp, t0:t0 + m],
                                                  rx[buf(l)][:, :, hp, t0 + m:t0 + 2 * m], start=True, stop=True)
                            if at + 4 * m == HB:
                                i.then_inc(bk.f(name), 1)

                def k_rows(b):
                    level_ready(pe, LAST, b)
                    for n in range(2):
                        ps = bk.open(pe, f"kt{n}", b)
                        for q in range(2 * n, min(2 * n + 2, QC - 1)):
                            for hp in range(HP):
                                col = ((q % 2) * HP + hp) * P
                                i = mm.transpose(ps[:, col:col + P], ks[buf(LAST)][:, hp, q * P:(q + 1) * P],
                                                 sh.ident[:])
                        i.then_inc(bk.f(f"kt{n}"), 1)

                def kv(b):
                    bk.emptied(pe, "v1", b)
                    for n in range(2):
                        bk.emptied(pe, f"kt{n}", b)
                        ps = bk.open(pe, f"kv{n}", b)
                        for q in range(2 * n, min(2 * n + 2, QC - 1)):
                            for hp in range(HP):
                                col = (q % 2) * C + hp * P
                                i = mm.matmul(ps[:, col:col + P], kt[:, q, hp, :], vv[:, q, hp * P:(hp + 1) * P],
                                              start=True, stop=True)
                        i.then_inc(bk.f(f"kv{n}"), 1)

                def outputs(b):
                    bk.emptied(pe, "c1", b)
                    for q in range(QC):
                        ps = bk.open(pe, f"y{q}", b)
                        if q:
                            state_before(pe, q, b)
                        for hp in range(HP):
                            for hl in range(2):
                                col = hp * P + hl * N
                                i = mm.matmul(ps[:, col:col + N], wt[:, q, hp, hl, :], vv[:, q, col:col + N],
                                              start=True, stop=(q == 0))
                                if q:
                                    i = mm.matmul(ps[:, col:col + N], rx[buf(LAST)][:, hl, hp, q * P:(q + 1) * P],
                                                  ss[:, q, hp, :], start=False, stop=True)
                        i.then_inc(bk.f(f"y{q}"), 1)

                def step(i, a, b, c):
                    if b:
                        level(i, 0)
                        level(i, 1)
                    if a:
                        pe.wait_ge(s["xn_made"], i + 2)
                        for k in range(CC):
                            transposes("xt", k, xn, i + 1)
                    if b:
                        level(i, 2)
                    if c:
                        pe.wait_ge(s["yn_made"], i)
                        for k in range(CC):
                            transposes("yt", k, yn, i - 1)
                    if a:
                        pe.wait_ge(s["xxx_made"], i + 2)
                        project("mixa", i + 1, sh.mix1, xxx, slice(0, P))
                        project("mixb", i + 1, sh.mix1, xxx, slice(P, 2 * P))
                    if b:
                        level(i, 3)
                        for k in range(CC):
                            project(f"g{k}", i, sh.wm["Wg"], xs[G_], slice(k * P, (k + 1) * P))
                    if c:
                        pe.wait_ge(s["gated"], i)
                        project_rows("o", i - 1, yt, sh.wm["Wo"])
                    if a:
                        if isinstance(i, int) and i == -1:
                            pe.wait_ge(mix_w_made, 1)
                        pe.wait_ge(s["mix_ready"], i + 2)
                        mixes(i + 1, MIXING[:8])
                    if b:
                        level(i, 4)
                    if a:
                        mixes(i + 1, MIXING[8:])
                        pe.wait_ge(s["xs_made"], 10 * i + 12)
                        project("d1", i + 1, sh.dw1, xs[W_], slice(0, P))
                    if b:
                        level(i, 5)
                    if a:
                        pe.wait_ge(s["xs_made"], 10 * i + 16)
                        for k in range(CC):
                            project(f"k{k}", i + 1, sh.wm["Wk"], xs[K_], slice(k * P, (k + 1) * P))
                    if c:
                        pe.wait_ge(s["zn_made"], i)
                        for k in range(CC):
                            transposes("zt", k, zn, i - 1)
                    if a:
                        for k in range(CC):
                            project(f"r{k}", i + 1, sh.wm["Wr"], xs[R_], slice(k * P, (k + 1) * P))
                    if c:
                        bk.emptied(pe, "zt1", i - 1)
                        ps = bk.open(pe, "lg", i - 1)
                        for t in range(TB):
                            for k in range(CC):
                                ins = mm.matmul(ps[:, t * E:(t + 1) * E], zt[:, k, t * P:(t + 1) * P],
                                                sh.w_router[:, k, :], start=(k == 0), stop=(k == CC - 1))
                        ins.then_inc(bk.f("lg"), 1)
                    if b:
                        wide_levels(i)
                    if a:
                        bk.emptied(pe, "d1", i + 1)
                        for k in range(CC):
                            one(f"d2{k}", i + 1, sh.dw2[:, k * P:(k + 1) * P], d1[:])
                    if b:
                        k_rows(i)
                    if a:
                        pe.wait_ge(s["xs_made"], 10 * i + 20)
                        project_rows("v", i + 1, xs[V_], sh.wm["Wv"])
                    if b:
                        kv(i)
                        outputs(i)

                rounds(pe, step)

            @block.scalar
            def _(act):
                ac = nc.scalar.activation
                act.wait_ge(sh.att_in, 16 * ATT_LOADS)
                for parts in mix_parts:
                    ac(parts[:], sh.ident[:, 0:1].to_broadcast([P, T]), ACT.Copy, scale=0.0)
                ac(mix_w[:], sh.mix2[:], ACT.Copy).then_inc(mix_w_high, 1)

                def keep(b, n):
                    level_ready(act, n, b)
                    if n == 0:
                        if not (isinstance(b, int) and b == 0):
                            level_read(act, 7, b - 1)
                    elif n == 1:
                        if not (isinstance(b, int) and b == 0):
                            level_read(act, 6, b - 1)
                    else:
                        level_read(act, n - 1, b)
                    m = 1 << n
                    ac(blocks(ks[buf(n + 1)][:], m)[:, :, 1, :], blocks(ks[buf(n)][:], m)[:, :, 1, :], ACT.Copy)
                    for hl in range(2):
                        r_ = slice(hl * N, hl * N + N)
                        i = ac(blocks(rx[buf(n + 1)][r_, hl], m)[:, :, 0, :], blocks(rx[buf(n)][r_, hl], m)[:, :, 0, :],
                               ACT.Copy)
                    i.then_inc(s["copied"], 1)

                def step(i, a, b, c):
                    if b:
                        keep(i, 1)
                    if a:
                        upto(act, "xs_made", 10 * (i + 1))
                        for k in range(CC):
                            ps = bk.filled(act, f"xt{k}", i + 1)
                            ac(xt[:, k, 1:T + 1], ps[:], ACT.Copy).then_inc(bk.e(f"xt{k}"), 1)
                    if b:
                        keep(i, 2)
                    if c:
                        bk.filled(act, "o1", i - 2)
                        for k in range(CC):
                            ac(yt[:, k, :], bk.filled(act, f"yt{k}", i - 1)[:], ACT.Identity,
                               bias=sh.vecs[:, 3, k:k + 1], scale=sh.vecs[:, 2, k:k + 1]).then_inc(bk.e(f"yt{k}"), 1)
                    if a:
                        bk.filled(act, "m41", i)
                        for name, to in (("mixa", mixa), ("mixb", mixb)):
                            ac(to[:], bk.filled(act, name, i + 1)[:], ACT.Tanh).then_inc(bk.e(name), 1)
                        bk.emptied(act, "mixa", i + 1)
                        bk.emptied(act, "mixb", i + 1)
                        for m in range(MIXES):
                            of = (mixa if m < 4 else mixb)[slot(m, 0), :]
                            ac(mix_parts[m][slot(m, 0), :], of, ACT.Copy)
                            ac(mix_parts[m][slot(m, 2), :], of, ACT.Copy).then_inc(s["mix_high"], 1)
                    if b:
                        keep(i, 3)
                        upto(act, "gated", i)
                        for k in range(CC):
                            ps = bk.filled(act, f"g{k}", i)
                            ac(gt[:, k, :], ps[:], ACT.Tanh, scale=0.5)
                            ac(gh[:, k, :], ps[:], ACT.Copy, scale=0.5).then_inc(bk.e(f"g{k}"), 1)
                    if b:
                        keep(i, 4)
                    if a:
                        bk.filled(act, "d21", i)
                        ac(d1[:], bk.filled(act, "d1", i + 1)[:], ACT.Tanh).then_inc(bk.e("d1"), 1)
                    if b:
                        keep(i, 5)
                        level_ready(act, 1, i)
                        bk.filled(act, "a13", i)
                    if a:
                        for k in range(CC):
                            ps = bk.filled(act, f"k{k}", i + 1)
                            ac(ks[0][:, k, :], ps[:], ACT.Copy)
                            ac(ku[:, k, :], ps[:], ACT.Copy, scale=sh.vecs[:, 1, k:k + 1]).then_inc(bk.e(f"k{k}"), 1)
                    if c:
                        bk.filled(act, "lg", i - 2)
                        for k in range(CC):
                            ac(zt[:, k, :], bk.filled(act, f"zt{k}", i - 1)[:], ACT.Copy).then_inc(bk.e(f"zt{k}"), 1)
                    if a:
                        if isinstance(i, int) and i == -1:
                            act.wait_ge(r_zeros_made, 1)
                        for k in range(CC):
                            ps = bk.filled(act, f"r{k}", i + 1)
                            ac(rx[0][0:N, 0, k, :], ps[0:N, :], ACT.Copy)
                            ac(rx[0][N:P, 1, k, :], ps[N:P, :], ACT.Copy).then_inc(bk.e(f"r{k}"), 1)
                    if b:
                        bk.emptied(act, "a163", i)
                        ps = bk.filled(act, "b", i)
                        for r0 in (0, 64):
                            ins = ac(wt[r0:r0 + 32, :, :, :, r0 + 32:r0 + 64].rearrange("p q h l t -> p (q h l) t"),
                                     ps[r0:r0 + 32, :].rearrange("p (n t) -> p n t", t=32), ACT.Copy)
                        ins.then_inc(bk.e("b"), 1)
                        keep(i, 6)
                        for n in range(2):
                            ac(wt[0:64, 2 * n:2 * n + 2, :, :, 64:128].rearrange("p q h l t -> p (q h l) t"),
                               bk.filled(act, f"c{n}", i)[0:64, :].rearrange("p (n t) -> p n t", t=64),
                               ACT.Copy).then_inc(bk.e(f"c{n}"), 1)
                    if a:
                        if b:
                            act.wait_ge(s["multiplied"], LAST * i + 1)
                            act.wait_ge(s["multiplied1"], LAST * i + 1)
                        for k in range(CC):
                            ac(tot[0][:, k, :], bk.filled(act, f"d2{k}", i + 1)[:], ACT.Exp,
                               bias=sh.vecs[:, 0, k:k + 1]).then_inc(bk.e(f"d2{k}"), 1)
                    if b:
                        for n, cols in ((0, 512), (1, 256)):
                            bk.filled(act, "kv1", i - 1)
                            ps = bk.filled(act, f"kt{n}", i)
                            ac(kt[:, 2 * n:min(2 * n + 2, QC - 1), :, :].rearrange("p q h s -> p (q h s)"),
                               ps[:, 0:cols], ACT.Copy).then_inc(bk.e(f"kt{n}"), 1)
                    if a:
                        bk.emptied(act, "d20", i + 1)
                        bk.emptied(act, "d21", i + 1)
                        ac(tot[0][:], tot[0][:], ACT.Exp, scale=-1.0).then_inc(s["decay_made"], 1)
                    if b:
                        upto(act, "yn_made", i)
                        for q in range(QC):
                            ac(y[:, q, :], bk.filled(act, f"y{q}", i)[:, 0:C], ACT.Copy).then_inc(bk.e(f"y{q}"), 1)
                    if a:
                        for n in range(2):
                            ac(vv[:, 2 * n:2 * n + 2, :].rearrange("p q c -> p (q c)"),
                               bk.filled(act, f"v{n}", i + 1)[:], ACT.Copy).then_inc(bk.e(f"v{n}"), 1)
                        keep(i + 1, 0)

                rounds(act, step)


def macaron(nc, x, attn, ffn_in, out):
    x1 = nc.dram_tensor("after_ffn1", [NTOK, C], F32, kind="Internal").ap()
    x2 = nc.dram_tensor("after_attention", [NTOK, C], F32, kind="Internal").ap()
    with ExitStack() as ctx:
        sh = Shared(nc, ctx)
        load_attention(sh)
        load_constants(sh, ffn_in)
        onehot = sh.sb("onehot", [P, NT, E])
        index = sh.sb("index", [P, NS], U32)
        expert = sh.sb("expert", [1, NS], I32)

        def ffn_loads(sp):
            start_ffn_loads(sp, sh, ffn_in)

        def all_loads(sp):
            ffn_loads(sp)
            with nc.allow_non_contiguous_dma(reason="vectors of 256 to 128 partitions"):
                start_attention_loads(sp, sh, attn)

        with ExitStack() as weights:
            place_ffn_weights(sh, weights)
            choose_experts(sh, x, onehot, all_loads)
            place_split_weights(sh, weights)
            place_tokens(sh, onehot, index, expert)
            ffn(sh, x, x1, index, expert)
        attention(sh, x1, x2, onehot)
        with ExitStack() as weights:
            place_ffn_weights(sh, weights)
            place_split_weights(sh, weights)
            place_tokens(sh, onehot, index, expert, ffn_loads)
            ffn(sh, x2, out, index, expert)


_ATTN = ["time_maa_x", "time_maa_w", "time_maa_k", "time_maa_v", "time_maa_r", "time_maa_g", "time_maa_w1",
         "time_maa_w2", "time_decay", "time_decay_w1", "time_decay_w2", "time_faaaa", "Wr", "Wk", "Wv", "Wg", "Wo",
         "ln_w", "ln_b"]
_FFN = ["W_router", "W1", "b1", "Wo", "bo", "ln_gamma", "ln_beta"]


def kernel(**inputs):
    import numpy as _np
    import concourse.bacc as _bacc
    from concourse import mybir as _mybir
    from concourse.bass_utils import run_bass_kernel_spmd as _run

    nc = _bacc.Bacc("TRN2", target_bir_lowering=False, num_devices=1)
    arrays = {}

    def given(name):
        a = _np.ascontiguousarray(inputs[name])
        arrays[f"in_{name}"] = a
        return nc.dram_tensor(f"in_{name}", a.shape, _mybir.dt.from_np(a.dtype), kind="ExternalInput").ap()

    x = given("L0_attn_x")
    attn = {k: given("L0_attn_" + k) for k in _ATTN}
    ffn_in = {k: given("L0_ffn_" + k) for k in _FFN}
    out = nc.dram_tensor("out_0", x.shape, F32, kind="ExternalOutput").ap()
    macaron(nc, x.rearrange("b t c -> (b t) c"), attn, ffn_in, out.rearrange("b t c -> (b t) c"))
    r = _run(nc, [arrays], core_ids=[0])
    return r.results[0]["out_0"]
```
